# Optimizing a Trainium2 kernel written in Bass

```python
import numpy as np
import jax
import jax.numpy as jnp

def _softmax(x, axis=-1):
    return jax.nn.softmax(x, axis=axis)

def _gelu(x):
    return jax.nn.gelu(x, approximate=True)

def _silu(x):
    return jax.nn.silu(x)

def _sigmoid(x):
    return jax.nn.sigmoid(x)

def _layernorm(x, axis=-1, eps=1e-05):
    m = jnp.mean(x, axis=axis, keepdims=True)
    v = jnp.var(x, axis=axis, keepdims=True)
    return (x - m) / jnp.sqrt(v + eps)

def _scatter_add(tgt, idx, src, axis=0):
    return tgt.at[idx].add(src)

def _segment_sum(src, seg, n):
    return jax.ops.segment_sum(src, seg, n)
kernel_name = 'mk_flamingo_gated_d2_seqx_r8_73eee4'

def setup_inputs(seed: int=0):
    np.random.seed(seed)
    _w = jnp.asarray

    def _rec_inputs():
        import jax
        import jax.numpy as jnp
        _rk = jax.random.key(seed)
        x = -0.0005207 + 1.001 * jax.random.normal(jax.random.fold_in(_rk, 1), (4, 256, 512), jnp.float32)
        _lenS = 256 - jax.random.randint(jax.random.fold_in(_rk, 7), (4,), 0, max(1, 256 // 4) + 1, jnp.int32)
        _lenS2 = 64 - jax.random.randint(jax.random.fold_in(_rk, 8), (4,), 0, max(1, 64 // 4) + 1, jnp.int32)
        _ctx_4096P = jax.random.normal(jax.random.fold_in(_rk, 11), (4, 16, 512), jnp.float32)
        _ctx_4096c = jax.random.dirichlet(jax.random.fold_in(_rk, 511), 0.3 * jnp.ones((16,), jnp.float32), (4, 64))
        _ctx_4096t = jnp.einsum('bsk,bkd->bsd', _ctx_4096c, _ctx_4096P)
        _ctx_4096t = _ctx_4096t * jax.lax.rsqrt(jnp.mean(jnp.square(_ctx_4096t)) + 1e-12) * 0.953939
        ctx_4096 = -0.00010331 + 0.999899 * (_ctx_4096t + 0.3 * jax.random.normal(jax.random.fold_in(_rk, 611), (4, 64, 512), jnp.float32))
        _validS = jnp.arange(256)[None, :] < _lenS[:, None]
        _validS2 = jnp.arange(64)[None, :] < _lenS2[:, None]
        _causal = jnp.tril(jnp.ones((256, 256), dtype=bool))
        mask_1x1xSxS2_ff0 = jnp.where(jnp.ones((1, 1, 256, 64), dtype=bool), 0.0, -1000000000.0).astype(jnp.float32)
        _g = jax.random.normal(jax.random.fold_in(_rk, 9001), (2, 2), jnp.float32)
        _g = jnp.sign(_g) * jnp.maximum(jnp.abs(_g), 1.0) + (_g == 0) * 1.0
        g_xattn = _g[0]
        g_ffn = _g[1]
        return (x, ctx_4096, mask_1x1xSxS2_ff0, g_xattn, g_ffn)
    x, ctx_4096, mask_1x1xSxS2_ff0, g_xattn, g_ffn = _rec_inputs()

    def _L0_xattn_setup():
        import jax, jax.numpy as jnp
        import numpy as np
        import math
        HIDDEN = 512
        N_HEADS = 32
        HEAD_DIM = 128
        N_KV_HEADS = 4
        N_GROUPS = N_HEADS // N_KV_HEADS
        key = jax.random.key(seed)
        ks = jax.random.split(key, 6)
        B, NL, S = (8, 64, 512)
        latents = jax.random.normal(ks[0], (B, NL, HIDDEN), dtype=jnp.float32)
        context = jax.random.normal(ks[1], (B, S, HIDDEN), dtype=jnp.float32)
        scale = 1.0 / math.sqrt(HIDDEN)
        Wq = jax.random.normal(ks[2], (HIDDEN, N_HEADS * HEAD_DIM), dtype=jnp.float32) * scale
        Wk = jax.random.normal(ks[3], (HIDDEN, N_KV_HEADS * HEAD_DIM), dtype=jnp.float32) * scale
        Wv = jax.random.normal(ks[4], (HIDDEN, N_KV_HEADS * HEAD_DIM), dtype=jnp.float32) * scale
        Wo = jax.random.normal(ks[5], (N_HEADS * HEAD_DIM, HIDDEN), dtype=jnp.float32) * scale
        return {'latents': latents, 'context': context, 'Wq': Wq, 'Wk': Wk, 'Wv': Wv, 'Wo': Wo}
    _L0_xattn_all = _L0_xattn_setup()
    _L0_xattn_in = {k: v for k, v in _L0_xattn_all.items() if k in ('Wq', 'Wk', 'Wv', 'Wo')}
    del _L0_xattn_all

    def _L0_ffn_setup():
        import jax, jax.numpy as jnp
        import numpy as np
        HIDDEN = 512
        INTER = 1376
        SPARSITY = 0.5

        def _ternary_weight(key, out_dim, in_dim, sparsity):
            k_mask, k_sign = jax.random.split(key)
            nonzero = jax.random.bernoulli(k_mask, 1.0 - sparsity, (out_dim, in_dim))
            sign = jnp.where(jax.random.bernoulli(k_sign, 0.5, (out_dim, in_dim)), 1.0, -1.0)
            return (nonzero * sign).astype(jnp.float32)
        key = jax.random.key(seed)
        kx, kg, ku, kd, ksg, ksu, ksd = jax.random.split(key, 7)
        x = jax.random.normal(kx, (4, 256, HIDDEN), dtype=jnp.float32)
        Wg = _ternary_weight(kg, INTER, HIDDEN, SPARSITY)
        Wu = _ternary_weight(ku, INTER, HIDDEN, SPARSITY)
        Wd = _ternary_weight(kd, HIDDEN, INTER, SPARSITY)
        ag = jax.random.uniform(ksg, (INTER,), dtype=jnp.float32, minval=0.5, maxval=1.5) / np.sqrt(HIDDEN)
        au = jax.random.uniform(ksu, (INTER,), dtype=jnp.float32, minval=0.5, maxval=1.5) / np.sqrt(HIDDEN)
        ad = jax.random.uniform(ksd, (HIDDEN,), dtype=jnp.float32, minval=0.5, maxval=1.5) / np.sqrt(INTER)
        return {'x': x, 'Wg': Wg, 'Wu': Wu, 'Wd': Wd, 'ag': ag, 'au': au, 'ad': ad}
    _L0_ffn_all = _L0_ffn_setup()
    _L0_ffn_in = {k: v for k, v in _L0_ffn_all.items() if k in ('Wg', 'Wu', 'Wd', 'ag', 'au', 'ad')}
    del _L0_ffn_all

    def _L1_xattn_setup():
        import jax, jax.numpy as jnp
        import numpy as np
        NUM_HEADS = 32
        NUM_KV_HEADS = 8
        HEAD_DIM = 128
        HIDDEN = 512
        EPS = 1e-05

        def rmsnorm(x, w, eps=EPS):
            xf = x.astype(jnp.float32)
            var = jnp.mean(xf * xf, axis=-1, keepdims=True)
            return w * (xf * jax.lax.rsqrt(var + eps)).astype(x.dtype)
        key = jax.random.key(seed)
        ks = jax.random.split(key, 10)
        B, Q, KV = (1, 128, 6404)
        s = 1.0 / np.sqrt(HIDDEN)
        return {'hidden_states': jax.random.normal(ks[0], (B, Q, HIDDEN), jnp.float32), 'cross_attention_states': jax.random.normal(ks[1], (B, KV, HIDDEN), jnp.float32), 'attention_mask': jnp.zeros((B, 1, Q, KV), jnp.float32), 'q_proj_w': jax.random.normal(ks[2], (NUM_HEADS * HEAD_DIM, HIDDEN), jnp.float32) * s, 'k_proj_w': jax.random.normal(ks[3], (NUM_KV_HEADS * HEAD_DIM, HIDDEN), jnp.float32) * s, 'v_proj_w': jax.random.normal(ks[4], (NUM_KV_HEADS * HEAD_DIM, HIDDEN), jnp.float32) * s, 'o_proj_w': jax.random.normal(ks[5], (HIDDEN, NUM_HEADS * HEAD_DIM), jnp.float32) * s, 'q_norm_w': jnp.ones((HEAD_DIM,), jnp.float32), 'k_norm_w': jnp.ones((HEAD_DIM,), jnp.float32)}
    _L1_xattn_all = _L1_xattn_setup()
    _L1_xattn_in = {k: v for k, v in _L1_xattn_all.items() if k in ('q_proj_w', 'k_proj_w', 'v_proj_w', 'o_proj_w', 'q_norm_w', 'k_norm_w')}
    del _L1_xattn_all

    def _L1_ffn_setup():
        import jax, jax.numpy as jnp
        import numpy as np
        HD, M = (512, 1792)
        key = jax.random.key(seed)
        k_x, k_g, k_u, k_d = jax.random.split(key, 4)
        scale = 1.0 / np.sqrt(HD)
        x = jax.random.normal(k_x, (4, 256, HD), dtype=jnp.float16)
        W_gate = jax.random.normal(k_g, (M, HD), dtype=jnp.float16) * jnp.float16(scale)
        W_up = jax.random.normal(k_u, (M, HD), dtype=jnp.float16) * jnp.float16(scale)
        W_down = jax.random.normal(k_d, (HD, M), dtype=jnp.float16) * jnp.float16(1.0 / np.sqrt(M))
        return {'x': x, 'W_gate': W_gate, 'W_up': W_up, 'W_down': W_down}
    _L1_ffn_all = _L1_ffn_setup()
    _L1_ffn_in = {k: v for k, v in _L1_ffn_all.items() if k in ('W_gate', 'W_up', 'W_down')}
    del _L1_ffn_all
    return {'x': x, 'ctx_4096': ctx_4096, 'mask_1x1xSxS2_ff0': mask_1x1xSxS2_ff0, 'g_xattn': g_xattn, 'g_ffn': g_ffn, 'L0_xattn_Wq': _L0_xattn_in['Wq'], 'L0_xattn_Wk': _L0_xattn_in['Wk'], 'L0_xattn_Wv': _L0_xattn_in['Wv'], 'L0_xattn_Wo': _L0_xattn_in['Wo'], 'L0_ffn_Wg': _L0_ffn_in['Wg'], 'L0_ffn_Wu': _L0_ffn_in['Wu'], 'L0_ffn_Wd': _L0_ffn_in['Wd'], 'L0_ffn_ag': _L0_ffn_in['ag'], 'L0_ffn_au': _L0_ffn_in['au'], 'L0_ffn_ad': _L0_ffn_in['ad'], 'L1_xattn_q_proj_w': _L1_xattn_in['q_proj_w'], 'L1_xattn_k_proj_w': _L1_xattn_in['k_proj_w'], 'L1_xattn_v_proj_w': _L1_xattn_in['v_proj_w'], 'L1_xattn_o_proj_w': _L1_xattn_in['o_proj_w'], 'L1_xattn_q_norm_w': _L1_xattn_in['q_norm_w'], 'L1_xattn_k_norm_w': _L1_xattn_in['k_norm_w'], 'L1_ffn_W_gate': _L1_ffn_in['W_gate'], 'L1_ffn_W_up': _L1_ffn_in['W_up'], 'L1_ffn_W_down': _L1_ffn_in['W_down']}

def reference(x, ctx_4096, mask_1x1xSxS2_ff0, g_xattn, g_ffn, L0_xattn_Wq, L0_xattn_Wk, L0_xattn_Wv, L0_xattn_Wo, L0_ffn_Wg, L0_ffn_Wu, L0_ffn_Wd, L0_ffn_ag, L0_ffn_au, L0_ffn_ad, L1_xattn_q_proj_w, L1_xattn_k_proj_w, L1_xattn_v_proj_w, L1_xattn_o_proj_w, L1_xattn_q_norm_w, L1_xattn_k_norm_w, L1_ffn_W_gate, L1_ffn_W_up, L1_ffn_W_down):
    import jax
    import jax.numpy as jnp

    def _L0_xattn_ref(latents, context, Wq, Wk, Wv, Wo):
        import jax, jax.numpy as jnp
        import numpy as np
        import math
        HIDDEN = 512
        N_HEADS = 32
        HEAD_DIM = 128
        N_KV_HEADS = 4
        N_GROUPS = N_HEADS // N_KV_HEADS
        b, q_len, _ = latents.shape
        kv_len = q_len + context.shape[1]
        hidden_states = jnp.concatenate([context, latents], axis=1)
        q = (latents @ Wq).reshape(b, q_len, N_KV_HEADS, N_GROUPS, HEAD_DIM)
        k = (hidden_states @ Wk).reshape(b, kv_len, N_KV_HEADS, HEAD_DIM)
        v = (hidden_states @ Wv).reshape(b, kv_len, N_KV_HEADS, HEAD_DIM)
        scale = 1.0 / math.sqrt(HEAD_DIM)
        scores = jnp.einsum('bqhgd,bkhd->bhgqk', q, k) * scale
        attn = jax.nn.softmax(scores.astype(jnp.float32), axis=-1).astype(q.dtype)
        out = jnp.einsum('bhgqk,bkhd->bqhgd', attn, v)
        out = out.reshape(b, q_len, N_HEADS * HEAD_DIM)
        return out @ Wo

    def _L0_ffn_ref(x, Wg, Wu, Wd, ag, au, ad):
        import jax, jax.numpy as jnp
        import numpy as np
        HIDDEN = 512
        INTER = 1376
        SPARSITY = 0.5

        def _ternary_weight(key, out_dim, in_dim, sparsity):
            k_mask, k_sign = jax.random.split(key)
            nonzero = jax.random.bernoulli(k_mask, 1.0 - sparsity, (out_dim, in_dim))
            sign = jnp.where(jax.random.bernoulli(k_sign, 0.5, (out_dim, in_dim)), 1.0, -1.0)
            return (nonzero * sign).astype(jnp.float32)
        gate = jnp.einsum('bsh,ih->bsi', x, Wg) * ag
        up = jnp.einsum('bsh,ih->bsi', x, Wu) * au
        h = jax.nn.silu(gate) * up
        out = jnp.einsum('bsi,hi->bsh', h, Wd) * ad
        return out

    def _L1_xattn_ref(hidden_states, cross_attention_states, attention_mask, q_proj_w, k_proj_w, v_proj_w, o_proj_w, q_norm_w, k_norm_w):
        import jax, jax.numpy as jnp
        import numpy as np
        NUM_HEADS = 32
        NUM_KV_HEADS = 8
        HEAD_DIM = 128
        HIDDEN = 512
        EPS = 1e-05

        def rmsnorm(x, w, eps=EPS):
            xf = x.astype(jnp.float32)
            var = jnp.mean(xf * xf, axis=-1, keepdims=True)
            return w * (xf * jax.lax.rsqrt(var + eps)).astype(x.dtype)
        B, Q, _ = hidden_states.shape
        KV = cross_attention_states.shape[1]
        n_rep = NUM_HEADS // NUM_KV_HEADS
        q = (hidden_states @ q_proj_w.T).reshape(B, Q, NUM_HEADS, HEAD_DIM).transpose(0, 2, 1, 3)
        k = (cross_attention_states @ k_proj_w.T).reshape(B, KV, NUM_KV_HEADS, HEAD_DIM).transpose(0, 2, 1, 3)
        v = (cross_attention_states @ v_proj_w.T).reshape(B, KV, NUM_KV_HEADS, HEAD_DIM).transpose(0, 2, 1, 3)
        q = rmsnorm(q, q_norm_w)
        k = jnp.repeat(k, n_rep, axis=1)
        v = jnp.repeat(v, n_rep, axis=1)
        k = rmsnorm(k, k_norm_w)
        scale = 1.0 / np.sqrt(HEAD_DIM)
        scores = jnp.einsum('bhqd,bhkd->bhqk', q, k) * scale + attention_mask
        attn = jax.nn.softmax(scores.astype(jnp.float32), axis=-1).astype(q.dtype)
        out = jnp.einsum('bhqk,bhkd->bhqd', attn, v)
        out = out.transpose(0, 2, 1, 3).reshape(B, Q, NUM_HEADS * HEAD_DIM)
        return out @ o_proj_w.T

    def _L1_ffn_ref(x, W_gate, W_up, W_down):
        import jax, jax.numpy as jnp
        import numpy as np
        HD, M = (512, 1792)
        gate = jnp.einsum('bsh,mh->bsm', x, W_gate)
        up = jnp.einsum('bsh,mh->bsm', x, W_up)
        h = jax.nn.silu(gate) * up
        out = jnp.einsum('bsm,hm->bsh', h, W_down)
        return out
    x = x + jnp.tanh(g_xattn[0]) * _L0_xattn_ref(_layernorm(x, axis=-1), ctx_4096, L0_xattn_Wq, L0_xattn_Wk, L0_xattn_Wv, L0_xattn_Wo)
    x = x + jnp.tanh(g_ffn[0]) * _L0_ffn_ref(_layernorm(x, axis=-1), L0_ffn_Wg, L0_ffn_Wu, L0_ffn_Wd, L0_ffn_ag, L0_ffn_au, L0_ffn_ad)
    x = x + jnp.tanh(g_xattn[1]) * _L1_xattn_ref(_layernorm(x, axis=-1), ctx_4096, mask_1x1xSxS2_ff0, L1_xattn_q_proj_w, L1_xattn_k_proj_w, L1_xattn_v_proj_w, L1_xattn_o_proj_w, L1_xattn_q_norm_w, L1_xattn_k_norm_w)
    x = x + jnp.tanh(g_ffn[1]) * _L1_ffn_ref(_layernorm(x, axis=-1), L1_ffn_W_gate, L1_ffn_W_up, L1_ffn_W_down)
    return x

_drawn_inputs = setup_inputs


def setup_inputs(seed=0):
    import zlib

    import numpy as np

    out = dict(_drawn_inputs(seed))
    spreads = {'g_ffn': (-1.0, 0.6), 'L1_xattn_q_norm_w': (1.0, 0.2), 'L1_xattn_k_norm_w': (1.0, 0.2)}
    factors = {}
    for name, (base, spread) in spreads.items():
        noise = np.random.default_rng([zlib.crc32(name.encode()), seed]).standard_normal(out[name].shape)
        drawn = base * np.exp(spread * noise) if base else spread * noise
        out[name] = jnp.asarray(drawn.astype(out[name].dtype))
    for name, factor in factors.items():
        out[name] = (out[name] * factor).astype(out[name].dtype)
    return out
```

```python
from contextlib import ExitStack

import concourse.bass as bass
from concourse import mybir

F32 = mybir.dt.float32
F32R = mybir.dt.float32r
F16 = mybir.dt.float16
ALU = mybir.AluOpType
ACT = mybir.ActivationFunctionType
AX_X = mybir.AxisListType.X

P = 128
BATCH, SEQ, DM = 4, 256, 512
CTX = 64
HD = 128
HEADS = 32
KV0, KV1 = 4, 8
KC = DM // P
NT = BATCH * SEQ // P
TB = SEQ // P
KVL0 = SEQ + CTX
SCALE = float(HD) ** -0.5
EPS = 1e-5

RING = 4
CHUNK = 1024

PAIRS0 = HEADS // KV0 // 2
UNITS0 = PAIRS0 * BATCH
QLEAD = 3
NCH0 = 3

GH1 = HEADS // KV1

F0, F0_PAD = 1376, 1408
F1 = 1792
NF0, NF1 = F0_PAD // P, F1 // P


def flamingo_two_layers(nc, x, ctxT, mask, g_xattn, g_ffn, wq0, wk0, wv0, wo0, wg0T, wu0T, wd0T,
                        ag, au, ad, wq1T, wk1T, wv1T, wo1T, qnorm, knorm, wg1T, wu1T, wd1T, out):
    ctx = ExitStack()

    def sem(name):
        return ctx.enter_context(nc.semaphore(name))

    def sb(stack, name, shape, dt=F32):
        return stack.enter_context(nc.sbuf_tensor(name, shape, dt))

    def f32(ap):
        return ap.bitcast(F32)

    with ctx:
        x_sb = sb(ctx, "x_sb", [P, NT, DM])
        xT_hi = sb(ctx, "xT_hi", [P, KC, NT * P], F32R)
        xT_lo = sb(ctx, "xT_lo", [P, KC, NT * P], F32R)
        cT_hi = sb(ctx, "cT_hi", [P, KC, BATCH * CTX], F32R)
        cT_lo = sb(ctx, "cT_lo", [P, KC, BATCH * CTX], F32R)
        ident = sb(ctx, "ident", [P, P])
        stage = sb(ctx, "stage", [P, RING, CHUNK])
        kv_stage = sb(ctx, "kv_stage", [P, 2, KC, HD])
        ln_out = sb(ctx, "ln_out", [P, 2, DM])
        ln_stats = sb(ctx, "ln_stats", [P, NT, 6])
        ln_mv = sb(ctx, "ln_mv", [P, NT, 2])
        ln_var = sb(ctx, "ln_var", [P, NT])
        ln_rstd = sb(ctx, "ln_rstd", [P, NT])
        neg_half = sb(ctx, "neg_half", [P, NT])
        gates = sb(ctx, "gates", [P, 4])
        tg = sb(ctx, "tg", [P, 4])
        mask_sb = sb(ctx, "mask_sb", [P, TB, CTX])
        qn_w = sb(ctx, "qn_w", [P, 1])
        kn_w = sb(ctx, "kn_w", [P, 1])
        kscale = sb(ctx, "kscale", [P, 1])
        ag_sb = sb(ctx, "ag_sb", [P, NF0])
        au_sb = sb(ctx, "au_sb", [P, NF0])

        r0 = ExitStack()
        wq_hi = sb(r0, "wq_hi", [P, 2, KC, 2 * HD], F32R)
        wq_lo = sb(r0, "wq_lo", [P, 2, KC, 2 * HD], F32R)
        wo_hi = sb(r0, "wo_hi", [P, 2, 2, DM], F32R)
        wo_lo = sb(r0, "wo_lo", [P, 2, 2, DM], F32R)
        wkv_hi = sb(r0, "wkv_hi", [P, 2, KC, HD], F32R)
        wkv_lo = sb(r0, "wkv_lo", [P, 2, KC, HD], F32R)
        k_hi = sb(r0, "k_hi", [P, BATCH, KVL0], F32R)
        k_lo = sb(r0, "k_lo", [P, BATCH, KVL0], F32R)
        v_hi = sb(r0, "v_hi", [P, NT + BATCH, HD], F32R)
        v_lo = sb(r0, "v_lo", [P, NT + BATCH, HD], F32R)
        vT = sb(r0, "vT", [P, NT + BATCH, P])
        qT_hi = sb(r0, "qT_hi", [P, 4, 2 * SEQ], F32R)
        qT_lo = sb(r0, "qT_lo", [P, 4, 2 * SEQ], F32R)
        prob = sb(r0, "prob", [P, 4, KVL0])
        probn = sb(r0, "probn", [P, 4, NCH0 * P])
        pT_hi = sb(r0, "pT_hi", [P, NCH0, 2 * SEQ], F32R)
        pT_lo = sb(r0, "pT_lo", [P, 2, 2 * SEQ], F32R)
        oT_hi = sb(r0, "oT_hi", [P, 2 * SEQ], F32R)
        oT_lo = sb(r0, "oT_lo", [P, 2 * SEQ], F32R)
        nmax = sb(r0, "nmax", [P, 4])
        rsum = sb(r0, "rsum", [P, 4])
        rinv = sb(r0, "rinv", [P, 4])
        r0.close()

        def ffn_buffers(n, parts):
            r = ExitStack()
            t = {}
            for part in parts:
                t["gu_" + part] = sb(r, f"gu{n}_{part}", [P, 2, 2, KC, P], F32R)
                t["wd_" + part] = sb(r, f"wd{n}_{part}", [P, 2, DM], F32R)
            t["s"] = sb(r, f"silu{n}", [P, 2, 2 * SEQ])
            t["h"] = sb(r, f"h{n}", [P, 2, 2 * SEQ])
            t["h_hi"] = sb(r, f"h{n}_hi", [P, 2, 2 * SEQ], F32R)
            t["h_lo"] = sb(r, f"h{n}_lo", [P, 2, 2 * SEQ], F32R)
            if n == 0:
                t["ad"] = sb(r, "ad_row", [P, DM])
                t["tgad"] = sb(r, "tgad", [P, DM])
                t["scaled"] = sb(r, "scaled", [P, 2, DM])
            r.close()
            return t

        ffn_t = [ffn_buffers(0, ("hi", "lo")), ffn_buffers(1, ("hi",))]

        r1 = ExitStack()
        wq1_hi = sb(r1, "wq1_hi", [P, 2, KC, GH1 * HD], F32R)
        wq1_lo = sb(r1, "wq1_lo", [P, 2, KC, GH1 * HD], F32R)
        wo1_hi = sb(r1, "wo1_hi", [P, 2, GH1, DM], F32R)
        wo1_lo = sb(r1, "wo1_lo", [P, 2, GH1, DM], F32R)
        wkv1_hi = sb(r1, "wkv1_hi", [P, 2, KC, HD], F32R)
        wkv1_lo = sb(r1, "wkv1_lo", [P, 2, KC, HD], F32R)
        k1_hi = sb(r1, "k1_hi", [P, 2, BATCH * CTX], F32R)
        k1_lo = sb(r1, "k1_lo", [P, 2, BATCH * CTX], F32R)
        v1_hi = sb(r1, "v1_hi", [P, 2, BATCH, HD], F32R)
        v1_lo = sb(r1, "v1_lo", [P, 2, BATCH, HD], F32R)
        v1T = sb(r1, "v1T", [P, BATCH, P])
        k_row = sb(r1, "k_row", [P, 2, HD])
        k_sq = sb(r1, "k_sq", [P, 2, HD])
        q_row = sb(r1, "q_row", [P, TB, GH1 * HD])
        q_sq = sb(r1, "q_sq", [P, GH1 * HD])
        q1T_hi = sb(r1, "q1T_hi", [P, TB, GH1 * P], F32R)
        q1T_lo = sb(r1, "q1T_lo", [P, TB, GH1 * P], F32R)
        logit = sb(r1, "logit", [P, TB * GH1, CTX])
        prob1 = sb(r1, "prob1", [P, TB * GH1, CTX])
        prob1n = sb(r1, "prob1n", [P, TB * GH1, 2, CTX])
        p1T = sb(r1, "p1T", [P, 2, 2 * SEQ], F32R)
        o1T_hi = sb(r1, "o1T_hi", [P, 2, 2 * SEQ], F32R)
        o1T_lo = sb(r1, "o1T_lo", [P, 2, 2 * SEQ], F32R)
        q_ss = sb(r1, "q_ss", [P, TB * GH1])
        q_var = sb(r1, "q_var", [P, TB * GH1])
        q_rms = sb(r1, "q_rms", [P, TB * GH1])
        k_ss = sb(r1, "k_ss", [P, 2])
        k_var = sb(r1, "k_var", [P, 2])
        k_rms = sb(r1, "k_rms", [P, 2])
        mx1 = sb(r1, "mx1", [P, TB * GH1])
        sum1 = sb(r1, "sum1", [P, TB * GH1])
        rinv1 = sb(r1, "rinv1", [P, TB * GH1])
        r1.close()

        def bank(name):
            return ctx.enter_context(nc.psum_tensor(name, [P, 512], F32))

        bank_s = [bank("bank_s0"), bank("bank_s1")]
        bank_t = [bank("bank_t0"), bank("bank_t1"), bank("bank_t2")]
        bank_o = bank("bank_o")
        bank_a, bank_b = bank("bank_a"), bank("bank_b")
        o1_bank = [bank_o, bank_t[2]]
        s1_bank, kv1_bank = bank_s[0], bank_s[1]
        ffn_g, ffn_u = [bank_s[0], bank_s[1]], [bank_o, bank_a]
        ffn_acc = [bank_t[0], bank_t[1], bank_t[2], bank_b]

        s_stage = [sem(f"stage_loaded{i}") for i in range(RING)]
        s_x = [sem(f"x_loaded{i}") for i in range(NT)]
        s_ctx = sem("ctx_loaded")
        s_small = sem("small_loaded")
        s_ad = sem("ad_loaded")
        s_kvst = sem("kv_stage_loaded")
        s_out = sem("out_stored")
        s_ident = sem("ident_ready")
        s_half = sem("neg_half_ready")
        s_tg = sem("tg_ready")
        s_ksc = sem("kscale_ready")
        s_chi, s_clo = sem("ctx_hi"), sem("ctx_lo")
        l_stats, l_mv, l_var, l_rstd = sem("ln_stats_done"), sem("ln_mv_done"), sem("ln_var_done"), sem("ln_rstd_done")
        l_xn, l_tr, l_hi, l_lo = sem("ln_out_done"), sem("ln_transposed"), sem("ln_hi_done"), sem("ln_lo_done")
        a_wq_hi, a_wq_lo = sem("a_wq_hi"), sem("a_wq_lo")
        a_wo_hi, a_wo_lo = sem("a_wo_hi"), sem("a_wo_lo")
        a_wkv_hi, a_wkv_lo = sem("a_wkv_hi"), sem("a_wkv_lo")
        a_q, a_qhi, a_qlo = sem("a_q"), sem("a_q_hi"), sem("a_q_lo")
        a_s, a_max, a_exp = sem("a_scores"), sem("a_max"), sem("a_exp")
        a_rec, a_norm, a_dup = sem("a_recip"), sem("a_norm"), sem("a_dup")
        a_t, a_thi, a_tlo = sem("a_pT"), sem("a_pT_hi"), sem("a_pT_lo")
        a_pv, a_ohi, a_olo = sem("a_pv"), sem("a_o_hi"), sem("a_o_lo")
        a_wo, a_acc = sem("a_wo"), sem("a_acc")
        a_k, a_khi, a_klo = sem("a_k"), sem("a_k_hi"), sem("a_k_lo")
        a_vT, a_vTc = sem("a_vT"), sem("a_vT_copied")
        a_v, a_vhi, a_vlo = sem("a_v"), sem("a_v_hi"), sem("a_v_lo")
        F = [{k: sem(f"f{n}_{k}") for k in ("gu_hi", "gu_lo", "wd_hi", "wd_lo", "gate", "up", "silu", "h",
                                             "h_hi", "h_lo", "down", "acc", "tgad", "scaled", "x")} for n in range(2)]
        b_wq_hi, b_wq_lo = sem("b_wq_hi"), sem("b_wq_lo")
        b_wo_hi, b_wo_lo = sem("b_wo_hi"), sem("b_wo_lo")
        b_wkv_hi, b_wkv_lo = sem("b_wkv_hi"), sem("b_wkv_lo")
        b_q, b_qcp, b_qsq, b_ss, b_var, b_rms = (sem("b_q"), sem("b_q_copied"), sem("b_q_squared"), sem("b_q_ss"),
                                                 sem("b_q_var"), sem("b_q_rms"))
        b_qT, b_qThi, b_qTlo = sem("b_qT"), sem("b_qT_hi"), sem("b_qT_lo")
        b_s, b_log, b_mask, b_max, b_sub, b_exp = (sem("b_scores"), sem("b_logit"), sem("b_masked"), sem("b_max"),
                                                   sem("b_sub"), sem("b_exp"))
        b_sum, b_rec, b_norm = sem("b_sum"), sem("b_recip"), sem("b_norm")
        b_t, b_thi, b_tlo = sem("b_pT"), sem("b_pT_hi"), sem("b_pT_lo")
        b_pv, b_ohi, b_olo = sem("b_pv"), sem("b_o_hi"), sem("b_o_lo")
        b_wo, b_acc = sem("b_wo"), sem("b_acc")
        b_kr, b_krc, b_krs, b_kss, b_kvar, b_krms, b_kn = (sem("b_krow"), sem("b_krow_copied"), sem("b_krow_squared"),
                                                           sem("b_k_ss"), sem("b_k_var"), sem("b_k_rms"), sem("b_k_normed"))
        b_kT, b_khi, b_klo = sem("b_kT"), sem("b_k_hi"), sem("b_k_lo")
        b_vT, b_vTc = sem("b_vT"), sem("b_vT_copied")
        b_v, b_vhi, b_vlo = sem("b_v"), sem("b_v_hi"), sem("b_v_lo")

        stream = []

        def slot(n):
            return stage[:, n % RING, :]

        def slot16(n):
            return stage[:, n % RING, :].bitcast(F16)

        def k_rows(w, a, b):
            return w.rearrange("(c p) n -> p c n", p=P)[:, :, a:b]

        def head_rows(w, a, b):
            return w[a * HD:b * HD, :].rearrange("(h p) n -> p h n", p=P)

        def gu_view(v):
            return v[:, 0:CHUNK].rearrange("p (w c n) -> p w c n", w=2, c=KC)

        def ffn_order(nf):
            yield from (("gu", 0), ("gu", 1), ("wd", 0), ("gu", 2), ("wd", 1))
            for m in range(2 * nf):
                if m + 3 < 2 * nf:
                    yield "gu", m + 3
                if m + 2 < 2 * nf:
                    yield "wd", m + 2

        def add_ffn(n, wg, wu, wd):
            nf, at = NFS[n], {}
            part = "lo" if n == 0 else "hi"
            for what, m in ffn_order(nf):
                f, k = m % nf, len(stream)
                v = slot(k) if n == 0 else slot16(k)
                at[what, m] = k
                if what == "gu":
                    v = gu_view(v)
                    dmas = [(v[:, 0], k_rows(wg, f * P, (f + 1) * P)), (v[:, 1], k_rows(wu, f * P, (f + 1) * P))]
                else:
                    dmas = [(v[:, 0:DM], wd[f * P:(f + 1) * P, :])]
                stream.append((dmas, F[n][f"{what}_{part}"], m + 1))
            return at

        NFS = (NF0, NF1)
        for pair in range(HEADS // 2):
            v = slot(len(stream)).rearrange("p (c n) -> p c n", c=KC)
            stream.append(([(v, k_rows(wq0, pair * 2 * HD, (pair + 1) * 2 * HD))], a_wq_lo, pair + 1))
            v = slot(len(stream)).rearrange("p (h n) -> p h n", h=2)
            stream.append(([(v, head_rows(wo0, 2 * pair, 2 * pair + 2))], a_wo_lo, pair + 1))
        ffn_at = [add_ffn(0, wg0T, wu0T, wd0T)]
        l1_base = len(stream)
        for j in range(KV1):
            for q in range(2):
                v = slot(len(stream)).rearrange("p (c n) -> p c n", c=2)
                stream.append(([(v, k_rows(wq1T, j * GH1 * HD, (j + 1) * GH1 * HD)[:, 2 * q:2 * q + 2, :])],
                               b_wq_lo, 2 * j + q + 1))
            for q in range(2):
                v = slot(len(stream)).rearrange("p (h n) -> p h n", h=2)
                h = j * GH1 + 2 * q
                stream.append(([(v, head_rows(wo1T, h, h + 2))], b_wo_lo, 2 * j + q + 1))
        l1_end = len(stream)
        ffn_at.append(add_ffn(1, wg1T, wu1T, wd1T))
        landed, slot_sum = [], [0] * RING
        for n, (dmas, _, _) in enumerate(stream):
            slot_sum[n % RING] += 16 * len(dmas)
            landed.append(slot_sum[n % RING])

        def chunk_wait(eng, k, per=0, it=0):
            eng.wait_ge(s_stage[k % RING], landed[k] + (it * (landed[k + per] - landed[k]) if per else 0))

        block = ctx.enter_context(nc.Block())

        def load_kv(sp, n, wk, wv, head):
            if 1 <= n <= KV0:
                sp.wait_ge(a_wkv_lo, n)
            elif n > KV0:
                sp.wait_ge(b_wkv_lo, n - KV0)
            for w, src in enumerate((wk, wv)):
                sp.dma_start(kv_stage[:, w, :, :], k_rows(src, head * HD, (head + 1) * HD)).then_inc(s_kvst, 16)

        @block.sync
        def _(sp):
            x_rows = x.rearrange("(t p) d -> t p d", p=P)
            for t in range(NT):
                sp.dma_start(x_sb[:, t, :], x_rows[t]).then_inc(s_x[t], 16)
            load_kv(sp, 0, wk0, wv0, 0)
            sp.dma_start(prob[:, :, 0:BATCH * CTX], ctxT.rearrange("(c p) n -> p c n", p=P)).then_inc(s_ctx, 16)
            for n in range(RING):
                for dst, src in stream[n][0]:
                    sp.dma_start(dst, src).then_inc(s_stage[n % RING], 16)
            for dst, src in ((gates[:, 0:2], g_xattn.rearrange("(a n) -> a n", a=1).broadcast_to([P, 2])),
                             (gates[:, 2:4], g_ffn.rearrange("(a n) -> a n", a=1).broadcast_to([P, 2])),
                             (mask_sb[:, :, :], mask.rearrange("(c p) n -> p c n", p=P)),
                             (qn_w[:, :], qnorm), (kn_w[:, :], knorm), (ag_sb[:, :], ag), (au_sb[:, :], au)):
                sp.dma_start(dst, src).then_inc(s_small, 16)
            kv_n = 1
            for n in range(RING, len(stream)):
                if n < l1_base and n % (2 * PAIRS0) == 4 and kv_n < KV0:
                    load_kv(sp, kv_n, wk0, wv0, kv_n)
                    kv_n += 1
                if n in [l1_base - RING] + [l1_base + 4 * j for j in range(1, KV1)]:
                    load_kv(sp, kv_n, wk1T, wv1T, kv_n - KV0)
                    kv_n += 1
                sp.wait_ge(stream[n - RING][1], stream[n - RING][2])
                for dst, src in stream[n][0]:
                    sp.dma_start(dst, src).then_inc(s_stage[n % RING], 16)
                if n == ffn_at[0]["gu", 2]:
                    sp.wait_ge(a_acc, 2 * KV0 * UNITS0 + 2)
                    sp.dma_start(ffn_t[0]["ad"][:, :],
                                 ad.rearrange("(a n) -> a n", a=1).broadcast_to([P, DM])).then_inc(s_ad, 16)
            o_rows = out.rearrange("(t p) d -> t p d", p=P)
            for t in range(NT):
                sp.wait_ge(F[1]["x"], t + 1)
                sp.dma_start(o_rows[t], x_sb[:, t, :]).then_inc(s_out, 16)
            sp.wait_ge(s_out, 16 * NT)

        def ln_vector(ve, k, x_ready):
            n0 = NT * k
            for t in range(NT):
                x_ready(t)
                ve.bn_stats(ln_stats[:, t, :], x_sb[:, t, :]).then_inc(l_stats, 1)
                if t >= 1:
                    ve.wait_ge(l_stats, n0 + t)
                    ve.bn_aggr(ln_mv[:, t - 1, :], ln_stats[:, t - 1, :]).then_inc(l_mv, 1)
                if t == NT // 2 + 1:
                    ln_eps(ve, k, 0)
            ve.wait_ge(l_stats, n0 + NT)
            ve.bn_aggr(ln_mv[:, NT - 1, :], ln_stats[:, NT - 1, :]).then_inc(l_mv, 1)
            ln_eps(ve, k, 1)
            for t in range(NT + 1):
                if t < NT:
                    if t % (NT // 2) == 0:
                        ve.wait_ge(l_rstd, 2 * k + t // (NT // 2) + 1)
                    if t >= 2:
                        ve.wait_ge(l_tr, n0 + t - 1)
                    ve.tensor_scalar(ln_out[:, t % 2, :], x_sb[:, t, :], ln_mv[:, t, 0:1], ln_rstd[:, t:t + 1],
                                     ALU.subtract, ALU.mult).then_inc(l_xn, 1)
                if t >= 1:
                    ve.wait_ge(l_hi, n0 + t)
                    ve.tensor_tensor(xT_lo[:, :, (t - 1) * P:t * P],
                                     bank_t[(t - 1) % 2][:, :].rearrange("p (c n) -> p c n", c=KC),
                                     f32(xT_hi[:, :, (t - 1) * P:t * P]), ALU.subtract).then_inc(l_lo, 1)

        def ln_eps(ve, k, half):
            a, b = half * NT // 2, (half + 1) * NT // 2
            ve.wait_ge(l_mv, NT * k + b)
            ve.tensor_scalar(ln_var[:, a:b], ln_mv[:, a:b, 1], EPS, None, ALU.add).then_inc(l_var, 1)

        def ln_gpsimd(po, k):
            for half in range(2):
                a, b = half * NT // 2, (half + 1) * NT // 2
                po.wait_ge(l_var, 2 * k + half + 1)
                po.tensor_tensor(ln_rstd[:, a:b], ln_var[:, a:b], neg_half[:, a:b], ALU.pow).then_inc(l_rstd, 1)

        def ln_tensor(pe, k):
            for t in range(NT):
                pe.wait_ge(l_xn, NT * k + t + 1)
                if t >= 2:
                    pe.wait_ge(l_lo, NT * k + t - 1)
                for c in range(KC):
                    mm = pe.transpose(bank_t[t % 2][:, c * P:(c + 1) * P], ln_out[:, t % 2, c * P:(c + 1) * P],
                                      ident[:, :])
                mm.then_inc(l_tr, 1)

        def ln_scalar(ac, k):
            for t in range(NT):
                ac.wait_ge(l_tr, NT * k + t + 1)
                ac.activation(xT_hi[:, :, t * P:(t + 1) * P],
                              bank_t[t % 2][:, :].rearrange("p (c n) -> p c n", c=KC), ACT.Copy).then_inc(l_hi, 1)

        def project(pe, out_ap, lhs, rhs, chunks=range(KC), first=True, last=True):
            (l_h, l_l), (r_h, r_l) = lhs, rhs
            for c in chunks:
                passes = [(l_h, r_h), (l_h, r_l)] + ([(l_l, r_h)] if l_l else [])
                for n, (a, b) in enumerate(passes):
                    mm = pe.matmul(out_ap, a(c), b(c), start=first and c == chunks[0] and n == 0,
                                   stop=last and c == chunks[-1] and n == len(passes) - 1)
            return mm

        def per_g(n, g):
            return g * n

        def pe_q(pe, g, blk, part):
            par, slot_, hh, half = (blk // 4) % 2, blk % 4, blk % 2, blk % 4 // 2
            if part == 0:
                if slot_ == 0:
                    pe.wait_ge(a_wq_lo, per_g(PAIRS0, g) + blk // 4 + 1)
                pe.wait_ge(a_qlo, per_g(UNITS0, g) + blk)
            mm = project(pe, bank_a[:, :],
                         (lambda c: wq_hi[:, par, c, hh * HD:(hh + 1) * HD], lambda c: wq_lo[:, par, c, hh * HD:(hh + 1) * HD]),
                         (lambda c: xT_hi[:, c, half * 512:(half + 1) * 512], lambda c: xT_lo[:, c, half * 512:(half + 1) * 512]),
                         chunks=(0, 1, 2) if part == 0 else (3,), first=part == 0, last=part == 1)
            if part == 1:
                mm.then_inc(a_q, 1)

        def pe_scores(pe, g, i, j):
            b, hh, c = i % 4, j // 2, j % 2
            s = (b // 2) * 2 + hh
            if c == 0:
                pe.wait_ge(a_qlo, per_g(UNITS0, g) + (i // 4) * 4 + s + 1)
            if i % UNITS0 == 0 and j == 0:
                pe.wait_ge(a_klo, per_g(3, g) + 3 * (i // UNITS0) + 3)
            pe.wait_ge(a_exp, per_g(4 * UNITS0, g) + 4 * i + j + 1)
            q0 = (b % 2) * SEQ + c * P
            for n, (q, kk) in enumerate(((qT_hi, k_hi), (qT_hi, k_lo), (qT_lo, k_hi))):
                mm = pe.matmul(bank_s[j % 2][:, 0:KVL0], q[:, s, q0:q0 + P], kk[:, b, :], start=n == 0, stop=n == 2)
            mm.then_inc(a_s, 1)

        def pe_pT(pe, g, i):
            pe.wait_ge(a_norm, per_g(4 * UNITS0, g) + 4 * i + 4)
            for c in range(NCH0):
                if c == 2:
                    pe.wait_ge(a_dup, per_g(UNITS0, g) + i + 1)
                    pe.wait_ge(a_acc, per_g(2 * UNITS0, g) + 2 * i + 2)
                for j in range(4):
                    mm = pe.transpose(bank_t[c][:, j * P:(j + 1) * P], probn[:, j, c * P:(c + 1) * P], ident[:, :])
                mm.then_inc(a_t, 1)

        def pe_pv(pe, g, i):
            b = i % 4
            pe.wait_ge(a_olo, per_g(UNITS0, g) + i + 1)
            if i == 0:
                pe.wait_ge(a_vlo, per_g(3, g) + 3)
            mms = []
            for c in range(2):
                v = TB * b + c
                mms += [(v_hi[:, v], pT_hi[:, c], c), (v_hi[:, v], pT_lo[:, c], c), (v_lo[:, v], pT_hi[:, c], c)]
            mms += [(v_hi[:, NT + b], pT_hi[:, 2], 2), (v_lo[:, NT + b], pT_hi[:, 2], 2)]
            for n, (v, p, c) in enumerate(mms):
                if n == 0 or mms[n - 1][2] != c:
                    pe.wait_ge(a_tlo, per_g(3 * UNITS0, g) + 3 * i + c + 1)
                mm = pe.matmul(bank_o[:, :], v, p, start=n == 0, stop=n == len(mms) - 1)
            mm.then_inc(a_pv, 1)

        def pe_wo(pe, g, i, c):
            par = (i // 4) % 2
            if c == 0:
                if i % 4 == 0:
                    pe.wait_ge(a_wo_lo, per_g(PAIRS0, g) + i // 4 + 1)
                pe.wait_ge(a_olo, per_g(UNITS0, g) + i + 2)
                pe.wait_ge(a_acc, per_g(2 * UNITS0, g) + 2 * i + 2)
                if i == 0:
                    pe.wait_ge(a_vlo, per_g(3, g) + 2)
            dst = bank_b if c == 0 else bank_t[2]
            for hh in range(2):
                q0 = hh * SEQ + c * P
                for n, (o, w) in enumerate(((oT_hi, wo_hi), (oT_hi, wo_lo), (oT_lo, wo_hi))):
                    mm = pe.matmul(dst[:, :], o[:, q0:q0 + P], w[:, par, hh, :], start=hh == 0 and n == 0,
                                   stop=hh == 1 and n == 2)
            mm.then_inc(a_wo, 1)

        def kv_rhs(n):
            if n < 2:
                return (lambda c: xT_hi[:, c, n * 512:(n + 1) * 512], lambda c: xT_lo[:, c, n * 512:(n + 1) * 512])
            return (lambda c: cT_hi[:, c, :], lambda c: cT_lo[:, c, :])

        def pe_k(pe, g, n):
            dst = (bank_a, bank_b, bank_a)[n]
            project(pe, dst[:, :] if n < 2 else dst[:, 0:BATCH * CTX],
                    (lambda c: wkv_hi[:, 0, c, :], lambda c: wkv_lo[:, 0, c, :]), kv_rhs(n)).then_inc(a_k, 1)

        def pe_vT(pe, g, n):
            project(pe, bank_a[:, :] if n < 2 else bank_a[:, 0:BATCH * CTX],
                    (lambda c: wkv_hi[:, 1, c, :], lambda c: wkv_lo[:, 1, c, :]), kv_rhs(n)).then_inc(a_vT, 1)

        def pe_v(pe, n):
            for q in range(4):
                mm = pe.transpose((bank_a, bank_b, bank_o)[n][:, q * P:(q + 1) * P], vT[:, 4 * n + q, :], ident[:, :])
            mm.then_inc(a_v, 1)

        def pe_unit0(pe, g, i, last):
            nxt = not (last and i == UNITS0 - 1)
            blk = not (last and i + QLEAD >= UNITS0)
            if nxt:
                pe_scores(pe, g, i + 1, 0)
                pe_scores(pe, g, i + 1, 1)
            pe_pT(pe, g, i)
            if nxt:
                pe_scores(pe, g, i + 1, 2)
                pe_scores(pe, g, i + 1, 3)
            if blk:
                if i in (11, 12, 13) and not last:
                    pe.wait_ge(a_vTc, per_g(3, g) + 3 + i - 10)
                if i == 15:
                    pe.wait_ge(a_klo, per_g(3, g) + 6)
                if i == 0:
                    pe.wait_ge(a_vlo, per_g(3, g) + 1)
                pe_q(pe, g, i + QLEAD, 0)
            pe_pv(pe, g, i)
            if blk:
                pe_q(pe, g, i + QLEAD, 1)
            pe_wo(pe, g, i, 0)
            pe_wo(pe, g, i, 1)
            if not last:
                if i in (10, 11, 12):
                    if i == 10:
                        pe.wait_ge(a_wkv_lo, g + 2)
                    pe.wait_ge(a_qlo, per_g(UNITS0, g) + i + QLEAD + 1)
                    pe_vT(pe, g, i - 10)
                if i == 14:
                    pe.wait_ge(a_qlo, per_g(UNITS0, g) + i + QLEAD + 1)
                    pe_k(pe, g, 0)
                    pe.wait_ge(a_acc, per_g(2 * UNITS0, g) + 2 * i + 3)
                    pe_k(pe, g, 1)
                    pe.wait_ge(a_klo, per_g(3, g) + 4)
                    pe_k(pe, g, 2)
                if i == 15:
                    pe.wait_ge(a_vTc, per_g(3, g) + 6)
                    pe.wait_ge(a_qlo, per_g(UNITS0, g) + i + QLEAD + 1)
                    pe_v(pe, 0)
                    pe.wait_ge(a_acc, per_g(2 * UNITS0, g) + 2 * i + 3)
                    pe_v(pe, 1)
                    pe_v(pe, 2)

        def pe_attn0(pe):
            pe.wait_ge(a_wkv_lo, 1)
            pe.wait_ge(s_clo, 1)
            pe_k_first = ((0, NT // 2), (1, NT))
            for n, tiles in pe_k_first:
                pe.wait_ge(l_lo, tiles)
                pe_k(pe, 0, n)
            pe.wait_ge(a_klo, 1)
            pe_k(pe, 0, 2)
            pe.wait_ge(a_klo, 3)
            for n in range(3):
                if n:
                    pe.wait_ge(a_vTc, n)
                pe_vT(pe, 0, n)
            pe.wait_ge(a_vTc, 3)
            for n in range(3):
                pe_v(pe, n)
            pe.wait_ge(a_vlo, 1)
            for blk in range(QLEAD):
                pe_q(pe, 0, blk, 0)
                pe_q(pe, 0, blk, 1)
            for j in range(4):
                pe_scores(pe, 0, 0, j)
            with pe.Fori(0, KV0 - 1) as g:
                for i in range(UNITS0):
                    pe_unit0(pe, g, i, False)
            for i in range(UNITS0):
                pe_unit0(pe, KV0 - 1, i, True)

        def split_hi(ac, dst, src, done):
            ac.activation(dst, src, ACT.Copy).then_inc(done, 1)

        def ac_wq(ac, g, pair):
            n = 2 * pair
            chunk_wait(ac, n, 2 * PAIRS0, g)
            if pair >= 2:
                ac.wait_ge(a_q, per_g(UNITS0, g) + 4 * (pair - 1))
            split_hi(ac, wq_hi[:, pair % 2], stage[:, n % RING, :].rearrange("p (c n) -> p c n", c=KC), a_wq_hi)

        def ac_wo(ac, g, pair):
            n = 2 * pair + 1
            chunk_wait(ac, n, 2 * PAIRS0, g)
            if pair >= 1:
                ac.wait_ge(a_wo, per_g(2 * UNITS0, g) + 8 * (pair - 1) + 1)
            split_hi(ac, wo_hi[:, pair % 2], stage[:, n % RING, :].rearrange("p (h n) -> p h n", h=2), a_wo_hi)

        def ac_exp(ac, g, i, j):
            ac.wait_ge(a_max, per_g(4 * UNITS0, g) + 4 * i + j + 1)
            ac.wait_ge(a_norm, per_g(4 * UNITS0, g) + 4 * i)
            ac.wait_ge(a_dup, per_g(UNITS0, g) + i)
            ac.activation(prob[:, j, :], bank_s[j % 2][:, 0:KVL0], ACT.Exp, bias=nmax[:, j:j + 1],
                          accum_out=rsum[:, j:j + 1]).then_inc(a_exp, 1)

        def ac_q(ac, g, blk):
            ac.wait_ge(a_q, per_g(UNITS0, g) + blk + 1)
            ac.activation(qT_hi[:, blk % 4, :], bank_a[:, :], ACT.Copy, scale=SCALE).then_inc(a_qhi, 1)

        def k_dst(t, n):
            if n < 2:
                return t[:, 2 * n:2 * n + 2, 0:SEQ]
            return t[:, :, SEQ:KVL0]

        def k_src(n):
            if n < 2:
                return (bank_a, bank_b)[n][:, :].rearrange("p (b n) -> p b n", b=2)
            return bank_a[:, 0:BATCH * CTX].rearrange("p (b n) -> p b n", b=BATCH)

        def ac_k(ac, g, n):
            ac.wait_ge(a_k, per_g(3, g) + n + 1)
            ac.activation(k_dst(k_hi, n), k_src(n), ACT.Copy).then_inc(a_khi, 1)

        def ac_vT(ac, g, n):
            ac.wait_ge(a_vT, per_g(3, g) + n + 1)
            if n < 2:
                ac.activation(vT[:, 4 * n:4 * n + 4, :], bank_a[:, :].rearrange("p (t n) -> p t n", t=4),
                              ACT.Copy).then_inc(a_vTc, 1)
            else:
                src = bank_a[:, 0:BATCH * CTX].rearrange("p (b r n) -> p b r n", b=BATCH, r=1)
                ac.activation(vT[:, NT:NT + BATCH, :].rearrange("p b (r n) -> p b r n", r=2),
                              src.broadcast_to([P, BATCH, 2, CTX]), ACT.Copy).then_inc(a_vTc, 1)

        def v_src(n):
            return (bank_a, bank_b, bank_o)[n][:, :].rearrange("p (t n) -> p t n", t=4)

        def ac_v(ac, g, n):
            ac.wait_ge(a_v, per_g(3, g) + n + 1)
            ac.activation(v_hi[:, 4 * n:4 * n + 4, :], v_src(n), ACT.Copy).then_inc(a_vhi, 1)

        def ac_wkv(ac, k, dst, done):
            ac.wait_ge(s_kvst, 32 * k + 32)
            split_hi(ac, dst[:, :, :, :], kv_stage[:, :, :, :], done)

        def ac_unit0(ac, g, i, last):
            nxt = not (last and i == UNITS0 - 1)
            blk = not (last and i + QLEAD >= UNITS0)
            if nxt:
                ac_exp(ac, g, i + 1, 0)
                ac_exp(ac, g, i + 1, 1)
            for c in range(NCH0):
                ac.wait_ge(a_t, per_g(3 * UNITS0, g) + 3 * i + c + 1)
                ac.activation(pT_hi[:, c, :], bank_t[c][:, :], ACT.Copy).then_inc(a_thi, 1)
            if nxt:
                ac_exp(ac, g, i + 1, 2)
                ac_exp(ac, g, i + 1, 3)
            ac.wait_ge(a_pv, per_g(UNITS0, g) + i + 1)
            ac.activation(oT_hi[:, :], bank_o[:, :], ACT.Copy).then_inc(a_ohi, 1)
            if blk:
                ac_q(ac, g, i + QLEAD)
            p = i // 4
            if i % 4 == 1 and not (last and p + 1 >= PAIRS0):
                ac_wo(ac, g, p + 1)
            if i % 4 == 2 and not (last and p + 2 >= PAIRS0):
                ac_wq(ac, g, p + 2)
            if not last:
                if i == 5:
                    ac.wait_ge(a_k, per_g(3, g) + 3)
                    ac.wait_ge(a_vT, per_g(3, g) + 3)
                    ac_wkv(ac, g + 1, wkv_hi, a_wkv_hi)
                if i in (10, 11, 12):
                    ac_vT(ac, g + 1, i - 10)
                if i == 14:
                    for n in range(3):
                        ac_k(ac, g + 1, n)
                if i == 15:
                    for n in range(3):
                        ac_v(ac, g + 1, n)

        def ac_attn0(ac):
            for n in range(3):
                ac_k(ac, 0, n)
            for n in range(3):
                ac_vT(ac, 0, n)
            for n in range(3):
                ac_v(ac, 0, n)
            for blk in range(QLEAD):
                ac_q(ac, 0, blk)
            for j in range(4):
                ac_exp(ac, 0, 0, j)
            with ac.Fori(0, KV0 - 1) as g:
                for i in range(UNITS0):
                    ac_unit0(ac, g, i, False)
            for i in range(UNITS0):
                ac_unit0(ac, KV0 - 1, i, True)

        def ve_max(ve, g, i, j):
            ve.wait_ge(a_s, per_g(4 * UNITS0, g) + 4 * i + j + 1)
            ve.tensor_reduce(nmax[:, j:j + 1], bank_s[j % 2][:, 0:KVL0], AX_X, ALU.max, negate=True).then_inc(a_max, 1)

        def ve_norm(ve, g, i):
            ve.wait_ge(a_exp, per_g(4 * UNITS0, g) + 4 * i + 4 + 2)
            ve.wait_ge(a_dup, per_g(UNITS0, g) + i)
            ve.reciprocal(rinv[:, :], rsum[:, :]).then_inc(a_rec, 1)
            ve.wait_ge(a_rec, per_g(UNITS0, g) + i + 1)
            ve.wait_ge(a_t, per_g(3 * UNITS0, g) + 3 * i)
            for j in range(4):
                ve.tensor_scalar(probn[:, j, 0:SEQ], prob[:, j, 0:SEQ], rinv[:, j:j + 1], None,
                                 ALU.mult).then_inc(a_norm, 1)

        def ve_q(ve, g, blk):
            ve.wait_ge(a_qhi, per_g(UNITS0, g) + blk + 1)
            ve.scalar_tensor_tensor(out=qT_lo[:, blk % 4, :], in0=bank_a[:, :], scalar=SCALE,
                                    in1=f32(qT_hi[:, blk % 4, :]), op0=ALU.mult, op1=ALU.subtract).then_inc(a_qlo, 1)

        def ve_k(ve, g, n):
            ve.wait_ge(a_khi, per_g(3, g) + n + 1)
            ve.tensor_tensor(k_dst(k_lo, n), k_src(n), f32(k_dst(k_hi, n)), ALU.subtract).then_inc(a_klo, 1)

        def ve_v(ve, g, n):
            ve.wait_ge(a_vhi, per_g(3, g) + n + 1)
            ve.tensor_tensor(v_lo[:, 4 * n:4 * n + 4, :], v_src(n), f32(v_hi[:, 4 * n:4 * n + 4, :]),
                             ALU.subtract).then_inc(a_vlo, 1)

        def ve_add0(ve, g, i, c):
            t = TB * (i % 4) + c
            ve.wait_ge(a_wo, per_g(2 * UNITS0, g) + 2 * i + c + 1)
            ve.scalar_tensor_tensor(out=x_sb[:, t, :], in0=(bank_b, bank_t[2])[c][:, :], scalar=tg[:, 0:1],
                                    in1=x_sb[:, t, :], op0=ALU.mult, op1=ALU.add).then_inc(a_acc, 1)

        def ve_unit0(ve, g, i, last):
            nxt = not (last and i == UNITS0 - 1)
            blk = not (last and i + QLEAD >= UNITS0)
            if nxt:
                ve_max(ve, g, i + 1, 0)
                ve_max(ve, g, i + 1, 1)
            for c in range(NCH0):
                ve.wait_ge(a_thi, per_g(3 * UNITS0, g) + 3 * i + c + 1)
                if c < 2:
                    ve.tensor_tensor(pT_lo[:, c, :], bank_t[c][:, :], f32(pT_hi[:, c, :]),
                                     ALU.subtract).then_inc(a_tlo, 1)
                else:
                    ve.tensor_tensor(pT_hi[CTX:P, c, :], bank_t[c][CTX:P, :], f32(pT_hi[CTX:P, c, :]),
                                     ALU.subtract).then_inc(a_tlo, 1)
            if nxt:
                ve_max(ve, g, i + 1, 2)
                ve_max(ve, g, i + 1, 3)
                ve_norm(ve, g, i + 1)
            ve.wait_ge(a_ohi, per_g(UNITS0, g) + i + 1)
            ve.tensor_tensor(oT_lo[:, :], bank_o[:, :], f32(oT_hi[:, :]), ALU.subtract).then_inc(a_olo, 1)
            if blk:
                ve_q(ve, g, i + QLEAD)
            ve_add0(ve, g, i, 0)
            ve_add0(ve, g, i, 1)
            if not last:
                if i == 14:
                    for n in range(3):
                        ve_k(ve, g + 1, n)
                if i == 15:
                    for n in range(3):
                        ve_v(ve, g + 1, n)

        def ve_attn0(ve):
            for n in range(3):
                ve_k(ve, 0, n)
            for n in range(3):
                ve_v(ve, 0, n)
            for blk in range(QLEAD):
                ve_q(ve, 0, blk)
            for j in range(4):
                ve_max(ve, 0, 0, j)
            ve_norm(ve, 0, 0)
            with ve.Fori(0, KV0 - 1) as g:
                for i in range(UNITS0):
                    ve_unit0(ve, g, i, False)
            for i in range(UNITS0):
                ve_unit0(ve, KV0 - 1, i, True)

        def split_lo(po, dst, src, hi, done):
            po.tensor_tensor(dst, src, f32(hi), ALU.subtract).then_inc(done, 1)

        def po_wq(po, g, pair):
            po.wait_ge(a_wq_hi, per_g(PAIRS0, g) + pair + 1)
            split_lo(po, wq_lo[:, pair % 2], stage[:, 2 * pair % RING, :].rearrange("p (c n) -> p c n", c=KC),
                     wq_hi[:, pair % 2], a_wq_lo)

        def po_wo(po, g, pair):
            po.wait_ge(a_wo_hi, per_g(PAIRS0, g) + pair + 1)
            split_lo(po, wo_lo[:, pair % 2], stage[:, (2 * pair + 1) % RING, :].rearrange("p (h n) -> p h n", h=2),
                     wo_hi[:, pair % 2], a_wo_lo)

        def po_wkv(po, hi, lo, hi_done, lo_done, n):
            po.wait_ge(hi_done, n)
            split_lo(po, lo[:, :, :, :], kv_stage[:, :, :, :], hi[:, :, :, :], lo_done)

        def po_dup(po, g, i):
            po.wait_ge(a_t, per_g(3 * UNITS0, g) + 3 * i)
            po.wait_ge(a_rec, per_g(UNITS0, g) + i + 1)
            src = prob[:, :, SEQ:KVL0].rearrange("p j (r n) -> p j r n", r=1).broadcast_to([P, 4, 2, CTX])
            r = rinv[:, :].rearrange("p (j r n) -> p j r n", r=1, n=1).broadcast_to([P, 4, 2, CTX])
            po.tensor_tensor(probn[:, :, SEQ:NCH0 * P].rearrange("p j (r n) -> p j r n", r=2), src, r,
                             ALU.mult).then_inc(a_dup, 1)

        def po_unit0(po, g, i, last):
            if not (last and i == UNITS0 - 1):
                po_dup(po, g, i + 1)
            p = i // 4
            if i % 4 == 1 and not (last and p + 1 >= PAIRS0):
                po_wo(po, g, p + 1)
            if i % 4 == 2 and not (last and p + 2 >= PAIRS0):
                po_wq(po, g, p + 2)
            if not last and i == 5:
                po_wkv(po, wkv_hi, wkv_lo, a_wkv_hi, a_wkv_lo, g + 2)

        def po_attn0(po):
            po_dup(po, 0, 0)
            with po.Fori(0, KV0 - 1) as g:
                for i in range(UNITS0):
                    po_unit0(po, g, i, False)
            for i in range(UNITS0):
                po_unit0(po, KV0 - 1, i, True)

        def steps(eng, nf, step):
            for half in range(2):
                first, end = half * nf, (half + 1) * nf
                step(first, first, 0, 0)
                rounds = (min(end - 2, 2 * nf - 4) - first) // 2
                with eng.Fori(0, rounds) as it:
                    for s in range(1, 3):
                        step(it * 2 + (first + s), first + s, it, RING)
                for m in range(first + 2 * rounds + 1, end):
                    step(m, m, 0, 0)

        def pe_gu(pe, n, m, ms):
            t, s = ffn_t[n], F[n]
            par, half = ms % 2, ms // NFS[n]
            pe.wait_ge(s["gu_lo" if n == 0 else "gu_hi"], m + 1)
            pe.wait_ge(s["h"], m + 1)
            for w, banks, done in ((0, ffn_g, s["gate"]), (1, ffn_u, s["up"])):
                def part(name):
                    return (lambda c: t[name][:, par, w, c, :]) if name in t else None
                project(pe, banks[par][:, :], (part("gu_hi"), part("gu_lo")),
                        (lambda c: xT_hi[:, c, half * 512:(half + 1) * 512],
                         lambda c: xT_lo[:, c, half * 512:(half + 1) * 512])).then_inc(done, 1)

        def pe_down(pe, n, m, ms):
            nf, t, s = NFS[n], ffn_t[n], F[n]
            par, f, half = ms % 2, ms % nf, ms // nf
            pe.wait_ge(s["h_lo"], m + 1)
            pe.wait_ge(s["wd_lo" if n == 0 else "wd_hi"], m + 1)
            passes = [("h_hi", "wd_hi"), ("h_lo", "wd_hi")] + ([("h_hi", "wd_lo")] if n == 0 else [])
            for q in range(4):
                if f == 0 and half == 1:
                    pe.wait_ge(s["x"], q + 1)
                for k, (h, w) in enumerate(passes):
                    mm = pe.matmul(ffn_acc[q][:, :], t[h][:, par, q * P:(q + 1) * P], t[w][:, par, :],
                                   start=f == 0 and k == 0, stop=f == nf - 1 and k == len(passes) - 1)
                if f == nf - 1:
                    mm.then_inc(s["acc"], 1)
            if f != nf - 1:
                mm.then_inc(s["down"], 1)

        def pe_ffn(pe, n, k):
            pe.wait_ge(l_lo, NT * k + NT // 2)
            pe_gu(pe, n, 0, 0)
            pe.wait_ge(l_lo, NT * k + NT)

            def step(m, ms, it, per):
                if ms + 1 < 2 * NFS[n]:
                    pe_gu(pe, n, m + 1, ms + 1)
                pe_down(pe, n, m, ms)
            steps(pe, NFS[n], step)

        def ac_gu(ac, n, m, ms, it, per):
            t, s = ffn_t[n], F[n]
            k = ffn_at[n]["gu", ms]
            chunk_wait(ac, k, per, it)
            if ms >= 2:
                ac.wait_ge(s["up"], m - 1)
            ac.activation(t["gu_hi"][:, ms % 2], gu_view(slot(k) if n == 0 else slot16(k)),
                          ACT.Copy).then_inc(s["gu_hi"], 1)

        def ac_wd(ac, n, m, ms, it, per):
            nf, t, s = NFS[n], ffn_t[n], F[n]
            k = ffn_at[n]["wd", ms]
            chunk_wait(ac, k, per, it)
            if ms >= 2:
                half, f = divmod(ms - 2, nf)
                if f == nf - 1:
                    ac.wait_ge(s["acc"], 4 * (half + 1))
                else:
                    ac.wait_ge(s["down"], m - 1 - half)
            ac.activation(t["wd_hi"][:, ms % 2, :], (slot(k) if n == 0 else slot16(k))[:, 0:DM],
                          ACT.Copy).then_inc(s["wd_hi"], 1)

        def ac_silu(ac, n, m, ms):
            t, s = ffn_t[n], F[n]
            half = ms // NFS[n]
            ac.wait_ge(s["gate"], m + 1)
            scale = ag_sb[:, bass.ds(m - half * NFS[n], 1)] if n == 0 else 1.0
            ac.activation(t["s"][:, ms % 2, :], ffn_g[ms % 2][:, :], ACT.Silu, scale=scale).then_inc(s["silu"], 1)
            ac.wait_ge(s["h"], m + 3)
            ac.activation(t["h_hi"][:, ms % 2, :], t["h"][:, ms % 2, :], ACT.Copy).then_inc(s["h_hi"], 1)

        def ac_ffn(ac, n, k, before):
            total = 2 * NFS[n]
            ac.sem_inc(F[n]["h"], 2)
            before()
            ac_gu(ac, n, 0, 0, 0, 0)
            ln_scalar(ac, k)
            ac_gu(ac, n, 1, 1, 0, 0)
            ac_wd(ac, n, 0, 0, 0, 0)
            ac_silu(ac, n, 0, 0)
            ac_gu(ac, n, 2, 2, 0, 0)
            ac_wd(ac, n, 1, 1, 0, 0)

            def step(m, ms, it, per):
                if ms + 1 < total:
                    ac_silu(ac, n, m + 1, ms + 1)
                if ms + 3 < total:
                    ac_gu(ac, n, m + 3, ms + 3, it, per)
                if ms + 2 < total:
                    ac_wd(ac, n, m + 2, ms + 2, it, per)
            steps(ac, NFS[n], step)

        def ve_h(ve, n, m, ms):
            t, s = ffn_t[n], F[n]
            half, par = ms // NFS[n], ms % 2
            ve.wait_ge(s["up"], m + 1)
            ve.wait_ge(s["silu"], m + 1)
            if n == 0:
                ve.scalar_tensor_tensor(out=t["h"][:, par, :], in0=ffn_u[par][:, :],
                                        scalar=au_sb[:, bass.ds(m - half * NFS[n], 1)], in1=t["s"][:, par, :],
                                        op0=ALU.mult, op1=ALU.mult).then_inc(s["h"], 1)
            else:
                ve.tensor_tensor(t["h"][:, par, :], ffn_u[par][:, :], t["s"][:, par, :], ALU.mult).then_inc(s["h"], 1)
            ve.wait_ge(s["h_hi"], m + 1)
            ve.tensor_tensor(t["h_lo"][:, par, :], t["h"][:, par, :], f32(t["h_hi"][:, par, :]),
                             ALU.subtract).then_inc(s["h_lo"], 1)

        def ve_ffn_x(ve, n, half):
            t, s = ffn_t[n], F[n]
            for q in range(4):
                tile = 4 * half + q
                ve.wait_ge(s["acc"], tile + 1)
                if n == 0:
                    if tile >= 2:
                        ve.wait_ge(s["x"], tile - 1)
                    ve.tensor_tensor(t["scaled"][:, q % 2, :], ffn_acc[q][:, :], t["tgad"][:, :],
                                     ALU.mult).then_inc(s["scaled"], 1)
                    ve.wait_ge(s["scaled"], tile + 1)
                    ve.tensor_tensor(x_sb[:, tile, :], x_sb[:, tile, :], t["scaled"][:, q % 2, :],
                                     ALU.add).then_inc(s["x"], 1)
                else:
                    ve.scalar_tensor_tensor(out=x_sb[:, tile, :], in0=ffn_acc[q][:, :], scalar=tg[:, 3:4],
                                            in1=x_sb[:, tile, :], op0=ALU.mult, op1=ALU.add).then_inc(s["x"], 1)

        def ve_ffn(ve, n):
            nf = NFS[n]
            ve_h(ve, n, 0, 0)

            def step(m, ms, it, per):
                if ms + 1 < 2 * nf:
                    ve_h(ve, n, m + 1, ms + 1)
                if ms % nf == nf - 1:
                    ve_ffn_x(ve, n, ms // nf)
            steps(ve, nf, step)

        def po_gu(po, m, ms):
            t, s = ffn_t[0], F[0]
            po.wait_ge(s["gu_hi"], m + 1)
            split_lo(po, t["gu_lo"][:, ms % 2], gu_view(slot(ffn_at[0]["gu", ms])), t["gu_hi"][:, ms % 2], s["gu_lo"])

        def po_wd(po, m, ms):
            t, s = ffn_t[0], F[0]
            po.wait_ge(s["wd_hi"], m + 1)
            split_lo(po, t["wd_lo"][:, ms % 2, :], slot(ffn_at[0]["wd", ms])[:, 0:DM], t["wd_hi"][:, ms % 2, :],
                     s["wd_lo"])

        def po_ffn0(po):
            total = 2 * NF0
            po_gu(po, 0, 0)
            ln_gpsimd(po, 1)
            po_gu(po, 1, 1)
            po_wd(po, 0, 0)
            po_gu(po, 2, 2)
            po_wd(po, 1, 1)

            def step(m, ms, it, per):
                if ms + 3 < total:
                    po_gu(po, m + 3, ms + 3)
                if ms + 2 < total:
                    po_wd(po, m + 2, ms + 2)
            steps(po, NF0, step)

        UN = 2 * BATCH
        PASSES = KV1 // 2

        def pe_q1(pe, it, i, c):
            par, b = (i // 4) % 2, i % 4
            t = TB * b + c
            if b == 0 and c == 0:
                pe.wait_ge(b_wq_lo, it * 4 + 2 * (i // 4) + 2)
            pe.wait_ge(b_acc, it * (2 * UN) + 2 * i + c + 1)
            project(pe, (bank_a, bank_b)[c][:, :],
                    (lambda k: xT_hi[:, k, t * P:(t + 1) * P], lambda k: xT_lo[:, k, t * P:(t + 1) * P]),
                    (lambda k: wq1_hi[:, par, k, :], lambda k: wq1_lo[:, par, k, :])).then_inc(b_q, 1)

        def pe_q1T(pe, it, i, c):
            pe.wait_ge(b_qcp, it * (2 * UN) + 2 * i + c + 1)
            for h in range(GH1):
                mm = pe.transpose((bank_o, bank_t[0])[c][:, h * P:(h + 1) * P], q_row[:, c, h * HD:(h + 1) * HD],
                                  ident[:, :])
            mm.then_inc(b_qT, 1)

        def pe_s1(pe, it, i, c):
            par, b = (i // 4) % 2, i % 4
            if c == 0:
                pe.wait_ge(b_log, it * UN + i)
                if b == 0:
                    pe.wait_ge(b_klo, it * 2 + i // 4 + 1)
            pe.wait_ge(b_qTlo, it * (2 * UN) + 2 * i + c + 1)
            for h in range(GH1):
                for n, (q, kk) in enumerate(((q1T_hi, k1_hi), (q1T_hi, k1_lo), (q1T_lo, k1_hi))):
                    mm = pe.matmul(s1_bank[:, (c * GH1 + h) * CTX:(c * GH1 + h + 1) * CTX],
                                   q[:, c, h * P:(h + 1) * P], kk[:, par, b * CTX:(b + 1) * CTX],
                                   start=n == 0, stop=n == 2)
            if c == 1:
                mm.then_inc(b_s, 1)

        def pe_p1T(pe, it, i):
            pe.wait_ge(b_norm, it * UN + i + 1)
            for hp in range(2):
                for hl in range(2):
                    for c in range(TB):
                        mm = pe.transpose(bank_t[hp][:, (hl * TB + c) * P:(hl * TB + c + 1) * P],
                                          prob1n[:, c * GH1 + 2 * hp + hl].rearrange("p r n -> p (r n)"), ident[:, :])
                mm.then_inc(b_t, 1)

        def pe_pv1(pe, it, i, nxt):
            par, b = (i // 4) % 2, i % 4
            if b == 0:
                pe.wait_ge(b_vlo, it * 2 + i // 4 + 1)
            for hp in range(2):
                pe.wait_ge(b_tlo, it * (2 * UN) + 2 * i + hp + 1)
                if hp == 0 and nxt:
                    pe.wait_ge(b_qTlo, it * (2 * UN) + 2 * (i + 1) + 1)
                for n, v in enumerate((v1_hi, v1_lo)):
                    mm = pe.matmul(o1_bank[hp][:, :], v[:, par, b, :], p1T[:, hp, :], start=n == 0, stop=n == 1)
                mm.then_inc(b_pv, 1)

        def pe_wo1(pe, it, i, c, nxt):
            par, b = (i // 4) % 2, i % 4
            if c == 0:
                if b == 0:
                    pe.wait_ge(b_wo_lo, it * 4 + 2 * (i // 4) + 2)
                pe.wait_ge(b_olo, it * (2 * UN) + 2 * i + 2)
            if nxt:
                pe.wait_ge(b_qsq, it * (2 * UN) + 2 * (i + 1) + c + 1)
            else:
                pe.wait_ge(b_acc, it * (2 * UN) + 2 * i + c + 3)
            for h in range(GH1):
                q0 = (h % 2) * SEQ + c * P
                for n, (o, w) in enumerate(((o1T_hi, wo1_hi), (o1T_hi, wo1_lo), (o1T_lo, wo1_hi))):
                    mm = pe.matmul((bank_a, bank_b)[c][:, :], o[:, h // 2, q0:q0 + P], w[:, par, h, :],
                                   start=h == 0 and n == 0, stop=h == GH1 - 1 and n == 2)
            mm.then_inc(b_wo, 1)

        def pe_krow(pe, jj):
            pe.wait_ge(b_wkv_lo, jj + 1)
            pe.wait_ge(b_vlo, jj)
            for c in range(2):
                mm = project(pe, kv1_bank[:, c * HD:(c + 1) * HD],
                             (lambda k: cT_hi[:, k, c * P:(c + 1) * P], lambda k: cT_lo[:, k, c * P:(c + 1) * P]),
                             (lambda k: wkv1_hi[:, 0, k, :], lambda k: wkv1_lo[:, 0, k, :]))
            mm.then_inc(b_kr, 1)

        def pe_kT(pe, jj):
            pe.wait_ge(b_kn, jj + 1)
            for c in range(2):
                mm = pe.transpose(kv1_bank[:, c * P:(c + 1) * P], k_row[:, c, :], ident[:, :])
            mm.then_inc(b_kT, 1)

        def pe_v1T(pe, jj):
            pe.wait_ge(b_klo, jj + 1)
            project(pe, kv1_bank[:, 0:BATCH * CTX],
                    (lambda k: wkv1_hi[:, 1, k, :], lambda k: wkv1_lo[:, 1, k, :]),
                    (lambda k: cT_hi[:, k, :], lambda k: cT_lo[:, k, :])).then_inc(b_vT, 1)

        def pe_v1(pe, jj):
            pe.wait_ge(b_vTc, jj + 1)
            for b in range(BATCH):
                mm = pe.transpose(kv1_bank[:, b * HD:(b + 1) * HD], v1T[:, b, :], ident[:, :])
            mm.then_inc(b_v, 1)

        def has_next_head(last, i):
            return not (last and i // 4 == 1)

        def pe_unit1(pe, it, i, last):
            nxt = not (last and i == UN - 1)
            if nxt:
                pe_q1(pe, it, i + 1, 0)
            pe_p1T(pe, it, i)
            if nxt:
                pe_q1T(pe, it, i + 1, 0)
                pe_q1(pe, it, i + 1, 1)
            pe_pv1(pe, it, i, nxt)
            if nxt:
                pe_q1T(pe, it, i + 1, 1)
                pe_s1(pe, it, i + 1, 0)
            pe_wo1(pe, it, i, 0, nxt)
            if nxt:
                pe_s1(pe, it, i + 1, 1)
            pe_wo1(pe, it, i, 1, nxt)
            if has_next_head(last, i):
                (pe_krow, pe_kT, pe_v1T, pe_v1)[i % 4](pe, it * 2 + i // 4 + 1)

        def pe_attn1(pe):
            pe.wait_ge(l_lo, 2 * NT + NT)
            pe_krow(pe, 0)
            pe_q1(pe, 0, 0, 0)
            pe_q1(pe, 0, 0, 1)
            pe_kT(pe, 0)
            pe_q1T(pe, 0, 0, 0)
            pe_q1T(pe, 0, 0, 1)
            pe_v1T(pe, 0)
            pe_s1(pe, 0, 0, 0)
            pe_s1(pe, 0, 0, 1)
            pe_v1(pe, 0)
            with pe.Fori(0, PASSES - 1) as it:
                for i in range(UN):
                    pe_unit1(pe, it, i, False)
            for i in range(UN):
                pe_unit1(pe, PASSES - 1, i, True)

        def ac_q1(ac, it, i, c):
            n = it * (2 * UN) + 2 * i + c
            src = (bank_a, bank_b)[c][:, :]
            ac.wait_ge(b_q, n + 1)
            ac.activation(q_row[:, c, :], src, ACT.Copy).then_inc(b_qcp, 1)
            ac.wait_ge(b_ss, n + 1)
            ac.activation(q_sq[:, :], src, ACT.Square).then_inc(b_qsq, 1)

        def ac_q1T(ac, it, i, c):
            ac.wait_ge(b_qT, it * (2 * UN) + 2 * i + c + 1)
            ac.activation(q1T_hi[:, c, :], (bank_o, bank_t[0])[c][:, :], ACT.Copy).then_inc(b_qThi, 1)

        def ac_exp1(ac, it, i):
            ac.wait_ge(b_sub, it * UN + i + 1)
            ac.activation(prob1[:, :, :], logit[:, :, :], ACT.Exp).then_inc(b_exp, 1)

        def ac_kv1(ac, job, jj, par):
            src = kv1_bank[:, 0:2 * HD].rearrange("p (c n) -> p c n", c=2)
            if job == 0:
                ac.wait_ge(b_kr, jj + 1)
                ac.activation(k_row[:, :, :], src, ACT.Copy).then_inc(b_krc, 1)
                ac.activation(k_sq[:, :, :], src, ACT.Square).then_inc(b_krs, 1)
            elif job == 1:
                ac.wait_ge(b_kT, jj + 1)
                ac.activation(k1_hi[:, par, :], kv1_bank[:, 0:BATCH * CTX], ACT.Identity,
                              scale=kscale[:, 0:1]).then_inc(b_khi, 1)
            elif job == 2:
                ac.wait_ge(b_vT, jj + 1)
                twice = kv1_bank[:, 0:BATCH * CTX].rearrange("p (b r n) -> p b r n", b=BATCH, r=1)
                ac.activation(v1T[:, :, :].rearrange("p b (r n) -> p b r n", r=2),
                              twice.broadcast_to([P, BATCH, 2, CTX]), ACT.Copy).then_inc(b_vTc, 1)
            else:
                ac.wait_ge(b_v, jj + 1)
                ac.activation(v1_hi[:, par], kv1_bank[:, :].rearrange("p (b n) -> p b n", b=BATCH),
                              ACT.Copy).then_inc(b_vhi, 1)

        def ac_wq1(ac, it, jl, q):
            k = l1_base + 4 * jl + q
            chunk_wait(ac, k, 8, it)
            if jl >= 2:
                ac.wait_ge(b_q, it * (2 * UN) + 2 * BATCH * (jl - 1))
            split_hi(ac, wq1_hi[:, jl % 2, 2 * q:2 * q + 2, :], slot(k).rearrange("p (c n) -> p c n", c=2), b_wq_hi)

        def ac_wo1(ac, it, jl, q):
            k = l1_base + 4 * jl + 2 + q
            chunk_wait(ac, k, 8, it)
            if jl >= 1:
                ac.wait_ge(b_wo, it * (2 * UN) + 2 * BATCH * (jl - 1) + 1)
            split_hi(ac, wo1_hi[:, jl % 2, 2 * q:2 * q + 2, :], slot(k).rearrange("p (h n) -> p h n", h=2), b_wo_hi)

        def ac_unit1(ac, it, i, last):
            nxt = not (last and i == UN - 1)
            if nxt:
                ac_q1(ac, it, i + 1, 0)
            for hp in range(2):
                ac.wait_ge(b_t, it * (2 * UN) + 2 * i + hp + 1)
                ac.activation(p1T[:, hp, :], bank_t[hp][:, :], ACT.Copy).then_inc(b_thi, 1)
            if nxt:
                ac_q1T(ac, it, i + 1, 0)
                ac_q1(ac, it, i + 1, 1)
            for hp in range(2):
                ac.wait_ge(b_pv, it * (2 * UN) + 2 * i + hp + 1)
                ac.activation(o1T_hi[:, hp, :], o1_bank[hp][:, :], ACT.Copy).then_inc(b_ohi, 1)
            if nxt:
                ac_q1T(ac, it, i + 1, 1)
            jl, b = i // 4, i % 4
            if b < 2 and not (last and jl == 1):
                ac_wo1(ac, it, jl + 1, b)
            if nxt:
                ac_exp1(ac, it, i + 1)
            if has_next_head(last, i):
                ac_kv1(ac, b, it * 2 + jl + 1, (jl + 1) % 2)
            if b == 3 and not last:
                ac_wq1(ac, it, jl + 2, 0)
                ac_wq1(ac, it, jl + 2, 1)
                ac.wait_ge(b_vT, it * 2 + jl + 2)
                ac_wkv(ac, it * 2 + (KV0 + jl + 2), wkv1_hi, b_wkv_hi)

        def ac_attn1(ac):
            ac.sem_inc(b_ss, 1)
            ac.wait_ge(F[0]["x"], NT)
            ac_wkv(ac, KV0, wkv1_hi, b_wkv_hi)
            ac_wq1(ac, 0, 0, 0)
            ac_wq1(ac, 0, 0, 1)
            ln_scalar(ac, 2)
            ac_kv1(ac, 0, 0, 0)
            ac_q1(ac, 0, 0, 0)
            ac_q1(ac, 0, 0, 1)
            ac_kv1(ac, 1, 0, 0)
            ac_q1T(ac, 0, 0, 0)
            ac_q1T(ac, 0, 0, 1)
            ac_kv1(ac, 2, 0, 0)
            ac_wo1(ac, 0, 0, 0)
            ac_wo1(ac, 0, 0, 1)
            ac_wkv(ac, KV0 + 1, wkv1_hi, b_wkv_hi)
            ac_wq1(ac, 0, 1, 0)
            ac_wq1(ac, 0, 1, 1)
            ac_exp1(ac, 0, 0)
            ac_kv1(ac, 3, 0, 0)
            with ac.Fori(0, PASSES - 1) as it:
                for i in range(UN):
                    ac_unit1(ac, it, i, False)
            for i in range(UN):
                ac_unit1(ac, PASSES - 1, i, True)

        def ve_ss(ve, it, i, c):
            n = it * (2 * UN) + 2 * i + c
            ve.wait_ge(b_qsq, n + 1)
            ve.tensor_reduce(q_ss[:, c * GH1:(c + 1) * GH1], q_sq[:, :].rearrange("p (h n) -> p h n", h=GH1), AX_X,
                             ALU.add).then_inc(b_ss, 1)
            if c == 1:
                ve.wait_ge(b_ss, n + 2)
                ve.tensor_scalar(q_var[:, :], q_ss[:, :], 1.0 / HD, EPS, ALU.mult, ALU.add).then_inc(b_var, 1)

        def ve_q1T(ve, it, i, c):
            ve.wait_ge(b_qThi, it * (2 * UN) + 2 * i + c + 1)
            ve.tensor_tensor(q1T_lo[:, c, :], (bank_o, bank_t[0])[c][:, :], f32(q1T_hi[:, c, :]),
                             ALU.subtract).then_inc(b_qTlo, 1)

        def wide(ap, n):
            a = ap.shape[1]
            return ap.rearrange("p (a n) -> p a n", n=1).broadcast_to([P, a, n])

        def ve_logit(ve, it, i):
            n = it * UN + i + 1
            ve.wait_ge(b_s, n)
            ve.wait_ge(b_rms, n)
            ve.tensor_tensor(logit[:, :, :], s1_bank[:, :].rearrange("p (a n) -> p a n", n=CTX),
                             wide(q_rms[:, :], CTX), ALU.mult).then_inc(b_log, 1)
            ve.wait_ge(b_log, n)
            m = mask_sb[:, :, :].rearrange("p c (h n) -> p c h n", h=1).broadcast_to([P, TB, GH1, CTX])
            l4 = logit[:, :, :].rearrange("p (c h) n -> p c h n", c=TB)
            ve.tensor_tensor(l4, l4, m, ALU.add).then_inc(b_mask, 1)
            ve.wait_ge(b_mask, n)
            ve.tensor_reduce(mx1[:, :], logit[:, :, :], AX_X, ALU.max).then_inc(b_max, 1)
            ve.wait_ge(b_max, n)
            ve.tensor_tensor(logit[:, :, :], logit[:, :, :], wide(mx1[:, :], CTX), ALU.subtract).then_inc(b_sub, 1)

        def ve_norm1(ve, it, i):
            n = it * UN + i + 1
            ve.wait_ge(b_exp, n)
            ve.tensor_reduce(sum1[:, :], prob1[:, :, :], AX_X, ALU.add).then_inc(b_sum, 1)
            ve.wait_ge(b_sum, n)
            ve.reciprocal(rinv1[:, :], sum1[:, :]).then_inc(b_rec, 1)
            ve.wait_ge(b_rec, n)
            ve.wait_ge(b_t, it * (2 * UN) + 2 * i)
            src = prob1[:, :, :].rearrange("p a (r n) -> p a r n", r=1).broadcast_to([P, TB * GH1, 2, CTX])
            r = rinv1[:, :].rearrange("p (a r n) -> p a r n", r=1, n=1).broadcast_to([P, TB * GH1, 2, CTX])
            ve.tensor_tensor(prob1n[:, :, :, :], src, r, ALU.mult).then_inc(b_norm, 1)

        def ve_add1(ve, it, i, c):
            t = TB * (i % 4) + c
            ve.wait_ge(b_wo, it * (2 * UN) + 2 * i + c + 1)
            ve.scalar_tensor_tensor(out=x_sb[:, t, :], in0=(bank_a, bank_b)[c][:, :], scalar=tg[:, 1:2],
                                    in1=x_sb[:, t, :], op0=ALU.mult, op1=ALU.add).then_inc(b_acc, 1)

        def ve_kv1(ve, job, jj, par):
            if job == 0:
                ve.wait_ge(b_krs, jj + 1)
                ve.tensor_reduce(k_ss[:, :], k_sq[:, :, :], AX_X, ALU.add).then_inc(b_kss, 1)
                ve.wait_ge(b_kss, jj + 1)
                ve.tensor_scalar(k_var[:, :], k_ss[:, :], 1.0 / HD, EPS, ALU.mult, ALU.add).then_inc(b_kvar, 1)
            elif job == 1:
                ve.wait_ge(b_khi, jj + 1)
                ve.scalar_tensor_tensor(out=k1_lo[:, par, :], in0=kv1_bank[:, 0:BATCH * CTX], scalar=kscale[:, 0:1],
                                        in1=f32(k1_hi[:, par, :]), op0=ALU.mult, op1=ALU.subtract).then_inc(b_klo, 1)
            elif job == 3:
                ve.wait_ge(b_vhi, jj + 1)
                ve.tensor_tensor(v1_lo[:, par], kv1_bank[:, :].rearrange("p (b n) -> p b n", b=BATCH),
                                 f32(v1_hi[:, par]), ALU.subtract).then_inc(b_vlo, 1)

        def ve_knorm(ve, jj):
            ve.wait_ge(b_krms, jj + 1)
            ve.tensor_tensor(k_row[:, :, :], k_row[:, :, :], wide(k_rms[:, :], HD), ALU.mult).then_inc(b_kn, 1)

        def ve_unit1(ve, it, i, last):
            nxt = not (last and i == UN - 1)
            jj, par = it * 2 + i // 4 + 1, (i // 4 + 1) % 2
            if nxt:
                ve_ss(ve, it, i + 1, 0)
            if i % 4 == 1 and has_next_head(last, i):
                ve_knorm(ve, jj)
            for hp in range(2):
                ve.wait_ge(b_thi, it * (2 * UN) + 2 * i + hp + 1)
                ve.tensor_tensor(p1T[CTX:P, hp, :], bank_t[hp][CTX:P, :], f32(p1T[CTX:P, hp, :]),
                                 ALU.subtract).then_inc(b_tlo, 1)
            if nxt:
                ve_q1T(ve, it, i + 1, 0)
                ve_ss(ve, it, i + 1, 1)
            for hp in range(2):
                ve.wait_ge(b_ohi, it * (2 * UN) + 2 * i + hp + 1)
                ve.tensor_tensor(o1T_lo[:, hp, :], o1_bank[hp][:, :], f32(o1T_hi[:, hp, :]),
                                 ALU.subtract).then_inc(b_olo, 1)
            if nxt:
                ve_q1T(ve, it, i + 1, 1)
            ve_add1(ve, it, i, 0)
            if nxt:
                ve_logit(ve, it, i + 1)
                ve_norm1(ve, it, i + 1)
            ve_add1(ve, it, i, 1)
            if has_next_head(last, i):
                ve_kv1(ve, i % 4, jj, par)

        def ve_attn1(ve):
            ve_kv1(ve, 0, 0, 0)
            ve_ss(ve, 0, 0, 0)
            ve_knorm(ve, 0)
            ve_ss(ve, 0, 0, 1)
            ve_kv1(ve, 1, 0, 0)
            ve_q1T(ve, 0, 0, 0)
            ve_q1T(ve, 0, 0, 1)
            ve_logit(ve, 0, 0)
            ve_norm1(ve, 0, 0)
            ve_kv1(ve, 3, 0, 0)
            with ve.Fori(0, PASSES - 1) as it:
                for i in range(UN):
                    ve_unit1(ve, it, i, False)
            for i in range(UN):
                ve_unit1(ve, PASSES - 1, i, True)

        def po_pow(po, out_ap, in_ap, done, wait, value):
            po.wait_ge(wait, value)
            po.tensor_tensor(out_ap, in_ap, neg_half[:, 0:in_ap.shape[1]], ALU.pow).then_inc(done, 1)

        def po_wq1(po, it, jl, q):
            po.wait_ge(b_wq_hi, it * 4 + 2 * jl + q + 1)
            split_lo(po, wq1_lo[:, jl % 2, 2 * q:2 * q + 2, :],
                     slot(l1_base + 4 * jl + q).rearrange("p (c n) -> p c n", c=2),
                     wq1_hi[:, jl % 2, 2 * q:2 * q + 2, :], b_wq_lo)

        def po_wo1(po, it, jl, q):
            po.wait_ge(b_wo_hi, it * 4 + 2 * jl + q + 1)
            split_lo(po, wo1_lo[:, jl % 2, 2 * q:2 * q + 2, :],
                     slot(l1_base + 4 * jl + 2 + q).rearrange("p (h n) -> p h n", h=2),
                     wo1_hi[:, jl % 2, 2 * q:2 * q + 2, :], b_wo_lo)

        def po_unit1(po, it, i, last):
            nxt = not (last and i == UN - 1)
            jl, b = i // 4, i % 4
            jj = it * 2 + jl + 1
            if b == 1 and has_next_head(last, i):
                po_pow(po, k_rms[:, :], k_var[:, :], b_krms, b_kvar, jj + 1)
            if nxt:
                po_pow(po, q_rms[:, :], q_var[:, :], b_rms, b_var, it * UN + i + 2)
            if b < 2 and not (last and jl == 1):
                po_wo1(po, it, jl + 1, b)
            if b == 3 and not last:
                po_wq1(po, it, jl + 2, 0)
                po_wq1(po, it, jl + 2, 1)
                po_wkv(po, wkv1_hi, wkv1_lo, b_wkv_hi, b_wkv_lo, it * 2 + jl + 3)

        def po_attn1(po):
            po_wkv(po, wkv1_hi, wkv1_lo, b_wkv_hi, b_wkv_lo, 1)
            ln_gpsimd(po, 2)
            po_wq1(po, 0, 0, 0)
            po_wq1(po, 0, 0, 1)
            po_pow(po, k_rms[:, :], k_var[:, :], b_krms, b_kvar, 1)
            po_pow(po, q_rms[:, :], q_var[:, :], b_rms, b_var, 1)
            po_wo1(po, 0, 0, 0)
            po_wo1(po, 0, 0, 1)
            po_wkv(po, wkv1_hi, wkv1_lo, b_wkv_hi, b_wkv_lo, 2)
            po_wq1(po, 0, 1, 0)
            po_wq1(po, 0, 1, 1)
            with po.Fori(0, PASSES - 1) as it:
                for i in range(UN):
                    po_unit1(po, it, i, False)
            for i in range(UN):
                po_unit1(po, PASSES - 1, i, True)

        @block.gpsimd
        def _(po):
            po.memset(neg_half[:, :], -0.5).then_inc(s_half, 1)
            po.memset(ident[:, :], 0.0).then_inc(s_ident, 1)
            po.wait_ge(s_ident, 1)
            po.affine_select(out=ident[:, :], in_=ident[:, :], compare_op=ALU.not_equal, fill=1.0, base=0,
                             pattern=[[-1, P]], channel_multiplier=1).then_inc(s_ident, 1)
            po.wait_ge(s_half, 1)
            po_wkv(po, wkv_hi, wkv_lo, a_wkv_hi, a_wkv_lo, 1)
            ln_gpsimd(po, 0)
            po.wait_ge(s_chi, 1)
            split_lo(po, cT_lo[:, :, :], prob[:, :, 0:BATCH * CTX], cT_hi[:, :, :], s_clo)
            po_wq(po, 0, 0)
            po_wo(po, 0, 0)
            po_wq(po, 0, 1)
            po_attn0(po)
            po_ffn0(po)
            po_attn1(po)
            ln_gpsimd(po, 3)

        @block.scalar
        def _(ac):
            ac.sem_inc(a_exp, 2)
            ac_wkv(ac, 0, wkv_hi, a_wkv_hi)
            ac.wait_ge(s_ctx, 16)
            split_hi(ac, cT_hi[:, :, :], prob[:, :, 0:BATCH * CTX], s_chi)
            ln_scalar(ac, 0)
            ac_wq(ac, 0, 0)
            ac_wo(ac, 0, 0)
            ac_wq(ac, 0, 1)
            ac.wait_ge(s_small, 16 * 7)
            ac.activation(tg[:, :], gates[:, :], ACT.Tanh).then_inc(s_tg, 1)
            ac_attn0(ac)
            ac_ffn(ac, 0, 1, lambda: ac.wait_ge(a_acc, 2 * KV0 * UNITS0 + 2))
            ac_attn1(ac)
            ac_ffn(ac, 1, 3, lambda: ac.wait_ge(b_acc, 4 + 2 * UN * PASSES))

        @block.vector
        def _(ve):
            ve.sem_inc(b_acc, 4)
            ve.sem_inc(a_acc, 2)
            ve.sem_inc(a_olo, 1)
            ln_vector(ve, 0, lambda t: ve.wait_ge(s_x[t], 16))
            ve.wait_ge(s_small, 16 * 7)
            ve.scalar_tensor_tensor(out=kscale[:, :], in0=qn_w[:, :], scalar=SCALE, in1=kn_w[:, :], op0=ALU.mult,
                                    op1=ALU.mult).then_inc(s_ksc, 1)
            ve.wait_ge(s_tg, 1)
            ve.wait_ge(s_ksc, 1)
            ve_attn0(ve)
            ln_vector(ve, 1, lambda t: ve.wait_ge(a_acc, 2 * KV0 * UNITS0 + 2 - NT + t + 1))
            ve.wait_ge(s_ad, 16)
            ve.tensor_scalar(ffn_t[0]["tgad"][:, :], ffn_t[0]["ad"][:, :], tg[:, 2:3], None,
                             ALU.mult).then_inc(F[0]["tgad"], 1)
            ve.wait_ge(F[0]["tgad"], 1)
            ve_ffn(ve, 0)
            ln_vector(ve, 2, lambda t: ve.wait_ge(F[0]["x"], t + 1))
            ve_attn1(ve)
            ln_vector(ve, 3, lambda t: ve.wait_ge(b_acc, 4 + 2 * UN * PASSES - NT + t + 1))
            ve_ffn(ve, 1)

        @block.tensor
        def _(pe):
            pe.wait_ge(s_ident, 2)
            ln_tensor(pe, 0)
            pe_attn0(pe)
            ln_tensor(pe, 1)
            pe_ffn(pe, 0, 1)
            ln_tensor(pe, 2)
            pe_attn1(pe)
            ln_tensor(pe, 3)
            pe_ffn(pe, 1, 3)


def kernel(x, ctx_4096, mask_1x1xSxS2_ff0, g_xattn, g_ffn, L0_xattn_Wq, L0_xattn_Wk, L0_xattn_Wv, L0_xattn_Wo,
           L0_ffn_Wg, L0_ffn_Wu, L0_ffn_Wd, L0_ffn_ag, L0_ffn_au, L0_ffn_ad, L1_xattn_q_proj_w, L1_xattn_k_proj_w,
           L1_xattn_v_proj_w, L1_xattn_o_proj_w, L1_xattn_q_norm_w, L1_xattn_k_norm_w, L1_ffn_W_gate, L1_ffn_W_up,
           L1_ffn_W_down):
    import numpy as np
    import concourse.bacc as bacc
    from concourse.bass_utils import run_bass_kernel_spmd

    def t(a):
        return np.ascontiguousarray(np.asarray(a).T)

    def padded(a, axis):
        a = np.asarray(a)
        width = [(0, 0)] * a.ndim
        width[axis] = (0, F0_PAD - F0)
        return np.pad(a, width)

    arrays = {
        "x": np.asarray(x).reshape(BATCH * SEQ, DM),
        "ctxT": t(np.asarray(ctx_4096).reshape(BATCH * CTX, DM)),
        "mask": np.asarray(mask_1x1xSxS2_ff0).reshape(SEQ, CTX),
        "g_xattn": np.asarray(g_xattn), "g_ffn": np.asarray(g_ffn),
        "wq0": np.asarray(L0_xattn_Wq), "wk0": np.asarray(L0_xattn_Wk),
        "wv0": np.asarray(L0_xattn_Wv), "wo0": np.asarray(L0_xattn_Wo),
        "wg0T": t(padded(L0_ffn_Wg, 0)), "wu0T": t(padded(L0_ffn_Wu, 0)), "wd0T": t(padded(L0_ffn_Wd, 1)),
        "ag": t(padded(L0_ffn_ag, 0).reshape(NF0, P)), "au": t(padded(L0_ffn_au, 0).reshape(NF0, P)),
        "ad": np.asarray(L0_ffn_ad),
        "wq1T": t(L1_xattn_q_proj_w), "wk1T": t(L1_xattn_k_proj_w), "wv1T": t(L1_xattn_v_proj_w),
        "wo1T": t(L1_xattn_o_proj_w),
        "qnorm": np.asarray(L1_xattn_q_norm_w).reshape(HD, 1), "knorm": np.asarray(L1_xattn_k_norm_w).reshape(HD, 1),
        "wg1T": t(L1_ffn_W_gate), "wu1T": t(L1_ffn_W_up), "wd1T": t(L1_ffn_W_down),
    }
    arrays = {f"in_{k}": np.ascontiguousarray(v) for k, v in arrays.items()}
    nc = bacc.Bacc("TRN2", target_bir_lowering=False, num_devices=1)
    aps = [nc.dram_tensor(k, v.shape, mybir.dt.from_np(v.dtype), kind="ExternalInput").ap() for k, v in arrays.items()]
    out = nc.dram_tensor("out_x", (BATCH * SEQ, DM), F32, kind="ExternalOutput").ap()
    flamingo_two_layers(nc, *aps, out)
    r = run_bass_kernel_spmd(nc, [arrays], core_ids=[0])
    return r.results[0]["out_x"].reshape(BATCH, SEQ, DM)
```

```python
from contextlib import ExitStack

import concourse.bass as bass
from concourse import mybir

F32 = mybir.dt.float32
F32R = mybir.dt.float32r
F16 = mybir.dt.float16
ALU = mybir.AluOpType
ACT = mybir.ActivationFunctionType
AX_X = mybir.AxisListType.X

P = 128
BATCH, SEQ, DM = 4, 256, 512
CTX = 64
HD = 128
HEADS = 32
KV0, KV1 = 4, 8
KC = DM // P
NT = BATCH * SEQ // P
TB = SEQ // P
KVL0 = SEQ + CTX
SCALE = float(HD) ** -0.5
EPS = 1e-5

RING = 4
CHUNK = 1024

PAIRS0 = HEADS // KV0 // 2
UNITS0 = PAIRS0 * BATCH
QLEAD = 3
NCH0 = 3

GH1 = HEADS // KV1

F0, F0_PAD = 1376, 1408
F1 = 1792
NF0, NF1 = F0_PAD // P, F1 // P


def flamingo_two_layers(nc, x, ctxT, mask, g_xattn, g_ffn, wq0, wk0, wv0, wo0, wg0T, wu0T, wd0T,
                        ag, au, ad, wq1T, wk1T, wv1T, wo1T, qnorm, knorm, wg1T, wu1T, wd1T, out):
    ctx = ExitStack()

    def sem(name):
        return ctx.enter_context(nc.semaphore(name))

    def sb(stack, name, shape, dt=F32):
        return stack.enter_context(nc.sbuf_tensor(name, shape, dt))

    def f32(ap):
        return ap.bitcast(F32)

    with ctx:
        x_sb = sb(ctx, "x_sb", [P, NT, DM])
        xT_hi = sb(ctx, "xT_hi", [P, KC, NT * P], F32R)
        xT_lo = sb(ctx, "xT_lo", [P, KC, NT * P], F32R)
        cT_hi = sb(ctx, "cT_hi", [P, KC, BATCH * CTX], F32R)
        cT_lo = sb(ctx, "cT_lo", [P, KC, BATCH * CTX], F32R)
        ident = sb(ctx, "ident", [P, P])
        stage = sb(ctx, "stage", [P, RING, CHUNK])
        kv_stage = sb(ctx, "kv_stage", [P, 2, KC, HD])
        ln_out = sb(ctx, "ln_out", [P, 2, DM])
        ln_stats = sb(ctx, "ln_stats", [P, NT, 6])
        ln_mv = sb(ctx, "ln_mv", [P, NT, 2])
        ln_var = sb(ctx, "ln_var", [P, NT])
        ln_rstd = sb(ctx, "ln_rstd", [P, NT])
        neg_half = sb(ctx, "neg_half", [P, NT])
        gates = sb(ctx, "gates", [P, 4])
        tg = sb(ctx, "tg", [P, 4])
        mask_sb = sb(ctx, "mask_sb", [P, TB, CTX])
        qn_w = sb(ctx, "qn_w", [P, 1])
        kn_w = sb(ctx, "kn_w", [P, 1])
        kscale = sb(ctx, "kscale", [P, 1])
        ag_sb = sb(ctx, "ag_sb", [P, NF0])
        au_sb = sb(ctx, "au_sb", [P, NF0])

        r0 = ExitStack()
        wq_hi = sb(r0, "wq_hi", [P, 2, KC, 2 * HD], F32R)
        wq_lo = sb(r0, "wq_lo", [P, 2, KC, 2 * HD], F32R)
        wo_hi = sb(r0, "wo_hi", [P, 2, 2, DM], F32R)
        wo_lo = sb(r0, "wo_lo", [P, 2, 2, DM], F32R)
        wkv_hi = sb(r0, "wkv_hi", [P, 2, KC, HD], F32R)
        wkv_lo = sb(r0, "wkv_lo", [P, 2, KC, HD], F32R)
        k_hi = sb(r0, "k_hi", [P, BATCH, KVL0], F32R)
        k_lo = sb(r0, "k_lo", [P, BATCH, KVL0], F32R)
        v_hi = sb(r0, "v_hi", [P, NT + BATCH, HD], F32R)
        v_lo = sb(r0, "v_lo", [P, NT + BATCH, HD], F32R)
        vT = sb(r0, "vT", [P, NT + BATCH, P])
        qT_hi = sb(r0, "qT_hi", [P, 4, 2 * SEQ], F32R)
        qT_lo = sb(r0, "qT_lo", [P, 4, 2 * SEQ], F32R)
        prob = sb(r0, "prob", [P, 4, KVL0])
        probn = sb(r0, "probn", [P, 4, NCH0 * P])
        pT_hi = sb(r0, "pT_hi", [P, NCH0, 2 * SEQ], F32R)
        pT_lo = sb(r0, "pT_lo", [P, 2, 2 * SEQ], F32R)
        oT_hi = sb(r0, "oT_hi", [P, 2 * SEQ], F32R)
        oT_lo = sb(r0, "oT_lo", [P, 2 * SEQ], F32R)
        nmax = sb(r0, "nmax", [P, 4])
        rsum = sb(r0, "rsum", [P, 4])
        rinv = sb(r0, "rinv", [P, 4])
        r0.close()

        def ffn_buffers(n, parts):
            r = ExitStack()
            t = {}
            for part in parts:
                t["gu_" + part] = sb(r, f"gu{n}_{part}", [P, 2, 2, KC, P], F32R)
                t["wd_" + part] = sb(r, f"wd{n}_{part}", [P, 2, DM], F32R)
            t["s"] = sb(r, f"silu{n}", [P, 2, 2 * SEQ])
            t["h"] = sb(r, f"h{n}", [P, 2, 2 * SEQ])
            t["h_hi"] = sb(r, f"h{n}_hi", [P, 2, 2 * SEQ], F32R)
            t["h_lo"] = sb(r, f"h{n}_lo", [P, 2, 2 * SEQ], F32R)
            if n == 0:
                t["ad"] = sb(r, "ad_row", [P, DM])
                t["tgad"] = sb(r, "tgad", [P, DM])
                t["scaled"] = sb(r, "scaled", [P, 2, DM])
            r.close()
            return t

        ffn_t = [ffn_buffers(0, ("hi", "lo")), ffn_buffers(1, ("hi",))]

        r1 = ExitStack()
        wq1_hi = sb(r1, "wq1_hi", [P, 2, KC, 2 * HD], F32R)
        wq1_lo = sb(r1, "wq1_lo", [P, 2, KC, 2 * HD], F32R)
        wo1_hi = sb(r1, "wo1_hi", [P, GH1, DM], F32R)
        wo1_lo = sb(r1, "wo1_lo", [P, GH1, DM], F32R)
        wkv1_hi = sb(r1, "wkv1_hi", [P, 2, KC, HD], F32R)
        wkv1_lo = sb(r1, "wkv1_lo", [P, 2, KC, HD], F32R)
        k1 = sb(r1, "k1", [P, BATCH, 2, CTX], F32R)
        v1_hi = sb(r1, "v1_hi", [P, 2, 3, CTX], F32R)
        v1_lo = sb(r1, "v1_lo", [P, 2, 3, CTX], F32R)
        vw_hi = sb(r1, "vw_hi", [P, 2, 2, 2, DM], F32R)
        vw_lo = sb(r1, "vw_lo", [P, 2, 2, 2, DM], F32R)
        k_row = sb(r1, "k_row", [P, 2, HD])
        k_sq = sb(r1, "k_sq", [P, 2, HD])
        q1T_hi = sb(r1, "q1T_hi", [P, GH1, SEQ], F32R)
        q1T_lo = sb(r1, "q1T_lo", [P, GH1, SEQ], F32R)
        q_sq = sb(r1, "q_sq", [P, GH1, SEQ])
        logit = sb(r1, "logit", [P, TB * GH1, CTX])
        prob1 = sb(r1, "prob1", [P, TB * GH1, CTX])
        prob1n = sb(r1, "prob1n", [P, TB * GH1, CTX])
        p1T_hi = sb(r1, "p1T_hi", [P, 2, SEQ], F32R)
        p1T_lo = sb(r1, "p1T_lo", [P, 2, SEQ], F32R)
        q_ss = sb(r1, "q_ss", [P, TB, GH1])
        q_var = sb(r1, "q_var", [P, TB * GH1])
        q_rms = sb(r1, "q_rms", [P, TB * GH1])
        k_ss = sb(r1, "k_ss", [P, 2])
        k_var = sb(r1, "k_var", [P, 2])
        k_rms = sb(r1, "k_rms", [P, 2])
        mx1 = sb(r1, "mx1", [P, TB * GH1])
        sum1 = sb(r1, "sum1", [P, TB * GH1])
        rinv1 = sb(r1, "rinv1", [P, TB * GH1])
        r1.close()

        def bank(name):
            return ctx.enter_context(nc.psum_tensor(name, [P, 512], F32))

        bank_ss = ctx.enter_context(nc.psum_tensor("bank_s", [P, 2, 512], F32))
        bank_s = [bank_ss[:, 0, :], bank_ss[:, 1, :]]
        bank_t = [bank("bank_t0"), bank("bank_t1"), bank("bank_t2")]
        bank_o = bank("bank_o")
        bank_a, bank_b = bank("bank_a"), bank("bank_b")
        t1_bank, w1_bank, o1_bank, kv1_bank = bank_t[0], bank_t[1], bank_t[2], bank_o
        ffn_g, ffn_u = [bank_s[0], bank_s[1]], [bank_o, bank_a]
        ffn_acc = [bank_t[0], bank_t[1], bank_t[2], bank_b]

        s_stage = [sem(f"stage_loaded{i}") for i in range(RING)]
        s_x = [sem(f"x_loaded{i}") for i in range(NT)]
        s_ctx = sem("ctx_loaded")
        s_small = sem("small_loaded")
        s_ad = sem("ad_loaded")
        s_kvst = sem("kv_stage_loaded")
        s_out = sem("out_stored")
        s_ident = sem("ident_ready")
        s_half = sem("neg_half_ready")
        s_tg = sem("tg_ready")
        s_ksc = sem("kscale_ready")
        s_chi, s_clo = sem("ctx_hi"), sem("ctx_lo")
        l_stats, l_mv, l_var, l_rstd = sem("ln_stats_done"), sem("ln_mv_done"), sem("ln_var_done"), sem("ln_rstd_done")
        l_xn, l_tr, l_hi, l_lo = sem("ln_out_done"), sem("ln_transposed"), sem("ln_hi_done"), sem("ln_lo_done")
        a_wq_hi, a_wq_lo = sem("a_wq_hi"), sem("a_wq_lo")
        a_wo_hi, a_wo_lo = sem("a_wo_hi"), sem("a_wo_lo")
        a_wkv_hi, a_wkv_lo = sem("a_wkv_hi"), sem("a_wkv_lo")
        a_q, a_qhi, a_qlo = sem("a_q"), sem("a_q_hi"), sem("a_q_lo")
        a_s, a_max, a_exp = sem("a_scores"), sem("a_max"), sem("a_exp")
        a_rec, a_norm, a_dup = sem("a_recip"), sem("a_norm"), sem("a_dup")
        a_t, a_thi, a_tlo = sem("a_pT"), sem("a_pT_hi"), sem("a_pT_lo")
        a_pv, a_ohi, a_olo = sem("a_pv"), sem("a_o_hi"), sem("a_o_lo")
        a_wo, a_acc = sem("a_wo"), sem("a_acc")
        a_k, a_khi, a_klo = sem("a_k"), sem("a_k_hi"), sem("a_k_lo")
        a_vT, a_vTc = sem("a_vT"), sem("a_vT_copied")
        a_v, a_vhi, a_vlo = sem("a_v"), sem("a_v_hi"), sem("a_v_lo")
        F = [{k: sem(f"f{n}_{k}") for k in ("gu_hi", "gu_lo", "wd_hi", "wd_lo", "gate", "up", "silu", "h",
                                             "h_hi", "h_lo", "down", "acc", "tgad", "scaled", "x")} for n in range(2)]
        b_wq_hi, b_wq_lo = sem("b_wq_hi"), sem("b_wq_lo")
        b_wo_hi, b_wo_lo = sem("b_wo_hi"), sem("b_wo_lo")
        b_wkv_hi, b_wkv_lo = sem("b_wkv_hi"), sem("b_wkv_lo")
        b_q, b_qhi, b_qlo, b_qsq = sem("b_q"), sem("b_q_hi"), sem("b_q_lo"), sem("b_q_squared")
        b_sqT, b_ss, b_var, b_rms = sem("b_q_sq_transposed"), sem("b_q_ss"), sem("b_q_var"), sem("b_q_rms")
        b_s, b_cross, b_add, b_log, b_mask = sem("b_scores"), sem("b_q_k_lo"), sem("b_added"), sem("b_logit"), sem("b_masked")
        b_max, b_sub, b_exp = sem("b_max"), sem("b_sub"), sem("b_exp")
        b_sum, b_rec, b_norm = sem("b_sum"), sem("b_recip"), sem("b_norm")
        b_t, b_thi, b_tlo = sem("b_pT"), sem("b_pT_hi"), sem("b_pT_lo")
        b_w, b_whi, b_wlo = sem("b_vw"), sem("b_vw_hi"), sem("b_vw_lo")
        b_o, b_acc = sem("b_out"), sem("b_acc")
        b_kr, b_krc, b_krs, b_kss, b_kvar, b_krms, b_kn = (sem("b_krow"), sem("b_krow_copied"), sem("b_krow_squared"),
                                                           sem("b_k_ss"), sem("b_k_var"), sem("b_k_rms"), sem("b_k_normed"))
        b_kT, b_khi, b_klo = sem("b_kT"), sem("b_k_hi"), sem("b_k_lo")
        b_v, b_vhi, b_vlo = sem("b_v"), sem("b_v_hi"), sem("b_v_lo")

        stream = []

        def slot(n):
            return stage[:, n % RING, :]

        def slot16(n):
            return stage[:, n % RING, :].bitcast(F16)

        def k_rows(w, a, b):
            return w.rearrange("(c p) n -> p c n", p=P)[:, :, a:b]

        def head_rows(w, a, b):
            return w[a * HD:b * HD, :].rearrange("(h p) n -> p h n", p=P)

        def gu_view(v):
            return v[:, 0:CHUNK].rearrange("p (w c n) -> p w c n", w=2, c=KC)

        def ffn_order(nf):
            yield from (("gu", 0), ("gu", 1), ("wd", 0), ("gu", 2), ("wd", 1))
            for m in range(2 * nf):
                if m + 3 < 2 * nf:
                    yield "gu", m + 3
                if m + 2 < 2 * nf:
                    yield "wd", m + 2

        def add_ffn(n, wg, wu, wd):
            nf, at = NFS[n], {}
            part = "lo" if n == 0 else "hi"
            for what, m in ffn_order(nf):
                f, k = m % nf, len(stream)
                v = slot(k) if n == 0 else slot16(k)
                at[what, m] = k
                if what == "gu":
                    v = gu_view(v)
                    dmas = [(v[:, 0], k_rows(wg, f * P, (f + 1) * P)), (v[:, 1], k_rows(wu, f * P, (f + 1) * P))]
                else:
                    dmas = [(v[:, 0:DM], wd[f * P:(f + 1) * P, :])]
                stream.append((dmas, F[n][f"{what}_{part}"], m + 1))
            return at

        NFS = (NF0, NF1)
        for pair in range(HEADS // 2):
            v = slot(len(stream)).rearrange("p (c n) -> p c n", c=KC)
            stream.append(([(v, k_rows(wq0, pair * 2 * HD, (pair + 1) * 2 * HD))], a_wq_lo, pair + 1))
            v = slot(len(stream)).rearrange("p (h n) -> p h n", h=2)
            stream.append(([(v, head_rows(wo0, 2 * pair, 2 * pair + 2))], a_wo_lo, pair + 1))
        ffn_at = [add_ffn(0, wg0T, wu0T, wd0T)]
        l1_base = len(stream)
        L1_CHUNKS = (("wq", 0), ("wq", 1), ("wo", 0), ("wo", 1)), (("wo", 0), ("wq", 0), ("wq", 1), ("wo", 1))
        for j in range(KV1):
            for what, part in L1_CHUNKS[min(j, 1)]:
                h = j * GH1 + 2 * part
                if what == "wq":
                    v = slot(len(stream)).rearrange("p (c n) -> p c n", c=KC)
                    stream.append(([(v, k_rows(wq1T, h * HD, (h + 2) * HD))], b_wq_lo, 2 * j + part + 1))
                else:
                    v = slot(len(stream)).rearrange("p (h n) -> p h n", h=2)
                    stream.append(([(v, head_rows(wo1T, h, h + 2))], b_wo_lo, 2 * j + part + 1))
        ffn_at.append(add_ffn(1, wg1T, wu1T, wd1T))
        landed, slot_sum = [], [0] * RING
        for n, (dmas, _, _) in enumerate(stream):
            slot_sum[n % RING] += 16 * len(dmas)
            landed.append(slot_sum[n % RING])

        def chunk_wait(eng, k, per=0, it=0):
            eng.wait_ge(s_stage[k % RING], landed[k] + (it * (landed[k + per] - landed[k]) if per else 0))

        block = ctx.enter_context(nc.Block())

        def load_kv(sp, n, wk, wv, head):
            if 1 <= n <= KV0:
                sp.wait_ge(a_wkv_lo, n)
            elif n > KV0:
                sp.wait_ge(b_wkv_lo, n - KV0)
            for w, src in enumerate((wk, wv)):
                sp.dma_start(kv_stage[:, w, :, :], k_rows(src, head * HD, (head + 1) * HD)).then_inc(s_kvst, 16)

        @block.sync
        def _(sp):
            x_rows = x.rearrange("(t p) d -> t p d", p=P)
            for t in range(NT):
                sp.dma_start(x_sb[:, t, :], x_rows[t]).then_inc(s_x[t], 16)
            load_kv(sp, 0, wk0, wv0, 0)
            sp.dma_start(prob[:, :, 0:BATCH * CTX], ctxT.rearrange("(c p) n -> p c n", p=P)).then_inc(s_ctx, 16)
            for n in range(RING):
                for dst, src in stream[n][0]:
                    sp.dma_start(dst, src).then_inc(s_stage[n % RING], 16)
            for dst, src in ((gates[:, 0:2], g_xattn.rearrange("(a n) -> a n", a=1).broadcast_to([P, 2])),
                             (gates[:, 2:4], g_ffn.rearrange("(a n) -> a n", a=1).broadcast_to([P, 2])),
                             (mask_sb[:, :, :], mask.rearrange("(c p) n -> p c n", p=P)),
                             (qn_w[:, :], qnorm), (kn_w[:, :], knorm), (ag_sb[:, :], ag), (au_sb[:, :], au)):
                sp.dma_start(dst, src).then_inc(s_small, 16)
            kv_n = 1
            for n in range(RING, len(stream)):
                if n < l1_base and n % (2 * PAIRS0) == 4 and kv_n < KV0:
                    load_kv(sp, kv_n, wk0, wv0, kv_n)
                    kv_n += 1
                if n in [l1_base - RING] + [l1_base + 4 * j for j in range(1, KV1)]:
                    load_kv(sp, kv_n, wk1T, wv1T, kv_n - KV0)
                    kv_n += 1
                sp.wait_ge(stream[n - RING][1], stream[n - RING][2])
                for dst, src in stream[n][0]:
                    sp.dma_start(dst, src).then_inc(s_stage[n % RING], 16)
                if n == ffn_at[0]["gu", 2]:
                    sp.wait_ge(a_acc, 2 * KV0 * UNITS0 + 2)
                    sp.dma_start(ffn_t[0]["ad"][:, :],
                                 ad.rearrange("(a n) -> a n", a=1).broadcast_to([P, DM])).then_inc(s_ad, 16)
            o_rows = out.rearrange("(t p) d -> t p d", p=P)
            for t in range(NT):
                sp.wait_ge(F[1]["x"], t + 1)
                sp.dma_start(o_rows[t], x_sb[:, t, :]).then_inc(s_out, 16)
            sp.wait_ge(s_out, 16 * NT)

        def ln_vector(ve, k, x_ready):
            n0 = NT * k
            for t in range(NT):
                x_ready(t)
                ve.bn_stats(ln_stats[:, t, :], x_sb[:, t, :]).then_inc(l_stats, 1)
                if t >= 1:
                    ve.wait_ge(l_stats, n0 + t)
                    ve.bn_aggr(ln_mv[:, t - 1, :], ln_stats[:, t - 1, :]).then_inc(l_mv, 1)
                if t == NT // 2 + 1:
                    ln_eps(ve, k, 0)
            ve.wait_ge(l_stats, n0 + NT)
            ve.bn_aggr(ln_mv[:, NT - 1, :], ln_stats[:, NT - 1, :]).then_inc(l_mv, 1)
            ln_eps(ve, k, 1)
            for t in range(NT + 1):
                if t < NT:
                    if t % (NT // 2) == 0:
                        ve.wait_ge(l_rstd, 2 * k + t // (NT // 2) + 1)
                    if t >= 2:
                        ve.wait_ge(l_tr, n0 + t - 1)
                    ve.tensor_scalar(ln_out[:, t % 2, :], x_sb[:, t, :], ln_mv[:, t, 0:1], ln_rstd[:, t:t + 1],
                                     ALU.subtract, ALU.mult).then_inc(l_xn, 1)
                if t >= 1:
                    ve.wait_ge(l_hi, n0 + t)
                    ve.tensor_tensor(xT_lo[:, :, (t - 1) * P:t * P],
                                     bank_t[(t - 1) % 2][:, :].rearrange("p (c n) -> p c n", c=KC),
                                     f32(xT_hi[:, :, (t - 1) * P:t * P]), ALU.subtract).then_inc(l_lo, 1)

        def ln_eps(ve, k, half):
            a, b = half * NT // 2, (half + 1) * NT // 2
            ve.wait_ge(l_mv, NT * k + b)
            ve.tensor_scalar(ln_var[:, a:b], ln_mv[:, a:b, 1], EPS, None, ALU.add).then_inc(l_var, 1)

        def ln_gpsimd(po, k):
            for half in range(2):
                a, b = half * NT // 2, (half + 1) * NT // 2
                po.wait_ge(l_var, 2 * k + half + 1)
                po.tensor_tensor(ln_rstd[:, a:b], ln_var[:, a:b], neg_half[:, a:b], ALU.pow).then_inc(l_rstd, 1)

        def ln_tensor(pe, k):
            for t in range(NT):
                pe.wait_ge(l_xn, NT * k + t + 1)
                if t >= 2:
                    pe.wait_ge(l_lo, NT * k + t - 1)
                for c in range(KC):
                    mm = pe.transpose(bank_t[t % 2][:, c * P:(c + 1) * P], ln_out[:, t % 2, c * P:(c + 1) * P],
                                      ident[:, :])
                mm.then_inc(l_tr, 1)

        def ln_scalar(ac, k):
            for t in range(NT):
                ac.wait_ge(l_tr, NT * k + t + 1)
                ac.activation(xT_hi[:, :, t * P:(t + 1) * P],
                              bank_t[t % 2][:, :].rearrange("p (c n) -> p c n", c=KC), ACT.Copy).then_inc(l_hi, 1)

        def project(pe, out_ap, lhs, rhs, chunks=range(KC), first=True, last=True):
            (l_h, l_l), (r_h, r_l) = lhs, rhs
            for c in chunks:
                passes = [(l_h, r_h), (l_h, r_l)] + ([(l_l, r_h)] if l_l else [])
                for n, (a, b) in enumerate(passes):
                    mm = pe.matmul(out_ap, a(c), b(c), start=first and c == chunks[0] and n == 0,
                                   stop=last and c == chunks[-1] and n == len(passes) - 1)
            return mm

        def per_g(n, g):
            return g * n

        def pe_q(pe, g, blk, part):
            par, slot_, hh, half = (blk // 4) % 2, blk % 4, blk % 2, blk % 4 // 2
            if part == 0:
                if slot_ == 0:
                    pe.wait_ge(a_wq_lo, per_g(PAIRS0, g) + blk // 4 + 1)
                pe.wait_ge(a_qlo, per_g(UNITS0, g) + blk)
            mm = project(pe, bank_a[:, :],
                         (lambda c: wq_hi[:, par, c, hh * HD:(hh + 1) * HD], lambda c: wq_lo[:, par, c, hh * HD:(hh + 1) * HD]),
                         (lambda c: xT_hi[:, c, half * 512:(half + 1) * 512], lambda c: xT_lo[:, c, half * 512:(half + 1) * 512]),
                         chunks=(0, 1) if part == 0 else (2, 3), first=part == 0, last=part == 1)
            if part == 1:
                mm.then_inc(a_q, 1)

        def pe_scores(pe, g, i, j):
            b, hh, c = i % 4, j // 2, j % 2
            s = (b // 2) * 2 + hh
            if c == 0:
                pe.wait_ge(a_qlo, per_g(UNITS0, g) + (i // 4) * 4 + s + 1)
            if i % UNITS0 == 0 and j == 0:
                pe.wait_ge(a_klo, per_g(3, g) + 3 * (i // UNITS0) + 3)
            pe.wait_ge(a_exp, per_g(4 * UNITS0, g) + 4 * i + j + 1)
            q0 = (b % 2) * SEQ + c * P
            for n, (q, kk) in enumerate(((qT_hi, k_hi), (qT_hi, k_lo), (qT_lo, k_hi))):
                mm = pe.matmul(bank_s[j % 2][:, 0:KVL0], q[:, s, q0:q0 + P], kk[:, b, :], start=n == 0, stop=n == 2)
            mm.then_inc(a_s, 1)

        def pe_pT(pe, g, i):
            for c in range(NCH0):
                if c == 0:
                    pe.wait_ge(a_norm, per_g(4 * UNITS0, g) + 4 * i + 4)
                if c == 2:
                    pe.wait_ge(a_dup, per_g(UNITS0, g) + i + 1)
                    pe.wait_ge(a_acc, per_g(2 * UNITS0, g) + 2 * i + 2)
                for j in range(4):
                    mm = pe.transpose(bank_t[c][:, j * P:(j + 1) * P], probn[:, j, c * P:(c + 1) * P], ident[:, :])
                mm.then_inc(a_t, 1)

        def pe_pv(pe, g, i):
            b = i % 4
            pe.wait_ge(a_olo, per_g(UNITS0, g) + i + 1)
            if i == 0:
                pe.wait_ge(a_vlo, per_g(3, g) + 3)
            mms = []
            for c in range(2):
                v = TB * b + c
                mms += [(v_hi[:, v], pT_hi[:, c], c), (v_hi[:, v], pT_lo[:, c], c), (v_lo[:, v], pT_hi[:, c], c)]
            mms += [(v_hi[:, NT + b], pT_hi[:, 2], 2), (v_lo[:, NT + b], pT_hi[:, 2], 2)]
            for n, (v, p, c) in enumerate(mms):
                if n == 0 or mms[n - 1][2] != c:
                    pe.wait_ge(a_tlo, per_g(3 * UNITS0, g) + 3 * i + c + 1)
                mm = pe.matmul(bank_o[:, :], v, p, start=n == 0, stop=n == len(mms) - 1)
            mm.then_inc(a_pv, 1)

        def pe_wo(pe, g, i, c, last):
            par = (i // 4) % 2
            if c == 0:
                if i % 4 == 0:
                    pe.wait_ge(a_wo_lo, per_g(PAIRS0, g) + i // 4 + 1)
                pe.wait_ge(a_olo, per_g(UNITS0, g) + i + 2)
                pe.wait_ge(a_acc, per_g(2 * UNITS0, g) + 2 * i + 2)
                if i in (11, 12, 13) and not last:
                    pe.wait_ge(a_vTc, per_g(3, g) + 3 + i - 10)
            dst = bank_b if c == 0 else bank_t[2]
            for hh in range(2):
                q0 = hh * SEQ + c * P
                for n, (o, w) in enumerate(((oT_hi, wo_hi), (oT_hi, wo_lo), (oT_lo, wo_hi))):
                    mm = pe.matmul(dst[:, :], o[:, q0:q0 + P], w[:, par, hh, :], start=hh == 0 and n == 0,
                                   stop=hh == 1 and n == 2)
            mm.then_inc(a_wo, 1)

        def kv_rhs(n):
            if n < 2:
                return (lambda c: xT_hi[:, c, n * 512:(n + 1) * 512], lambda c: xT_lo[:, c, n * 512:(n + 1) * 512])
            return (lambda c: cT_hi[:, c, :], lambda c: cT_lo[:, c, :])

        KV_ORDER = (2, 0, 1)
        k_bank = (bank_b, bank_o, bank_a)
        v_bank = (bank_b, bank_a, bank_o)

        def pe_k(pe, n):
            project(pe, k_bank[n][:, :] if n < 2 else k_bank[n][:, 0:BATCH * CTX],
                    (lambda c: wkv_hi[:, 0, c, :], lambda c: wkv_lo[:, 0, c, :]), kv_rhs(n)).then_inc(a_k, 1)

        def pe_vT(pe, bank, n):
            project(pe, bank[:, :] if n < 2 else bank[:, 0:BATCH * CTX],
                    (lambda c: wkv_hi[:, 1, c, :], lambda c: wkv_lo[:, 1, c, :]), kv_rhs(n)).then_inc(a_vT, 1)

        def pe_v(pe, n):
            for q in range(4):
                mm = pe.transpose(v_bank[n][:, q * P:(q + 1) * P], vT[:, 4 * n + q, :], ident[:, :])
            mm.then_inc(a_v, 1)

        def pe_unit0(pe, g, i, last):
            ahead = not (last and i + 2 >= UNITS0)
            blk = not (last and i + QLEAD >= UNITS0)
            pe_pT(pe, g, i)
            if blk:
                if i == 14 and not last:
                    pe.wait_ge(a_klo, per_g(3, g) + 4)
                if i == 0:
                    pe.wait_ge(a_vlo, per_g(3, g) + 3)
                pe_q(pe, g, i + QLEAD, 0)
            if i == 14 and not last:
                pe.wait_ge(a_klo, per_g(3, g) + 6)
            pe_pv(pe, g, i)
            if blk:
                pe_q(pe, g, i + QLEAD, 1)
            if ahead:
                pe_scores(pe, g, i + 2, 0)
                pe_scores(pe, g, i + 2, 1)
            pe_wo(pe, g, i, 0, last)
            if ahead:
                pe_scores(pe, g, i + 2, 2)
                pe_scores(pe, g, i + 2, 3)
            pe_wo(pe, g, i, 1, last)
            if not last:
                if i in (10, 11, 12):
                    if i == 10:
                        pe.wait_ge(a_wkv_lo, g + 2)
                    pe.wait_ge(a_acc, per_g(2 * UNITS0, g) + 2 * i + 3)
                    pe_vT(pe, bank_b, i - 10)
                if i == 13:
                    pe.wait_ge(a_qlo, per_g(UNITS0, g) + i + QLEAD + 1)
                    pe_k(pe, 2)
                    pe.wait_ge(a_acc, per_g(2 * UNITS0, g) + 2 * i + 3)
                    pe_k(pe, 0)
                    pe_k(pe, 1)
                if i == 15:
                    pe_v(pe, 2)
                    pe.wait_ge(a_acc, per_g(2 * UNITS0, g) + 2 * i + 3)
                    pe_v(pe, 0)
                    pe.wait_ge(a_qlo, per_g(UNITS0, g) + i + QLEAD + 1)
                    pe_v(pe, 1)

        def pe_attn0(pe):
            pe.wait_ge(a_wkv_lo, 1)
            pe.wait_ge(s_clo, 1)
            for n in KV_ORDER:
                if n < 2:
                    pe.wait_ge(l_lo, NT * (n + 1) // 2)
                pe_k(pe, n)
            for step, n in enumerate(KV_ORDER):
                pe.wait_ge(a_klo, step + 1)
                pe_vT(pe, k_bank[n], n)
            for blk in range(QLEAD):
                pe.wait_ge(a_vTc, 3)
                pe_q(pe, 0, blk, 0)
                pe_q(pe, 0, blk, 1)
            pe_v(pe, 2)
            pe_v(pe, 0)
            for u in range(2):
                for j in range(4):
                    pe_scores(pe, 0, u, j)
            pe_v(pe, 1)
            with pe.Fori(0, KV0 - 1) as g:
                for i in range(UNITS0):
                    pe_unit0(pe, g, i, False)
            for i in range(UNITS0):
                pe_unit0(pe, KV0 - 1, i, True)

        def split_hi(ac, dst, src, done):
            ac.activation(dst, src, ACT.Copy).then_inc(done, 1)

        def ac_wq(ac, g, pair):
            n = 2 * pair
            chunk_wait(ac, n, 2 * PAIRS0, g)
            if pair >= 2:
                ac.wait_ge(a_q, per_g(UNITS0, g) + 4 * (pair - 1))
            split_hi(ac, wq_hi[:, pair % 2], stage[:, n % RING, :].rearrange("p (c n) -> p c n", c=KC), a_wq_hi)

        def ac_wo(ac, g, pair):
            n = 2 * pair + 1
            chunk_wait(ac, n, 2 * PAIRS0, g)
            if pair >= 1:
                ac.wait_ge(a_wo, per_g(2 * UNITS0, g) + 8 * (pair - 1) + 1)
            split_hi(ac, wo_hi[:, pair % 2], stage[:, n % RING, :].rearrange("p (h n) -> p h n", h=2), a_wo_hi)

        def ac_exp(ac, g, i, j):
            ac.wait_ge(a_max, per_g(4 * UNITS0, g) + 4 * i + j + 1)
            ac.wait_ge(a_norm, per_g(4 * UNITS0, g) + 4 * i)
            ac.wait_ge(a_dup, per_g(UNITS0, g) + i)
            ac.activation(prob[:, j, :], bank_s[j % 2][:, 0:KVL0], ACT.Exp, bias=nmax[:, j:j + 1],
                          accum_out=rsum[:, j:j + 1]).then_inc(a_exp, 1)

        def ac_q(ac, g, blk):
            ac.wait_ge(a_q, per_g(UNITS0, g) + blk + 1)
            ac.activation(qT_hi[:, blk % 4, :], bank_a[:, :], ACT.Copy, scale=SCALE).then_inc(a_qhi, 1)

        def k_dst(t, n):
            if n < 2:
                return t[:, 2 * n:2 * n + 2, 0:SEQ]
            return t[:, :, SEQ:KVL0]

        def k_src(n):
            if n < 2:
                return k_bank[n][:, :].rearrange("p (b n) -> p b n", b=2)
            return k_bank[n][:, 0:BATCH * CTX].rearrange("p (b n) -> p b n", b=BATCH)

        def ac_k(ac, g, step):
            n = KV_ORDER[step]
            ac.wait_ge(a_k, per_g(3, g) + step + 1)
            ac.activation(k_dst(k_hi, n), k_src(n), ACT.Copy).then_inc(a_khi, 1)

        def ac_vT(ac, g, step, bank, n):
            ac.wait_ge(a_vT, per_g(3, g) + step + 1)
            if n < 2:
                ac.activation(vT[:, 4 * n:4 * n + 4, :], bank[:, :].rearrange("p (t n) -> p t n", t=4),
                              ACT.Copy).then_inc(a_vTc, 1)
            else:
                src = bank[:, 0:BATCH * CTX].rearrange("p (b r n) -> p b r n", b=BATCH, r=1)
                ac.activation(vT[:, NT:NT + BATCH, :].rearrange("p b (r n) -> p b r n", r=2),
                              src.broadcast_to([P, BATCH, 2, CTX]), ACT.Copy).then_inc(a_vTc, 1)

        def v_src(n):
            return v_bank[n][:, :].rearrange("p (t n) -> p t n", t=4)

        def ac_v(ac, g, step):
            n = KV_ORDER[step]
            ac.wait_ge(a_v, per_g(3, g) + step + 1)
            ac.activation(v_hi[:, 4 * n:4 * n + 4, :], v_src(n), ACT.Copy).then_inc(a_vhi, 1)

        def ac_wkv(ac, k, dst, done):
            ac.wait_ge(s_kvst, 32 * k + 32)
            split_hi(ac, dst[:, :, :, :], kv_stage[:, :, :, :], done)

        def ac_unit0(ac, g, i, last):
            ahead = not (last and i + 2 >= UNITS0)
            blk = not (last and i + QLEAD >= UNITS0)
            p = i // 4
            for c in range(NCH0):
                ac.wait_ge(a_t, per_g(3 * UNITS0, g) + 3 * i + c + 1)
                ac.activation(pT_hi[:, c, :], bank_t[c][:, :], ACT.Copy).then_inc(a_thi, 1)
                if c == 2 and i % 4 == 1 and not (last and p + 1 >= PAIRS0):
                    ac_wo(ac, g, p + 1)
                if c == 2 and i % 4 == 2 and not (last and p + 2 >= PAIRS0):
                    ac_wq(ac, g, p + 2)
                if c == 2 and i == 4 and not last:
                    ac.wait_ge(a_k, per_g(3, g) + 3)
                    ac.wait_ge(a_vT, per_g(3, g) + 3)
                    ac_wkv(ac, g + 1, wkv_hi, a_wkv_hi)
            ac.wait_ge(a_pv, per_g(UNITS0, g) + i + 1)
            ac.activation(oT_hi[:, :], bank_o[:, :], ACT.Copy).then_inc(a_ohi, 1)
            if blk:
                ac_q(ac, g, i + QLEAD)
            if ahead:
                for j in range(4):
                    ac_exp(ac, g, i + 2, j)
            if not last:
                if i in (10, 11, 12):
                    ac_vT(ac, g + 1, i - 10, bank_b, i - 10)
                if i == 13:
                    for step in range(3):
                        ac_k(ac, g + 1, step)
                if i == 15:
                    for step in range(3):
                        ac_v(ac, g + 1, step)

        def ac_attn0(ac):
            for step in range(3):
                ac_k(ac, 0, step)
            for step, n in enumerate(KV_ORDER):
                ac_vT(ac, 0, step, k_bank[n], n)
            for blk in range(QLEAD):
                ac_q(ac, 0, blk)
            ac_v(ac, 0, 0)
            ac_v(ac, 0, 1)
            for u in range(2):
                for j in range(4):
                    ac_exp(ac, 0, u, j)
            ac_v(ac, 0, 2)
            with ac.Fori(0, KV0 - 1) as g:
                for i in range(UNITS0):
                    ac_unit0(ac, g, i, False)
            for i in range(UNITS0):
                ac_unit0(ac, KV0 - 1, i, True)

        def ve_max(ve, g, i, j):
            ve.wait_ge(a_s, per_g(4 * UNITS0, g) + 4 * i + j + 1)
            ve.tensor_reduce(nmax[:, j:j + 1], bank_s[j % 2][:, 0:KVL0], AX_X, ALU.max, negate=True).then_inc(a_max, 1)

        def ve_norm(ve, g, i, first=False):
            ve.wait_ge(a_exp, per_g(4 * UNITS0, g) + 4 * i + 4 + 2)
            ve.wait_ge(a_dup, per_g(UNITS0, g) + i)
            ve.reciprocal(rinv[:, :], rsum[:, :]).then_inc(a_rec, 1)
            ve.wait_ge(a_rec, per_g(UNITS0, g) + i + 1)
            if not first:
                ve.wait_ge(a_t, per_g(3 * UNITS0, g) + 3 * i - 1)
            for j in range(4):
                ve.tensor_scalar(probn[:, j, 0:SEQ], prob[:, j, 0:SEQ], rinv[:, j:j + 1], None,
                                 ALU.mult).then_inc(a_norm, 1)

        def ve_q(ve, g, blk):
            ve.wait_ge(a_qhi, per_g(UNITS0, g) + blk + 1)
            ve.scalar_tensor_tensor(out=qT_lo[:, blk % 4, :], in0=bank_a[:, :], scalar=SCALE,
                                    in1=f32(qT_hi[:, blk % 4, :]), op0=ALU.mult, op1=ALU.subtract).then_inc(a_qlo, 1)

        def ve_k(ve, g, step):
            n = KV_ORDER[step]
            ve.wait_ge(a_khi, per_g(3, g) + step + 1)
            ve.tensor_tensor(k_dst(k_lo, n), k_src(n), f32(k_dst(k_hi, n)), ALU.subtract).then_inc(a_klo, 1)

        def ve_v(ve, g, step):
            n = KV_ORDER[step]
            ve.wait_ge(a_vhi, per_g(3, g) + step + 1)
            ve.tensor_tensor(v_lo[:, 4 * n:4 * n + 4, :], v_src(n), f32(v_hi[:, 4 * n:4 * n + 4, :]),
                             ALU.subtract).then_inc(a_vlo, 1)

        def ve_add0(ve, g, i, c):
            t = TB * (i % 4) + c
            ve.wait_ge(a_wo, per_g(2 * UNITS0, g) + 2 * i + c + 1)
            ve.scalar_tensor_tensor(out=x_sb[:, t, :], in0=(bank_b, bank_t[2])[c][:, :], scalar=tg[:, 0:1],
                                    in1=x_sb[:, t, :], op0=ALU.mult, op1=ALU.add).then_inc(a_acc, 1)

        def ve_pT(ve, g, i, c):
            ve.wait_ge(a_thi, per_g(3 * UNITS0, g) + 3 * i + c + 1)
            if c < 2:
                ve.tensor_tensor(pT_lo[:, c, :], bank_t[c][:, :], f32(pT_hi[:, c, :]), ALU.subtract).then_inc(a_tlo, 1)
            else:
                ve.tensor_tensor(pT_hi[CTX:P, c, :], bank_t[c][CTX:P, :], f32(pT_hi[CTX:P, c, :]),
                                 ALU.subtract).then_inc(a_tlo, 1)

        def ve_unit0(ve, g, i, last):
            ahead = not (last and i + 2 >= UNITS0)
            blk = not (last and i + QLEAD >= UNITS0)
            ve_pT(ve, g, i, 0)
            ve_pT(ve, g, i, 1)
            ve_pT(ve, g, i, 2)
            if not (last and i == UNITS0 - 1):
                ve_norm(ve, g, i + 1)
            ve.wait_ge(a_ohi, per_g(UNITS0, g) + i + 1)
            ve.tensor_tensor(oT_lo[:, :], bank_o[:, :], f32(oT_hi[:, :]), ALU.subtract).then_inc(a_olo, 1)
            if ahead:
                ve_max(ve, g, i + 2, 0)
                ve_max(ve, g, i + 2, 1)
            if blk:
                ve_q(ve, g, i + QLEAD)
            ve_add0(ve, g, i, 0)
            if ahead:
                ve_max(ve, g, i + 2, 2)
                ve_max(ve, g, i + 2, 3)
            ve_add0(ve, g, i, 1)
            if not last:
                if i == 13:
                    for step in range(3):
                        ve_k(ve, g + 1, step)
                if i == 15:
                    for step in range(3):
                        ve_v(ve, g + 1, step)

        def ve_attn0(ve):
            for step in range(3):
                ve_k(ve, 0, step)
            for blk in range(QLEAD):
                ve_q(ve, 0, blk)
            ve_v(ve, 0, 0)
            ve_v(ve, 0, 1)
            for u in range(2):
                for j in range(4):
                    ve_max(ve, 0, u, j)
                if u == 0:
                    ve_norm(ve, 0, 0, first=True)
            ve_v(ve, 0, 2)
            with ve.Fori(0, KV0 - 1) as g:
                for i in range(UNITS0):
                    ve_unit0(ve, g, i, False)
            for i in range(UNITS0):
                ve_unit0(ve, KV0 - 1, i, True)

        def split_lo(po, dst, src, hi, done):
            po.tensor_tensor(dst, src, f32(hi), ALU.subtract).then_inc(done, 1)

        def po_wq(po, g, pair):
            po.wait_ge(a_wq_hi, per_g(PAIRS0, g) + pair + 1)
            split_lo(po, wq_lo[:, pair % 2], stage[:, 2 * pair % RING, :].rearrange("p (c n) -> p c n", c=KC),
                     wq_hi[:, pair % 2], a_wq_lo)

        def po_wo(po, g, pair):
            po.wait_ge(a_wo_hi, per_g(PAIRS0, g) + pair + 1)
            split_lo(po, wo_lo[:, pair % 2], stage[:, (2 * pair + 1) % RING, :].rearrange("p (h n) -> p h n", h=2),
                     wo_hi[:, pair % 2], a_wo_lo)

        def po_wkv(po, hi, lo, hi_done, lo_done, n):
            po.wait_ge(hi_done, n)
            split_lo(po, lo[:, :, :, :], kv_stage[:, :, :, :], hi[:, :, :, :], lo_done)

        def po_dup(po, g, i):
            po.wait_ge(a_t, per_g(3 * UNITS0, g) + 3 * i)
            po.wait_ge(a_rec, per_g(UNITS0, g) + i + 1)
            src = prob[:, :, SEQ:KVL0].rearrange("p j (r n) -> p j r n", r=1).broadcast_to([P, 4, 2, CTX])
            r = rinv[:, :].rearrange("p (j r n) -> p j r n", r=1, n=1).broadcast_to([P, 4, 2, CTX])
            po.tensor_tensor(probn[:, :, SEQ:NCH0 * P].rearrange("p j (r n) -> p j r n", r=2), src, r,
                             ALU.mult).then_inc(a_dup, 1)

        def po_unit0(po, g, i, last):
            if not (last and i == UNITS0 - 1):
                po_dup(po, g, i + 1)
            p = i // 4
            if i % 4 == 1 and not (last and p + 1 >= PAIRS0):
                po_wo(po, g, p + 1)
            if i % 4 == 2 and not (last and p + 2 >= PAIRS0):
                po_wq(po, g, p + 2)
            if not last and i == 4:
                po_wkv(po, wkv_hi, wkv_lo, a_wkv_hi, a_wkv_lo, g + 2)

        def po_attn0(po):
            po_dup(po, 0, 0)
            with po.Fori(0, KV0 - 1) as g:
                for i in range(UNITS0):
                    po_unit0(po, g, i, False)
            for i in range(UNITS0):
                po_unit0(po, KV0 - 1, i, True)

        def steps(eng, nf, step):
            for half in range(2):
                first, end = half * nf, (half + 1) * nf
                step(first, first, 0, 0)
                rounds = (min(end - 2, 2 * nf - 4) - first) // 2
                with eng.Fori(0, rounds) as it:
                    for s in range(1, 3):
                        step(it * 2 + (first + s), first + s, it, RING)
                for m in range(first + 2 * rounds + 1, end):
                    step(m, m, 0, 0)

        def pe_gu(pe, n, m, ms):
            t, s = ffn_t[n], F[n]
            par, half = ms % 2, ms // NFS[n]
            pe.wait_ge(s["gu_lo" if n == 0 else "gu_hi"], m + 1)
            pe.wait_ge(s["h"], m + 1)
            for w, banks, done in ((0, ffn_g, s["gate"]), (1, ffn_u, s["up"])):
                def part(name):
                    return (lambda c: t[name][:, par, w, c, :]) if name in t else None
                project(pe, banks[par][:, :], (part("gu_hi"), part("gu_lo")),
                        (lambda c: xT_hi[:, c, half * 512:(half + 1) * 512],
                         lambda c: xT_lo[:, c, half * 512:(half + 1) * 512])).then_inc(done, 1)

        def pe_down(pe, n, m, ms):
            nf, t, s = NFS[n], ffn_t[n], F[n]
            par, f, half = ms % 2, ms % nf, ms // nf
            pe.wait_ge(s["h_lo"], m + 1)
            pe.wait_ge(s["wd_lo" if n == 0 else "wd_hi"], m + 1)
            passes = [("h_hi", "wd_hi"), ("h_lo", "wd_hi")] + ([("h_hi", "wd_lo")] if n == 0 else [])
            for q in range(4):
                if f == 0 and half == 1:
                    pe.wait_ge(s["x"], q + 1)
                for k, (h, w) in enumerate(passes):
                    mm = pe.matmul(ffn_acc[q][:, :], t[h][:, par, q * P:(q + 1) * P], t[w][:, par, :],
                                   start=f == 0 and k == 0, stop=f == nf - 1 and k == len(passes) - 1)
                if f == nf - 1:
                    mm.then_inc(s["acc"], 1)
            if f != nf - 1:
                mm.then_inc(s["down"], 1)

        def pe_ffn(pe, n, k):
            pe.wait_ge(l_lo, NT * k + NT // 2)
            pe_gu(pe, n, 0, 0)
            pe.wait_ge(l_lo, NT * k + NT)

            def step(m, ms, it, per):
                if ms + 1 < 2 * NFS[n]:
                    pe_gu(pe, n, m + 1, ms + 1)
                pe_down(pe, n, m, ms)
            steps(pe, NFS[n], step)

        def ac_gu(ac, n, m, ms, it, per):
            t, s = ffn_t[n], F[n]
            k = ffn_at[n]["gu", ms]
            chunk_wait(ac, k, per, it)
            if ms >= 2:
                ac.wait_ge(s["up"], m - 1)
            ac.activation(t["gu_hi"][:, ms % 2], gu_view(slot(k) if n == 0 else slot16(k)),
                          ACT.Copy).then_inc(s["gu_hi"], 1)

        def ac_wd(ac, n, m, ms, it, per):
            nf, t, s = NFS[n], ffn_t[n], F[n]
            k = ffn_at[n]["wd", ms]
            chunk_wait(ac, k, per, it)
            if ms >= 2:
                half, f = divmod(ms - 2, nf)
                if f == nf - 1:
                    ac.wait_ge(s["acc"], 4 * (half + 1))
                else:
                    ac.wait_ge(s["down"], m - 1 - half)
            ac.activation(t["wd_hi"][:, ms % 2, :], (slot(k) if n == 0 else slot16(k))[:, 0:DM],
                          ACT.Copy).then_inc(s["wd_hi"], 1)

        def ac_silu(ac, n, m, ms):
            t, s = ffn_t[n], F[n]
            half = ms // NFS[n]
            ac.wait_ge(s["gate"], m + 1)
            scale = ag_sb[:, bass.ds(m - half * NFS[n], 1)] if n == 0 else 1.0
            ac.activation(t["s"][:, ms % 2, :], ffn_g[ms % 2][:, :], ACT.Silu, scale=scale).then_inc(s["silu"], 1)
            ac.wait_ge(s["h"], m + 3)
            ac.activation(t["h_hi"][:, ms % 2, :], t["h"][:, ms % 2, :], ACT.Copy).then_inc(s["h_hi"], 1)

        def ac_ffn(ac, n, k, before):
            total = 2 * NFS[n]
            ac.sem_inc(F[n]["h"], 2)
            before()
            ac_gu(ac, n, 0, 0, 0, 0)
            ln_scalar(ac, k)
            ac_gu(ac, n, 1, 1, 0, 0)
            ac_wd(ac, n, 0, 0, 0, 0)
            ac_silu(ac, n, 0, 0)
            ac_gu(ac, n, 2, 2, 0, 0)
            ac_wd(ac, n, 1, 1, 0, 0)

            def step(m, ms, it, per):
                if ms + 1 < total:
                    ac_silu(ac, n, m + 1, ms + 1)
                if ms + 3 < total:
                    ac_gu(ac, n, m + 3, ms + 3, it, per)
                if ms + 2 < total:
                    ac_wd(ac, n, m + 2, ms + 2, it, per)
            steps(ac, NFS[n], step)

        def ve_h(ve, n, m, ms):
            t, s = ffn_t[n], F[n]
            half, par = ms // NFS[n], ms % 2
            ve.wait_ge(s["up"], m + 1)
            ve.wait_ge(s["silu"], m + 1)
            if n == 0:
                ve.scalar_tensor_tensor(out=t["h"][:, par, :], in0=ffn_u[par][:, :],
                                        scalar=au_sb[:, bass.ds(m - half * NFS[n], 1)], in1=t["s"][:, par, :],
                                        op0=ALU.mult, op1=ALU.mult).then_inc(s["h"], 1)
            else:
                ve.tensor_tensor(t["h"][:, par, :], ffn_u[par][:, :], t["s"][:, par, :], ALU.mult).then_inc(s["h"], 1)
            ve.wait_ge(s["h_hi"], m + 1)
            ve.tensor_tensor(t["h_lo"][:, par, :], t["h"][:, par, :], f32(t["h_hi"][:, par, :]),
                             ALU.subtract).then_inc(s["h_lo"], 1)

        def ve_ffn_x(ve, n, half):
            t, s = ffn_t[n], F[n]
            for q in range(4):
                tile = 4 * half + q
                ve.wait_ge(s["acc"], tile + 1)
                if n == 0:
                    if tile >= 2:
                        ve.wait_ge(s["x"], tile - 1)
                    ve.tensor_tensor(t["scaled"][:, q % 2, :], ffn_acc[q][:, :], t["tgad"][:, :],
                                     ALU.mult).then_inc(s["scaled"], 1)
                    ve.wait_ge(s["scaled"], tile + 1)
                    ve.tensor_tensor(x_sb[:, tile, :], x_sb[:, tile, :], t["scaled"][:, q % 2, :],
                                     ALU.add).then_inc(s["x"], 1)
                else:
                    ve.scalar_tensor_tensor(out=x_sb[:, tile, :], in0=ffn_acc[q][:, :], scalar=tg[:, 3:4],
                                            in1=x_sb[:, tile, :], op0=ALU.mult, op1=ALU.add).then_inc(s["x"], 1)

        def ve_ffn(ve, n):
            nf = NFS[n]
            ve_h(ve, n, 0, 0)

            def step(m, ms, it, per):
                if ms + 1 < 2 * nf:
                    ve_h(ve, n, m + 1, ms + 1)
                if ms % nf == nf - 1:
                    ve_ffn_x(ve, n, ms // nf)
            steps(ve, nf, step)

        def po_gu(po, m, ms):
            t, s = ffn_t[0], F[0]
            po.wait_ge(s["gu_hi"], m + 1)
            split_lo(po, t["gu_lo"][:, ms % 2], gu_view(slot(ffn_at[0]["gu", ms])), t["gu_hi"][:, ms % 2], s["gu_lo"])

        def po_wd(po, m, ms):
            t, s = ffn_t[0], F[0]
            po.wait_ge(s["wd_hi"], m + 1)
            split_lo(po, t["wd_lo"][:, ms % 2, :], slot(ffn_at[0]["wd", ms])[:, 0:DM], t["wd_hi"][:, ms % 2, :],
                     s["wd_lo"])

        def po_ffn0(po):
            total = 2 * NF0
            po_gu(po, 0, 0)
            ln_gpsimd(po, 1)
            po_gu(po, 1, 1)
            po_wd(po, 0, 0)
            po_gu(po, 2, 2)
            po_wd(po, 1, 1)

            def step(m, ms, it, per):
                if ms + 3 < total:
                    po_gu(po, m + 3, ms + 3)
                if ms + 2 < total:
                    po_wd(po, m + 2, ms + 2)
            steps(po, NF0, step)

        UNITS1 = BATCH

        def place1(h, i):
            return h ^ (i % 2)

        def pe_q1(pe, j, i, part):
            b = i % UNITS1
            if b == 0:
                pe.wait_ge(b_wq_lo, (j + i // UNITS1) * 2 + part + 1)
            for hh in range(2):
                mm = project(pe, (bank_a, bank_b)[part][:, hh * SEQ:(hh + 1) * SEQ],
                             (lambda k: wq1_hi[:, part, k, hh * HD:(hh + 1) * HD],
                              lambda k: wq1_lo[:, part, k, hh * HD:(hh + 1) * HD]),
                             (lambda k: xT_hi[:, k, b * SEQ:(b + 1) * SEQ], lambda k: xT_lo[:, k, b * SEQ:(b + 1) * SEQ]))
            mm.then_inc(b_q, 1)

        def pe_s1(pe, j, i, part, first=False):
            if part == 0:
                if not first:
                    pe.wait_ge(b_add, j * UNITS1 + i)
                if i % UNITS1 == 0:
                    pe.wait_ge(b_klo, j + i // UNITS1 + 1)
            pe.wait_ge(b_qlo, j * (2 * UNITS1) + 2 * i + part + 1)
            for h in (2 * part, 2 * part + 1):
                for c in range(TB):
                    at = place1(h, i) * 2 * CTX
                    for n, q in enumerate((q1T_hi, q1T_lo)):
                        mm = pe.matmul(bank_ss[:, c, at:at + 2 * CTX], q[:, h, c * P:(c + 1) * P],
                                       k1[:, i % UNITS1].rearrange("p r n -> p (r n)"), start=n == 0, stop=n == 1)
            if part == 1:
                mm.then_inc(b_s, 1)

        def pe_sqT(pe, j, i, part):
            pe.wait_ge(b_qsq, j * (2 * UNITS1) + 2 * i + part + 1)
            for c in range(TB):
                for h in (2 * part, 2 * part + 1):
                    at = (2 * c + place1(h, i) % 2) * P
                    mm = pe.transpose(kv1_bank[:, at:at + P], q_sq[:, h, c * P:(c + 1) * P], ident[:, :])
            mm.then_inc(b_sqT, 1)

        def pe_p1T(pe, j, i):
            pe.wait_ge(b_norm, j * UNITS1 + i + 1)
            for hp in range(2):
                for c in range(TB):
                    at = c * GH1 + 2 * hp
                    mm = pe.transpose(t1_bank[:, (hp * TB + c) * P:(hp * TB + c + 1) * P],
                                      prob1n[:, at:at + 2, :].rearrange("p a n -> p (a n)"), ident[:, :])
            mm.then_inc(b_t, 1)

        def pe_vw(pe, j, n, h):
            if n % 2 == 0 and h % 2 == 0:
                if h == 0:
                    pe.wait_ge(b_vlo, (j + n // 2) * 2 + 2)
                pe.wait_ge(b_wo_lo, (j + n // 2) * 2 + h // 2 + 1)
            if not (isinstance(j, int) and j < 0 and h == 0):
                pe.wait_ge(b_wlo, (j + 1) * 16 + (n - 2) * 8 + 2 * h)
            at = (h % 2) * CTX
            v = [t[:, n % 2].rearrange("p r n -> p (r n)")[:, at:at + 2 * CTX] for t in (v1_hi, v1_lo)]
            for k, (a, w) in enumerate(((v[0], wo1_hi), (v[0], wo1_lo), (v[1], wo1_hi))):
                mm = pe.matmul(w1_bank[:, :], a, w[:, h, :], start=k == 0, stop=k == 2)
            mm.then_inc(b_w, 1)

        def pe_o1(pe, j, i, c):
            if c == 0:
                pe.wait_ge(b_tlo, j * UNITS1 + i + 1)
                if i % 2 == 0:
                    pe.wait_ge(b_wlo, j * 16 + (i // 2) * 8 + 8)
            pe.wait_ge(b_acc, j * (2 * UNITS1) + 2 * i + c + 1)
            for hp in range(2):
                for k, (p, w) in enumerate(((p1T_hi, vw_hi), (p1T_hi, vw_lo), (p1T_lo, vw_hi))):
                    mm = pe.matmul(o1_bank[:, :], p[:, hp, c * P:(c + 1) * P], w[:, i // 2 % 2, i % 2, hp, :],
                                   start=hp == 0 and k == 0, stop=hp == 1 and k == 2)
            mm.then_inc(b_o, 1)

        def pe_krow(pe, g):
            pe.wait_ge(b_wkv_lo, g + 1)
            if not (isinstance(g, int) and g == 0):
                pe.wait_ge(b_klo, g)
            for c in range(2):
                mm = project(pe, kv1_bank[:, c * HD:(c + 1) * HD],
                             (lambda k: cT_hi[:, k, c * P:(c + 1) * P], lambda k: cT_lo[:, k, c * P:(c + 1) * P]),
                             (lambda k: wkv1_hi[:, 0, k, :], lambda k: wkv1_lo[:, 0, k, :]))
            mm.then_inc(b_kr, 1)

        def pe_v1(pe, g):
            pe.wait_ge(b_krs, g + 1)
            project(pe, kv1_bank[:, 0:BATCH * CTX],
                    (lambda k: wkv1_hi[:, 1, k, :], lambda k: wkv1_lo[:, 1, k, :]),
                    (lambda k: cT_hi[:, k, :], lambda k: cT_lo[:, k, :])).then_inc(b_v, 1)

        def pe_kT(pe, g):
            pe.wait_ge(b_kn, g + 1)
            pe.wait_ge(b_vlo, g * 2 + 2)
            for c in range(2):
                mm = pe.transpose(kv1_bank[:, c * P:(c + 1) * P], k_row[:, c, :], ident[:, :])
            mm.then_inc(b_kT, 1)

        def pe_unit1(pe, j, i, last):
            next1, next2 = not (last and i + 1 >= UNITS1), not (last and i + 2 >= UNITS1)
            pe_p1T(pe, j, i)
            if next1:
                pe_s1(pe, j, i + 1, 0)
                if i == 1 and not last:
                    pe.wait_ge(b_krs, j + 2)
                if i == 2 and not last:
                    pe.wait_ge(b_vlo, (j + 2) * 2)
                pe.wait_ge(b_ss, j * (2 * UNITS1) + 2 * i + 3)
                pe_sqT(pe, j, i + 1, 1)
                pe_s1(pe, j, i + 1, 1)
            if next2:
                pe_vw(pe, j, i // 2 + 1, i % 2 * 2)
            pe_o1(pe, j, i, 0)
            if i == 2 and not last:
                pe.wait_ge(b_ss, j * (2 * UNITS1) + 2 * i + 4)
                pe_kT(pe, j + 1)
            if next2:
                pe_q1(pe, j, i + 2, 0)
            pe_o1(pe, j, i, 1)
            if next2:
                pe_vw(pe, j, i // 2 + 1, i % 2 * 2 + 1)
                pe.wait_ge(b_ss, j * (2 * UNITS1) + 2 * i + 4)
                if i == 2:
                    pe.wait_ge(b_klo, j + 2)
                pe_sqT(pe, j, i + 2, 0)
                pe_q1(pe, j, i + 2, 1)
            if not last and i < 2:
                pe.wait_ge(b_ss, j * (2 * UNITS1) + 2 * i + 5)
                (pe_krow, pe_v1)[i](pe, j + 1)

        def pe_attn1(pe):
            pe.wait_ge(l_lo, 2 * NT + NT)
            pe_krow(pe, 0)
            pe_q1(pe, 0, 0, 0)
            pe_q1(pe, 0, 0, 1)
            pe_v1(pe, 0)
            pe_kT(pe, 0)
            pe_s1(pe, 0, 0, 0, first=True)
            pe_s1(pe, 0, 0, 1)
            pe_sqT(pe, 0, 0, 0)
            pe_q1(pe, 0, 1, 0)
            pe.wait_ge(b_ss, 1)
            pe_sqT(pe, 0, 0, 1)
            pe_q1(pe, 0, 1, 1)
            pe.wait_ge(b_ss, 2)
            pe_sqT(pe, 0, 1, 0)
            for h in range(GH1):
                pe_vw(pe, -1, 2, h)
            with pe.Fori(0, KV1 - 1) as j:
                for i in range(UNITS1):
                    pe_unit1(pe, j, i, False)
            for i in range(UNITS1):
                pe_unit1(pe, KV1 - 1, i, True)

        def ac_q1(ac, j, i, part):
            src = (bank_a, bank_b)[part][:, :].rearrange("p (h n) -> p h n", h=2)
            ac.wait_ge(b_q, j * (2 * UNITS1) + 2 * i + part + 1)
            ac.activation(q_sq[:, 2 * part:2 * part + 2, :], src, ACT.Square).then_inc(b_qsq, 1)
            ac.activation(q1T_hi[:, 2 * part:2 * part + 2, :], src, ACT.Copy).then_inc(b_qhi, 1)

        def ac_p1T(ac, j, i):
            ac.wait_ge(b_t, j * UNITS1 + i + 1)
            ac.activation(p1T_hi[:, :, :], t1_bank[:, :].rearrange("p (h n) -> p h n", h=2), ACT.Copy).then_inc(b_thi, 1)

        def vw_halves(n, h):
            for half in range(2):
                rows = slice(half * CTX, (half + 1) * CTX)
                yield rows, (n % 2, half ^ (h % 2), h // 2)

        def ac_vw(ac, j, n, h):
            ac.wait_ge(b_w, (j + 1) * 8 + (n - 2) * 4 + h + 1)
            for rows, (a, b, c) in vw_halves(n, h):
                ac.activation(vw_hi[rows, a, b, c, :], w1_bank[rows, :], ACT.Copy).then_inc(b_whi, 1)

        def score_parts(r):
            return bank_ss[:, :, :].rearrange("p c (h r n) -> p c h r n", h=GH1, r=2)[:, :, :, r, :]

        def ac_cross(ac, j, i):
            ac.wait_ge(b_s, j * UNITS1 + i + 1)
            ac.activation(logit[:, :, :].rearrange("p (c h) n -> p c h n", c=TB), score_parts(1),
                          ACT.Copy).then_inc(b_cross, 1)

        def ac_exp1(ac, j, i):
            ac.wait_ge(b_sub, j * UNITS1 + i + 1)
            ac.activation(prob1[:, :, :], logit[:, :, :], ACT.Exp).then_inc(b_exp, 1)

        def v1_copies(t, src):
            s4 = src.rearrange("p (m b n) -> p m b n", m=2, b=2)
            return (t[:, :, 0:2, :], s4), (t[:, :, 2, :], s4[:, :, 0, :])

        def ac_kv1(ac, job, g):
            rows = kv1_bank[:, 0:2 * HD].rearrange("p (c n) -> p c n", c=2)
            if job == 0:
                ac.wait_ge(b_kr, g + 1)
                ac.activation(k_row[:, :, :], rows, ACT.Copy).then_inc(b_krc, 1)
                ac.activation(k_sq[:, :, :], rows, ACT.Square).then_inc(b_krs, 1)
            elif job == 1:
                ac.wait_ge(b_v, g + 1)
                for dst, src in v1_copies(v1_hi, kv1_bank[:, 0:BATCH * CTX]):
                    ac.activation(dst, src, ACT.Copy).then_inc(b_vhi, 1)
            else:
                ac.wait_ge(b_kT, g + 1)
                ac.activation(k1[:, :, 0, :], kv1_bank[:, 0:BATCH * CTX].rearrange("p (b n) -> p b n", b=BATCH),
                              ACT.Identity, scale=kscale[:, 0:1]).then_inc(b_khi, 1)

        def l1_chunk(g, what, part):
            return l1_base + 4 * g + L1_CHUNKS[min(g, 1)].index((what, part))

        def ac_wq1(ac, j, n, part):
            k = l1_chunk(n, "wq", part)
            chunk_wait(ac, k, 4 if n else 0, j)
            if n:
                ac.wait_ge(b_q, j * (2 * UNITS1) + 2 * UNITS1 - 1 + part)
            split_hi(ac, wq1_hi[:, part], slot(k).rearrange("p (c n) -> p c n", c=KC), b_wq_hi)

        def ac_wo1(ac, j, n, part):
            k = l1_chunk(n, "wo", part)
            chunk_wait(ac, k, 4 if n else 0, j)
            if n:
                ac.wait_ge(b_w, j * 8 + 4 + 2 * part + 2)
            split_hi(ac, wo1_hi[:, 2 * part:2 * part + 2, :], slot(k).rearrange("p (h n) -> p h n", h=2), b_wo_hi)

        def ac_unit1(ac, j, i, last):
            next1, next2 = not (last and i + 1 >= UNITS1), not (last and i + 2 >= UNITS1)
            ac_p1T(ac, j, i)
            if next1:
                ac_cross(ac, j, i + 1)
            if not last:
                if i == 0:
                    ac.wait_ge(b_v, j + 1)
                    ac_wkv(ac, j + (KV0 + 1), wkv1_hi, b_wkv_hi)
                if i == 1:
                    ac_wo1(ac, j, 1, 0)
                if i == 2:
                    ac_wq1(ac, j, 1, 1)
            if next2:
                ac_vw(ac, j, i // 2 + 1, i % 2 * 2)
                if i == 2:
                    ac_kv1(ac, 2, j + 1)
                    ac_wo1(ac, j, 1, 1)
                ac_q1(ac, j, i + 2, 0)
            if next1:
                ac_exp1(ac, j, i + 1)
            if next2:
                ac_vw(ac, j, i // 2 + 1, i % 2 * 2 + 1)
            if i == 1 and not last:
                ac_wq1(ac, j, 1, 0)
            if next2:
                ac_q1(ac, j, i + 2, 1)
            if not last and i < 2:
                ac_kv1(ac, i, j + 1)

        def ac_attn1(ac):
            ac.wait_ge(F[0]["x"], NT)
            ac_wkv(ac, KV0, wkv1_hi, b_wkv_hi)
            ac_wq1(ac, 0, 0, 0)
            ac_wq1(ac, 0, 0, 1)
            ln_scalar(ac, 2)
            ac_kv1(ac, 0, 0)
            ac_q1(ac, 0, 0, 0)
            ac_q1(ac, 0, 0, 1)
            ac_kv1(ac, 1, 0)
            ac_wo1(ac, 0, 0, 0)
            ac_kv1(ac, 2, 0)
            ac_wo1(ac, 0, 0, 1)
            ac_cross(ac, 0, 0)
            ac_q1(ac, 0, 1, 0)
            ac_q1(ac, 0, 1, 1)
            ac_exp1(ac, 0, 0)
            for h in range(GH1):
                ac_vw(ac, -1, 2, h)
            with ac.Fori(0, KV1 - 1) as j:
                for i in range(UNITS1):
                    ac_unit1(ac, j, i, False)
            for i in range(UNITS1):
                ac_unit1(ac, KV1 - 1, i, True)

        def wide(ap, n):
            a = ap.shape[1]
            return ap.rearrange("p (a n) -> p a n", n=1).broadcast_to([P, a, n])

        def ve_q1(ve, j, i, part):
            ve.wait_ge(b_qhi, j * (2 * UNITS1) + 2 * i + part + 1)
            ve.tensor_tensor(q1T_lo[:, 2 * part:2 * part + 2, :],
                             (bank_a, bank_b)[part][:, :].rearrange("p (h n) -> p h n", h=2),
                             f32(q1T_hi[:, 2 * part:2 * part + 2, :]), ALU.subtract).then_inc(b_qlo, 1)

        def ve_p1T(ve, j, i):
            ve.wait_ge(b_thi, j * UNITS1 + i + 1)
            ve.tensor_tensor(p1T_lo[:, :, :], t1_bank[:, :].rearrange("p (h n) -> p h n", h=2), f32(p1T_hi[:, :, :]),
                             ALU.subtract).then_inc(b_tlo, 1)

        def ve_ss(ve, j, i, part):
            n = j * (2 * UNITS1) + 2 * i + part + 1
            ve.wait_ge(b_sqT, n)
            ve.tensor_reduce(q_ss[:, :, 2 * part:2 * part + 2], kv1_bank[:, :].rearrange("p (c h n) -> p c h n", c=TB, h=2),
                             AX_X, ALU.add).then_inc(b_ss, 1)
            if part == 1:
                ve.wait_ge(b_ss, n)
                ve.tensor_scalar(q_var[:, :], q_ss[:, :, :].rearrange("p c h -> p (c h)"), 1.0 / HD, EPS, ALU.mult,
                                 ALU.add).then_inc(b_var, 1)

        def ve_log_add(ve, j, i):
            ve.wait_ge(b_cross, j * UNITS1 + i + 1)
            l4 = logit[:, :, :].rearrange("p (c h) n -> p c h n", c=TB)
            ve.tensor_tensor(l4, score_parts(0), l4, ALU.add).then_inc(b_add, 1)

        def ve_log_rms(ve, j, i):
            n = j * UNITS1 + i + 1
            ve.wait_ge(b_add, n)
            ve.wait_ge(b_rms, n)
            ve.tensor_tensor(logit[:, :, :], logit[:, :, :], wide(q_rms[:, :], CTX), ALU.mult).then_inc(b_log, 1)

        def ve_log_max(ve, j, i):
            n = j * UNITS1 + i + 1
            ve.wait_ge(b_mask, n)
            ve.tensor_reduce(mx1[:, :], logit[:, :, :], AX_X, ALU.max).then_inc(b_max, 1)

        def ve_log_sub(ve, j, i):
            ve.wait_ge(b_max, j * UNITS1 + i + 1)
            ve.tensor_tensor(logit[:, :, :], logit[:, :, :], wide(mx1[:, :], CTX), ALU.subtract).then_inc(b_sub, 1)

        def ve_rec1(ve, j, i):
            n = j * UNITS1 + i + 1
            ve.wait_ge(b_exp, n)
            ve.tensor_reduce(sum1[:, :], prob1[:, :, :], AX_X, ALU.add).then_inc(b_sum, 1)
            ve.wait_ge(b_sum, n)
            ve.reciprocal(rinv1[:, :], sum1[:, :]).then_inc(b_rec, 1)

        def ve_vw(ve, j, n, h):
            at = (j + 1) * 16 + (n - 2) * 8 + 2 * h
            for half, (rows, (a, b, c)) in enumerate(vw_halves(n, h)):
                ve.wait_ge(b_whi, at + half + 1)
                ve.tensor_tensor(vw_lo[rows, a, b, c, :], w1_bank[rows, :], f32(vw_hi[rows, a, b, c, :]),
                                 ALU.subtract).then_inc(b_wlo, 1)

        def ve_add1(ve, j, i, c):
            t = TB * i + c
            ve.wait_ge(b_o, j * (2 * UNITS1) + 2 * i + c + 1)
            ve.scalar_tensor_tensor(out=x_sb[:, t, :], in0=o1_bank[:, :], scalar=tg[:, 1:2],
                                    in1=x_sb[:, t, :], op0=ALU.mult, op1=ALU.add).then_inc(b_acc, 1)

        def ve_kv1(ve, job, g):
            if job == 0:
                ve.wait_ge(b_krs, g + 1)
                ve.tensor_reduce(k_ss[:, :], k_sq[:, :, :], AX_X, ALU.add).then_inc(b_kss, 1)
                ve.wait_ge(b_kss, g + 1)
                ve.tensor_scalar(k_var[:, :], k_ss[:, :], 1.0 / HD, EPS, ALU.mult, ALU.add).then_inc(b_kvar, 1)
            elif job == 1:
                ve.wait_ge(b_vhi, g * 2 + 2)
                for (dst, src), (hi, _) in zip(v1_copies(v1_lo, kv1_bank[:, 0:BATCH * CTX]),
                                               v1_copies(v1_hi, kv1_bank[:, 0:BATCH * CTX])):
                    ve.tensor_tensor(dst, src, f32(hi), ALU.subtract).then_inc(b_vlo, 1)
            else:
                ve.wait_ge(b_khi, g + 1)
                ve.scalar_tensor_tensor(out=k1[:, :, 1, :], in0=kv1_bank[:, 0:BATCH * CTX].rearrange("p (b n) -> p b n", b=BATCH),
                                        scalar=kscale[:, 0:1], in1=f32(k1[:, :, 0, :]), op0=ALU.mult,
                                        op1=ALU.subtract).then_inc(b_klo, 1)

        def ve_knorm(ve, g):
            ve.wait_ge(b_krms, g + 1)
            ve.tensor_tensor(k_row[:, :, :], k_row[:, :, :], wide(k_rms[:, :], HD), ALU.mult).then_inc(b_kn, 1)

        def ve_unit1(ve, j, i, last):
            next1, next2 = not (last and i + 1 >= UNITS1), not (last and i + 2 >= UNITS1)
            ve_p1T(ve, j, i)
            if next1:
                ve_ss(ve, j, i + 1, 1)
                ve_log_add(ve, j, i + 1)
            if next2:
                ve_vw(ve, j, i // 2 + 1, i % 2 * 2)
            ve_add1(ve, j, i, 0)
            if i == 2 and not last:
                ve_kv1(ve, 2, j + 1)
            if next1:
                ve_log_rms(ve, j, i + 1)
                ve_log_max(ve, j, i + 1)
                ve_log_sub(ve, j, i + 1)
            if next2:
                ve_q1(ve, j, i + 2, 0)
            if next1:
                ve_rec1(ve, j, i + 1)
            if next2:
                ve_ss(ve, j, i + 2, 0)
            ve_add1(ve, j, i, 1)
            if next2:
                ve_vw(ve, j, i // 2 + 1, i % 2 * 2 + 1)
            if i == 1 and not last:
                ve_knorm(ve, j + 1)
            if next2:
                ve_q1(ve, j, i + 2, 1)
            if not last and i < 2:
                ve_kv1(ve, i, j + 1)

        def ve_attn1(ve):
            ve_kv1(ve, 0, 0)
            ve_q1(ve, 0, 0, 0)
            ve_knorm(ve, 0)
            ve_q1(ve, 0, 0, 1)
            ve_kv1(ve, 1, 0)
            ve_kv1(ve, 2, 0)
            ve_log_add(ve, 0, 0)
            ve_ss(ve, 0, 0, 0)
            ve_q1(ve, 0, 1, 0)
            ve_ss(ve, 0, 0, 1)
            ve_log_rms(ve, 0, 0)
            ve_log_max(ve, 0, 0)
            ve_log_sub(ve, 0, 0)
            ve_q1(ve, 0, 1, 1)
            ve_ss(ve, 0, 1, 0)
            ve_rec1(ve, 0, 0)
            for h in range(GH1):
                ve_vw(ve, -1, 2, h)
            with ve.Fori(0, KV1 - 1) as j:
                for i in range(UNITS1):
                    ve_unit1(ve, j, i, False)
            for i in range(UNITS1):
                ve_unit1(ve, KV1 - 1, i, True)

        def po_pow(po, out_ap, in_ap, done, wait, value):
            po.wait_ge(wait, value)
            po.tensor_tensor(out_ap, in_ap, neg_half[:, 0:in_ap.shape[1]], ALU.pow).then_inc(done, 1)

        def po_log_mask(po, j, i):
            po.wait_ge(b_log, j * UNITS1 + i + 1)
            m = mask_sb[:, :, :].rearrange("p c (h n) -> p c h n", h=1).broadcast_to([P, TB, GH1, CTX])
            l4 = logit[:, :, :].rearrange("p (c h) n -> p c h n", c=TB)
            po.tensor_tensor(l4, l4, m, ALU.add).then_inc(b_mask, 1)

        def po_norm1(po, j, i, first=False):
            po.wait_ge(b_rec, j * UNITS1 + i + 1)
            if not first:
                po.wait_ge(b_t, j * UNITS1 + i)
            po.tensor_tensor(prob1n[:, :, :], prob1[:, :, :], wide(rinv1[:, :], CTX), ALU.mult).then_inc(b_norm, 1)

        def po_wq1(po, j, n, part):
            po.wait_ge(b_wq_hi, (j + n) * 2 + part + 1)
            split_lo(po, wq1_lo[:, part], slot(l1_chunk(n, "wq", part)).rearrange("p (c n) -> p c n", c=KC),
                     wq1_hi[:, part], b_wq_lo)

        def po_wo1(po, j, n, part):
            po.wait_ge(b_wo_hi, (j + n) * 2 + part + 1)
            split_lo(po, wo1_lo[:, 2 * part:2 * part + 2, :],
                     slot(l1_chunk(n, "wo", part)).rearrange("p (h n) -> p h n", h=2),
                     wo1_hi[:, 2 * part:2 * part + 2, :], b_wo_lo)

        def po_unit1(po, j, i, last):
            next1 = not (last and i + 1 >= UNITS1)
            if next1:
                po_pow(po, q_rms[:, :], q_var[:, :], b_rms, b_var, j * UNITS1 + i + 2)
            if not last:
                if i == 0:
                    po_wkv(po, wkv1_hi, wkv1_lo, b_wkv_hi, b_wkv_lo, j + 2)
                if i == 1:
                    po_pow(po, k_rms[:, :], k_var[:, :], b_krms, b_kvar, j + 2)
                    po_wo1(po, j, 1, 0)
                if i == 2:
                    po_wq1(po, j, 1, 1)
            if next1:
                po_log_mask(po, j, i + 1)
            if i == 2 and not last:
                po_wo1(po, j, 1, 1)
            if next1:
                po_norm1(po, j, i + 1)
            if i == 1 and not last:
                po_wq1(po, j, 1, 0)

        def po_attn1(po):
            po_wkv(po, wkv1_hi, wkv1_lo, b_wkv_hi, b_wkv_lo, 1)
            ln_gpsimd(po, 2)
            po_wq1(po, 0, 0, 0)
            po_wq1(po, 0, 0, 1)
            po_pow(po, k_rms[:, :], k_var[:, :], b_krms, b_kvar, 1)
            po_wo1(po, 0, 0, 0)
            po_pow(po, q_rms[:, :], q_var[:, :], b_rms, b_var, 1)
            po_log_mask(po, 0, 0)
            po_wo1(po, 0, 0, 1)
            po_norm1(po, 0, 0, first=True)
            with po.Fori(0, KV1 - 1) as j:
                for i in range(UNITS1):
                    po_unit1(po, j, i, False)
            for i in range(UNITS1):
                po_unit1(po, KV1 - 1, i, True)

        @block.gpsimd
        def _(po):
            po.memset(neg_half[:, :], -0.5).then_inc(s_half, 1)
            po.memset(ident[:, :], 0.0).then_inc(s_ident, 1)
            po.wait_ge(s_ident, 1)
            po.affine_select(out=ident[:, :], in_=ident[:, :], compare_op=ALU.not_equal, fill=1.0, base=0,
                             pattern=[[-1, P]], channel_multiplier=1).then_inc(s_ident, 1)
            po.wait_ge(s_half, 1)
            po_wkv(po, wkv_hi, wkv_lo, a_wkv_hi, a_wkv_lo, 1)
            ln_gpsimd(po, 0)
            po.wait_ge(s_chi, 1)
            split_lo(po, cT_lo[:, :, :], prob[:, :, 0:BATCH * CTX], cT_hi[:, :, :], s_clo)
            po_wq(po, 0, 0)
            po_wo(po, 0, 0)
            po_wq(po, 0, 1)
            po_attn0(po)
            po_ffn0(po)
            po_attn1(po)
            ln_gpsimd(po, 3)

        @block.scalar
        def _(ac):
            ac.sem_inc(a_exp, 2)
            ac_wkv(ac, 0, wkv_hi, a_wkv_hi)
            ac.wait_ge(s_ctx, 16)
            split_hi(ac, cT_hi[:, :, :], prob[:, :, 0:BATCH * CTX], s_chi)
            ln_scalar(ac, 0)
            ac_wq(ac, 0, 0)
            ac_wo(ac, 0, 0)
            ac_wq(ac, 0, 1)
            ac.wait_ge(s_small, 16 * 7)
            ac.activation(tg[:, :], gates[:, :], ACT.Tanh).then_inc(s_tg, 1)
            ac_attn0(ac)
            ac_ffn(ac, 0, 1, lambda: ac.wait_ge(a_acc, 2 * KV0 * UNITS0 + 2))
            ac_attn1(ac)
            ac_ffn(ac, 1, 3, lambda: ac.wait_ge(b_acc, 1 + 2 * UNITS1 * KV1))

        @block.vector
        def _(ve):
            ve.sem_inc(b_acc, 1)
            ve.sem_inc(a_acc, 2)
            ve.sem_inc(a_olo, 1)
            ln_vector(ve, 0, lambda t: ve.wait_ge(s_x[t], 16))
            ve.wait_ge(s_small, 16 * 7)
            ve.scalar_tensor_tensor(out=kscale[:, :], in0=qn_w[:, :], scalar=SCALE, in1=kn_w[:, :], op0=ALU.mult,
                                    op1=ALU.mult).then_inc(s_ksc, 1)
            ve.wait_ge(s_tg, 1)
            ve.wait_ge(s_ksc, 1)
            ve_attn0(ve)
            ln_vector(ve, 1, lambda t: ve.wait_ge(a_acc, 2 * KV0 * UNITS0 + 2 - NT + t + 1))
            ve.wait_ge(s_ad, 16)
            ve.tensor_scalar(ffn_t[0]["tgad"][:, :], ffn_t[0]["ad"][:, :], tg[:, 2:3], None,
                             ALU.mult).then_inc(F[0]["tgad"], 1)
            ve.wait_ge(F[0]["tgad"], 1)
            ve_ffn(ve, 0)
            ln_vector(ve, 2, lambda t: ve.wait_ge(F[0]["x"], t + 1))
            ve_attn1(ve)
            ln_vector(ve, 3, lambda t: ve.wait_ge(b_acc, 1 + 2 * UNITS1 * KV1 - NT + t + 1))
            ve_ffn(ve, 1)

        @block.tensor
        def _(pe):
            pe.wait_ge(s_ident, 2)
            ln_tensor(pe, 0)
            pe_attn0(pe)
            ln_tensor(pe, 1)
            pe_ffn(pe, 0, 1)
            ln_tensor(pe, 2)
            pe_attn1(pe)
            ln_tensor(pe, 3)
            pe_ffn(pe, 1, 3)


def kernel(x, ctx_4096, mask_1x1xSxS2_ff0, g_xattn, g_ffn, L0_xattn_Wq, L0_xattn_Wk, L0_xattn_Wv, L0_xattn_Wo,
           L0_ffn_Wg, L0_ffn_Wu, L0_ffn_Wd, L0_ffn_ag, L0_ffn_au, L0_ffn_ad, L1_xattn_q_proj_w, L1_xattn_k_proj_w,
           L1_xattn_v_proj_w, L1_xattn_o_proj_w, L1_xattn_q_norm_w, L1_xattn_k_norm_w, L1_ffn_W_gate, L1_ffn_W_up,
           L1_ffn_W_down):
    import numpy as np
    import concourse.bacc as bacc
    from concourse.bass_utils import run_bass_kernel_spmd

    def t(a):
        return np.ascontiguousarray(np.asarray(a).T)

    def padded(a, axis):
        a = np.asarray(a)
        width = [(0, 0)] * a.ndim
        width[axis] = (0, F0_PAD - F0)
        return np.pad(a, width)

    arrays = {
        "x": np.asarray(x).reshape(BATCH * SEQ, DM),
        "ctxT": t(np.asarray(ctx_4096).reshape(BATCH * CTX, DM)),
        "mask": np.asarray(mask_1x1xSxS2_ff0).reshape(SEQ, CTX),
        "g_xattn": np.asarray(g_xattn), "g_ffn": np.asarray(g_ffn),
        "wq0": np.asarray(L0_xattn_Wq), "wk0": np.asarray(L0_xattn_Wk),
        "wv0": np.asarray(L0_xattn_Wv), "wo0": np.asarray(L0_xattn_Wo),
        "wg0T": t(padded(L0_ffn_Wg, 0)), "wu0T": t(padded(L0_ffn_Wu, 0)), "wd0T": t(padded(L0_ffn_Wd, 1)),
        "ag": t(padded(L0_ffn_ag, 0).reshape(NF0, P)), "au": t(padded(L0_ffn_au, 0).reshape(NF0, P)),
        "ad": np.asarray(L0_ffn_ad),
        "wq1T": t(L1_xattn_q_proj_w), "wk1T": t(L1_xattn_k_proj_w), "wv1T": t(L1_xattn_v_proj_w),
        "wo1T": t(L1_xattn_o_proj_w),
        "qnorm": np.asarray(L1_xattn_q_norm_w).reshape(HD, 1), "knorm": np.asarray(L1_xattn_k_norm_w).reshape(HD, 1),
        "wg1T": t(L1_ffn_W_gate), "wu1T": t(L1_ffn_W_up), "wd1T": t(L1_ffn_W_down),
    }
    arrays = {f"in_{k}": np.ascontiguousarray(v) for k, v in arrays.items()}
    nc = bacc.Bacc("TRN2", target_bir_lowering=False, num_devices=1)
    aps = [nc.dram_tensor(k, v.shape, mybir.dt.from_np(v.dtype), kind="ExternalInput").ap() for k, v in arrays.items()]
    out = nc.dram_tensor("out_x", (BATCH * SEQ, DM), F32, kind="ExternalOutput").ap()
    flamingo_two_layers(nc, *aps, out)
    r = run_bass_kernel_spmd(nc, [arrays], core_ids=[0])
    return r.results[0]["out_x"].reshape(BATCH, SEQ, DM)
```

```python
from contextlib import ExitStack

import concourse.bass as bass
from concourse import mybir

F32 = mybir.dt.float32
F32R = mybir.dt.float32r
F16 = mybir.dt.float16
ALU = mybir.AluOpType
ACT = mybir.ActivationFunctionType
AX_X = mybir.AxisListType.X

P = 128
BATCH, SEQ, DM = 4, 256, 512
CTX = 64
HD = 128
HEADS = 32
KV0, KV1 = 4, 8
KC = DM // P
NT = BATCH * SEQ // P
TB = SEQ // P
KVL0 = SEQ + CTX
SCALE = float(HD) ** -0.5
EPS = 1e-5

RING = 4
CHUNK = 1024

PAIRS0 = HEADS // KV0 // 2
UNITS0 = PAIRS0 * BATCH
QLEAD = 3
NCH0 = 3

GH1 = HEADS // KV1

F0, F0_PAD = 1376, 1408
F1 = 1792
NF0, NF1 = F0_PAD // P, F1 // P


def flamingo_two_layers(nc, x, ctxT, mask, g_xattn, g_ffn, wq0, wk0, wv0, wo0, wg0T, wu0T, wd0T,
                        ag, au, ad, wq1T, wk1T, wv1T, wo1T, qnorm, knorm, wg1T, wu1T, wd1T, out):
    ctx = ExitStack()

    def sem(name):
        return ctx.enter_context(nc.semaphore(name))

    def sb(stack, name, shape, dt=F32):
        return stack.enter_context(nc.sbuf_tensor(name, shape, dt))

    def f32(ap):
        return ap.bitcast(F32)

    with ctx:
        x_sb = sb(ctx, "x_sb", [P, NT, DM])
        xT_hi = sb(ctx, "xT_hi", [P, KC, NT * P], F32R)
        xT_lo = sb(ctx, "xT_lo", [P, KC, NT * P], F32R)
        cT_hi = sb(ctx, "cT_hi", [P, KC, BATCH * CTX], F32R)
        cT_lo = sb(ctx, "cT_lo", [P, KC, BATCH * CTX], F32R)
        ident = sb(ctx, "ident", [P, P])
        stage = sb(ctx, "stage", [P, RING, CHUNK])
        kv_stage = sb(ctx, "kv_stage", [P, 2, KC, HD])
        ln_out = sb(ctx, "ln_out", [P, 4, DM])
        ln_stats = sb(ctx, "ln_stats", [P, NT, 6])
        ln_mv = sb(ctx, "ln_mv", [P, NT, 2])
        ln_var = sb(ctx, "ln_var", [P, NT])
        ln_rstd = sb(ctx, "ln_rstd", [P, NT])
        neg_half = sb(ctx, "neg_half", [P, NT])
        gates = sb(ctx, "gates", [P, 4])
        tg = sb(ctx, "tg", [P, 4])
        mask_sb = sb(ctx, "mask_sb", [P, TB, CTX])
        qn_w = sb(ctx, "qn_w", [P, 1])
        kn_w = sb(ctx, "kn_w", [P, 1])
        kscale = sb(ctx, "kscale", [P, 1])
        ag_sb = sb(ctx, "ag_sb", [P, NF0])
        au_sb = sb(ctx, "au_sb", [P, NF0])
        ad_row = sb(ctx, "ad_row", [P, DM])
        tgad = sb(ctx, "tgad", [P, DM])

        r0 = ExitStack()
        wq_hi = sb(r0, "wq_hi", [P, 2, KC, 2 * HD], F32R)
        wq_lo = sb(r0, "wq_lo", [P, 2, KC, 2 * HD], F32R)
        wo_hi = sb(r0, "wo_hi", [P, 2, 2, DM], F32R)
        wo_lo = sb(r0, "wo_lo", [P, 2, 2, DM], F32R)
        wkv_hi = sb(r0, "wkv_hi", [P, 2, KC, HD], F32R)
        wkv_lo = sb(r0, "wkv_lo", [P, 2, KC, HD], F32R)
        k_hi = sb(r0, "k_hi", [P, BATCH, KVL0], F32R)
        k_lo = sb(r0, "k_lo", [P, BATCH, KVL0], F32R)
        v_hi = sb(r0, "v_hi", [P, NT + BATCH, HD], F32R)
        v_lo = sb(r0, "v_lo", [P, NT + BATCH, HD], F32R)
        vT = sb(r0, "vT", [P, NT + BATCH, P])
        qT_hi = sb(r0, "qT_hi", [P, 4, 2 * SEQ], F32R)
        qT_lo = sb(r0, "qT_lo", [P, 4, 2 * SEQ], F32R)
        prob = sb(r0, "prob", [P, 4, KVL0])
        probn = sb(r0, "probn", [P, 4, NCH0 * P])
        pT_hi = sb(r0, "pT_hi", [P, NCH0, 2 * SEQ], F32R)
        pT_lo = sb(r0, "pT_lo", [P, 2, 2 * SEQ], F32R)
        oT_hi = sb(r0, "oT_hi", [P, 2 * SEQ], F32R)
        oT_lo = sb(r0, "oT_lo", [P, 2 * SEQ], F32R)
        nmax = sb(r0, "nmax", [P, 4])
        rsum = sb(r0, "rsum", [P, 4])
        rinv = sb(r0, "rinv", [P, 4])
        r0.close()

        def ffn_buffers(n, parts, behind=0):
            r = ExitStack()
            if behind:
                sb(r, f"ffn{n}_behind", [P, behind])
            t = {}
            for part in parts:
                t["gu_" + part] = sb(r, f"gu{n}_{part}", [P, 2, 2, KC, P], F32R)
            for part in parts:
                t["wd_" + part] = sb(r, f"wd{n}_{part}", [P, 2, DM], F32R)
            t["s"] = sb(r, f"silu{n}", [P, 2, 2 * SEQ])
            t["h"] = sb(r, f"h{n}", [P, 2, 2 * SEQ])
            t["h_hi"] = sb(r, f"h{n}_hi", [P, 2, 2 * SEQ], F32R)
            t["h_lo"] = sb(r, f"h{n}_lo", [P, 2, 2 * SEQ], F32R)
            if n == 0:
                t["scaled"] = sb(r, "scaled", [P, 2, DM])
            r.close()
            return t

        VW, Q1, L1 = 8 * DM, GH1 * SEQ, TB * GH1 * CTX
        ffn_t = [ffn_buffers(0, ("hi", "lo")), ffn_buffers(1, ("hi",), behind=2 * VW + 3 * Q1 + 3 * L1)]

        r1 = ExitStack()
        vw_hi = sb(r1, "vw_hi", [P, 2, 2, 2, DM], F32R)
        vw_lo = sb(r1, "vw_lo", [P, 2, 2, 2, DM], F32R)
        q1T_hi = sb(r1, "q1T_hi", [P, GH1, SEQ], F32R)
        q1T_lo = sb(r1, "q1T_lo", [P, GH1, SEQ], F32R)
        q_sq = sb(r1, "q_sq", [P, GH1, SEQ])
        logit = sb(r1, "logit", [P, TB * GH1, CTX])
        prob1 = sb(r1, "prob1", [P, TB * GH1, CTX])
        prob1n = sb(r1, "prob1n", [P, TB * GH1, CTX])
        wq1_hi = sb(r1, "wq1_hi", [P, 2, KC, 2 * HD], F32R)
        wq1_lo = sb(r1, "wq1_lo", [P, 2, KC, 2 * HD], F32R)
        wo1_hi = sb(r1, "wo1_hi", [P, GH1, DM], F32R)
        wo1_lo = sb(r1, "wo1_lo", [P, GH1, DM], F32R)
        wkv1_hi = sb(r1, "wkv1_hi", [P, 2, KC, HD], F32R)
        wkv1_lo = sb(r1, "wkv1_lo", [P, 2, KC, HD], F32R)
        k1 = sb(r1, "k1", [P, BATCH, 2, CTX], F32R)
        v1_hi = sb(r1, "v1_hi", [P, 2, 3, CTX], F32R)
        v1_lo = sb(r1, "v1_lo", [P, 2, 3, CTX], F32R)
        k_row = sb(r1, "k_row", [P, 2, HD])
        k_sq = sb(r1, "k_sq", [P, 2, HD])
        p1T_hi = sb(r1, "p1T_hi", [P, 2, SEQ], F32R)
        p1T_lo = sb(r1, "p1T_lo", [P, 2, SEQ], F32R)
        q_ss = sb(r1, "q_ss", [P, TB, GH1])
        q_var = sb(r1, "q_var", [P, TB * GH1])
        q_rms = sb(r1, "q_rms", [P, TB * GH1])
        k_ss = sb(r1, "k_ss", [P, 2])
        k_var = sb(r1, "k_var", [P, 2])
        k_rms = sb(r1, "k_rms", [P, 2])
        mx1 = sb(r1, "mx1", [P, TB * GH1])
        sum1 = sb(r1, "sum1", [P, TB * GH1])
        rinv1 = sb(r1, "rinv1", [P, TB * GH1])
        r1.close()

        def bank(name):
            return ctx.enter_context(nc.psum_tensor(name, [P, 512], F32))

        bank_ss = ctx.enter_context(nc.psum_tensor("bank_s", [P, 2, 512], F32))
        bank_s = [bank_ss[:, 0, :], bank_ss[:, 1, :]]
        bank_t = [bank("bank_t0"), bank("bank_t1"), bank("bank_t2")]
        bank_o = bank("bank_o")
        bank_a, bank_b = bank("bank_a"), bank("bank_b")
        t1_bank, w1_bank, o1_bank, kv1_bank = bank_t[0], bank_t[1], bank_t[2], bank_o
        ffn_g, ffn_u = [bank_s[0], bank_s[1]], [bank_o, bank_a]
        ffn_acc = [bank_t[0], bank_t[1], bank_t[2], bank_b]

        s_stage = [sem(f"stage_loaded{i}") for i in range(RING)]
        s_x = [sem(f"x_loaded{i}") for i in range(NT)]
        s_ctx = sem("ctx_loaded")
        s_small = sem("small_loaded")
        s_kvst = sem("kv_stage_loaded")
        s_out = sem("out_stored")
        s_ident = sem("ident_ready")
        s_half = sem("neg_half_ready")
        s_tg = sem("tg_ready")
        s_ksc = sem("kscale_ready")
        s_chi, s_clo = sem("ctx_hi"), sem("ctx_lo")
        l_stats, l_mv, l_var, l_rstd = sem("ln_stats_done"), sem("ln_mv_done"), sem("ln_var_done"), sem("ln_rstd_done")
        l_xn, l_tr, l_hi, l_lo = sem("ln_out_done"), sem("ln_transposed"), sem("ln_hi_done"), sem("ln_lo_done")
        a_wq_hi, a_wq_lo = sem("a_wq_hi"), sem("a_wq_lo")
        a_wo_hi, a_wo_lo = sem("a_wo_hi"), sem("a_wo_lo")
        a_wkv_hi, a_wkv_lo = sem("a_wkv_hi"), sem("a_wkv_lo")
        a_q, a_qhi, a_qlo = sem("a_q"), sem("a_q_hi"), sem("a_q_lo")
        a_s, a_max, a_exp = sem("a_scores"), sem("a_max"), sem("a_exp")
        a_rec, a_norm, a_dup = sem("a_recip"), sem("a_norm"), sem("a_dup")
        a_t, a_thi, a_tlo = sem("a_pT"), sem("a_pT_hi"), sem("a_pT_lo")
        a_pv, a_ohi, a_olo = sem("a_pv"), sem("a_o_hi"), sem("a_o_lo")
        a_wo, a_acc = sem("a_wo"), sem("a_acc")
        a_k, a_khi, a_klo = sem("a_k"), sem("a_k_hi"), sem("a_k_lo")
        a_vT, a_vTc = sem("a_vT"), sem("a_vT_copied")
        a_v, a_vhi, a_vlo = sem("a_v"), sem("a_v_hi"), sem("a_v_lo")
        F = [{k: sem(f"f{n}_{k}") for k in ("gu_hi", "wd_hi", "gate", "up", "silu", "h", "h_hi", "h_lo", "down",
                                             "acc", "x") + ("gu_lo", "wd_lo", "tgad", "scaled") * (n == 0)}
             for n in range(2)]
        b_wq_hi, b_wq_lo = sem("b_wq_hi"), sem("b_wq_lo")
        b_wo_hi, b_wo_lo = sem("b_wo_hi"), sem("b_wo_lo")
        b_wkv_hi, b_wkv_lo = sem("b_wkv_hi"), sem("b_wkv_lo")
        b_q, b_qhi, b_qlo, b_qsq = sem("b_q"), sem("b_q_hi"), sem("b_q_lo"), sem("b_q_squared")
        b_sqT, b_ss, b_var, b_rms = sem("b_q_sq_transposed"), sem("b_q_ss"), sem("b_q_var"), sem("b_q_rms")
        b_s, b_cross, b_add, b_log, b_mask = sem("b_scores"), sem("b_q_k_lo"), sem("b_added"), sem("b_logit"), sem("b_masked")
        b_max, b_sub, b_exp = sem("b_max"), sem("b_sub"), sem("b_exp")
        b_sum, b_rec, b_norm = sem("b_sum"), sem("b_recip"), sem("b_norm")
        b_t, b_thi, b_tlo = sem("b_pT"), sem("b_pT_hi"), sem("b_pT_lo")
        b_w, b_whi, b_wlo = sem("b_vw"), sem("b_vw_hi"), sem("b_vw_lo")
        b_o, b_acc = sem("b_out"), sem("b_acc")
        b_kr, b_krs, b_kss = sem("b_krow"), sem("b_krow_copied_and_squared"), sem("b_k_ss")
        b_kvar, b_krms, b_kn = sem("b_k_var"), sem("b_k_rms"), sem("b_k_normed")
        b_kT, b_khi, b_klo = sem("b_kT"), sem("b_k_hi"), sem("b_k_lo")
        b_v, b_vhi, b_vlo = sem("b_v"), sem("b_v_hi"), sem("b_v_lo")

        stream = []

        def slot(n):
            return stage[:, n % RING, :]

        def slot16(n):
            return stage[:, n % RING, :].bitcast(F16)

        def k_rows(w, a, b):
            return w.rearrange("(c p) n -> p c n", p=P)[:, :, a:b]

        def head_rows(w, a, b):
            return w[a * HD:b * HD, :].rearrange("(h p) n -> p h n", p=P)

        def gu_view(v):
            return v[:, 0:CHUNK].rearrange("p (w c n) -> p w c n", w=2, c=KC)

        def ffn_order(nf):
            yield from (("gu", 0), ("gu", 1), ("wd", 0), ("gu", 2), ("wd", 1))
            for m in range(2 * nf):
                if m + 3 < 2 * nf:
                    yield "gu", m + 3
                if m + 2 < 2 * nf:
                    yield "wd", m + 2

        def add_ffn(n, wg, wu, wd):
            nf, at = NFS[n], {}
            part = "lo" if n == 0 else "hi"
            for what, m in ffn_order(nf):
                f, k = m % nf, len(stream)
                v = slot(k) if n == 0 else slot16(k)
                at[what, m] = k
                if what == "gu":
                    v = gu_view(v)
                    dmas = [(v[:, 0], k_rows(wg, f * P, (f + 1) * P)), (v[:, 1], k_rows(wu, f * P, (f + 1) * P))]
                else:
                    dmas = [(v[:, 0:DM], wd[f * P:(f + 1) * P, :])]
                stream.append((dmas, F[n][f"{what}_{part}"], m + 1))
            return at

        NFS = (NF0, NF1)
        for pair in range(HEADS // 2):
            v = slot(len(stream)).rearrange("p (c n) -> p c n", c=KC)
            stream.append(([(v, k_rows(wq0, pair * 2 * HD, (pair + 1) * 2 * HD))], a_wq_lo, pair + 1))
            v = slot(len(stream)).rearrange("p (h n) -> p h n", h=2)
            stream.append(([(v, head_rows(wo0, 2 * pair, 2 * pair + 2))], a_wo_lo, pair + 1))
        ffn_at = [add_ffn(0, wg0T, wu0T, wd0T)]
        l1_base = len(stream)
        L1_CHUNKS = (("wq", 0), ("wq", 1), ("wo", 0), ("wo", 1)), (("wo", 0), ("wq", 0), ("wq", 1), ("wo", 1))
        for j in range(KV1):
            for what, part in L1_CHUNKS[min(j, 1)]:
                h = j * GH1 + 2 * part
                if what == "wq":
                    v = slot(len(stream)).rearrange("p (c n) -> p c n", c=KC)
                    stream.append(([(v, k_rows(wq1T, h * HD, (h + 2) * HD))], b_wq_lo, 2 * j + part + 1))
                else:
                    v = slot(len(stream)).rearrange("p (h n) -> p h n", h=2)
                    stream.append(([(v, head_rows(wo1T, h, h + 2))], b_wo_lo, 2 * j + part + 1))
        ffn_at.append(add_ffn(1, wg1T, wu1T, wd1T))
        landed, slot_sum = [], [0] * RING
        for n, (dmas, _, _) in enumerate(stream):
            slot_sum[n % RING] += 16 * len(dmas)
            landed.append(slot_sum[n % RING])

        def chunk_wait(eng, k, per=0, it=0):
            eng.wait_ge(s_stage[k % RING], landed[k] + (it * (landed[k + per] - landed[k]) if per else 0))

        block = ctx.enter_context(nc.Block())

        def load_kv(sp, n, wk, wv, head):
            if 1 <= n <= KV0:
                sp.wait_ge(a_wkv_lo, n)
            elif n > KV0:
                sp.wait_ge(b_wkv_lo, n - KV0)
            for w, src in enumerate((wk, wv)):
                sp.dma_start(kv_stage[:, w, :, :], k_rows(src, head * HD, (head + 1) * HD)).then_inc(s_kvst, 16)

        @block.sync
        def _(sp):
            x_rows = x.rearrange("(t p) d -> t p d", p=P)
            for t in range(NT):
                sp.dma_start(x_sb[:, t, :], x_rows[t]).then_inc(s_x[t], 16)
            load_kv(sp, 0, wk0, wv0, 0)
            sp.dma_start(prob[:, :, 0:BATCH * CTX], ctxT.rearrange("(c p) n -> p c n", p=P)).then_inc(s_ctx, 16)
            for n in range(RING):
                for dst, src in stream[n][0]:
                    sp.dma_start(dst, src).then_inc(s_stage[n % RING], 16)
            for dst, src in ((gates[:, 0:2], g_xattn.rearrange("(a n) -> a n", a=1).broadcast_to([P, 2])),
                             (gates[:, 2:4], g_ffn.rearrange("(a n) -> a n", a=1).broadcast_to([P, 2])),
                             (mask_sb[:, :, :], mask.rearrange("(c p) n -> p c n", p=P)),
                             (qn_w[:, :], qnorm), (kn_w[:, :], knorm), (ag_sb[:, :], ag), (au_sb[:, :], au),
                             (ad_row[:, :], ad.rearrange("(a n) -> a n", a=1).broadcast_to([P, DM]))):
                sp.dma_start(dst, src).then_inc(s_small, 16)
            kv_n = 1
            for n in range(RING, len(stream)):
                if n < l1_base and n % (2 * PAIRS0) == 4 and kv_n < KV0:
                    load_kv(sp, kv_n, wk0, wv0, kv_n)
                    kv_n += 1
                if n in [l1_base - RING] + [l1_base + 4 * j for j in range(1, KV1)]:
                    load_kv(sp, kv_n, wk1T, wv1T, kv_n - KV0)
                    kv_n += 1
                sp.wait_ge(stream[n - RING][1], stream[n - RING][2])
                for dst, src in stream[n][0]:
                    sp.dma_start(dst, src).then_inc(s_stage[n % RING], 16)
            o_rows = out.rearrange("(t p) d -> t p d", p=P)
            for t in range(NT):
                sp.wait_ge(F[1]["x"], t + 1)
                sp.dma_start(o_rows[t], x_sb[:, t, :]).then_inc(s_out, 16)
            sp.wait_ge(s_out, 16 * NT)

        def ve_ln_stats(ve, k, b, x_ready):
            for t in (2 * b, 2 * b + 1):
                x_ready(t)
                ve.bn_stats(ln_stats[:, t, :], x_sb[:, t, :]).then_inc(l_stats, 1)
            for t in (2 * b, 2 * b + 1):
                ve.wait_ge(l_stats, NT * k + t + 1)
                ve.bn_aggr(ln_mv[:, t, :], ln_stats[:, t, :]).then_inc(l_mv, 1)
            ve.wait_ge(l_mv, NT * k + 2 * b + 2)
            ve.tensor_scalar(ln_var[:, 2 * b:2 * b + 2], ln_mv[:, 2 * b:2 * b + 2, 1], EPS, None,
                             ALU.add).then_inc(l_var, 1)

        def po_ln(po, k, b):
            po.wait_ge(l_var, BATCH * k + b + 1)
            po.tensor_tensor(ln_rstd[:, 2 * b:2 * b + 2], ln_var[:, 2 * b:2 * b + 2], neg_half[:, 0:2],
                             ALU.pow).then_inc(l_rstd, 1)

        def ve_ln_norm(ve, k, b):
            ve.wait_ge(l_rstd, BATCH * k + b + 1)
            if BATCH * k + b >= 2:
                ve.wait_ge(l_tr, NT * k + 2 * b - 2)
            for t in (2 * b, 2 * b + 1):
                ve.tensor_scalar(ln_out[:, t % 4, :], x_sb[:, t, :], ln_mv[:, t, 0:1], ln_rstd[:, t:t + 1],
                                 ALU.subtract, ALU.mult).then_inc(l_xn, 1)

        def pe_ln(pe, k, b, banks):
            for t in (2 * b, 2 * b + 1):
                pe.wait_ge(l_xn, NT * k + t + 1)
                for c in range(KC):
                    mm = pe.transpose(banks[t % 2][:, c * P:(c + 1) * P], ln_out[:, t % 4, c * P:(c + 1) * P], ident[:, :])
                mm.then_inc(l_tr, 1)

        def ac_ln(ac, k, b, banks):
            for t in (2 * b, 2 * b + 1):
                ac.wait_ge(l_tr, NT * k + t + 1)
                ac.activation(xT_hi[:, :, t * P:(t + 1) * P], banks[t % 2][:, :].rearrange("p (c n) -> p c n", c=KC),
                              ACT.Copy).then_inc(l_hi, 1)

        def ve_ln_lo(ve, k, b, banks):
            for t in (2 * b, 2 * b + 1):
                ve.wait_ge(l_hi, NT * k + t + 1)
                ve.tensor_tensor(xT_lo[:, :, t * P:(t + 1) * P], banks[t % 2][:, :].rearrange("p (c n) -> p c n", c=KC),
                                 f32(xT_hi[:, :, t * P:(t + 1) * P]), ALU.subtract).then_inc(l_lo, 1)

        ln0_banks = ((bank_t[0], bank_t[1]), (bank_s[0], bank_s[1]))
        ln1_banks = (bank_s[0], bank_s[1])
        ln2_banks = (bank_t[0], bank_t[2])
        ln3_banks = (bank_a, bank_b)
        x_after = (lambda eng, t: eng.wait_ge(s_x[t], 16),
                   lambda eng, t: eng.wait_ge(a_acc, 2 * KV0 * BATCH * PAIRS0 + 2 - NT + t + 1),
                   lambda eng, t: eng.wait_ge(F[0]["x"], t + 1),
                   lambda eng, t: eng.wait_ge(b_acc, 1 + 2 * BATCH * KV1 - NT + t + 1))

        def project(pe, out_ap, lhs, rhs, chunks=range(KC), first=True, last=True):
            (l_h, l_l), (r_h, r_l) = lhs, rhs
            for c in chunks:
                passes = [(l_h, r_h), (l_h, r_l)] + ([(l_l, r_h)] if l_l else [])
                for n, (a, b) in enumerate(passes):
                    mm = pe.matmul(out_ap, a(c), b(c), start=first and c == chunks[0] and n == 0,
                                   stop=last and c == chunks[-1] and n == len(passes) - 1)
            return mm

        def per_g(n, g):
            return g * n

        Q_PARTS = ((0,), (1,), (2, 3))

        def pe_q(pe, g, blk, part):
            par, slot_, hh, half = (blk // 4) % 2, blk % 4, blk % 2, blk % 4 // 2
            if part == 0:
                if slot_ == 0:
                    pe.wait_ge(a_wq_lo, per_g(PAIRS0, g) + blk // 4 + 1)
                pe.wait_ge(a_qlo, per_g(UNITS0, g) + blk)
            mm = project(pe, bank_a[:, :],
                         (lambda c: wq_hi[:, par, c, hh * HD:(hh + 1) * HD], lambda c: wq_lo[:, par, c, hh * HD:(hh + 1) * HD]),
                         (lambda c: xT_hi[:, c, half * 512:(half + 1) * 512], lambda c: xT_lo[:, c, half * 512:(half + 1) * 512]),
                         chunks=Q_PARTS[part], first=part == 0, last=part == 2)
            if part == 2:
                mm.then_inc(a_q, 1)

        def pe_scores(pe, g, i, j):
            b, hh, c = i % 4, j // 2, j % 2
            s = (b // 2) * 2 + hh
            if c == 0:
                pe.wait_ge(a_qlo, per_g(UNITS0, g) + (i // 4) * 4 + s + 1)
            if i % UNITS0 == 0 and j == 0:
                pe.wait_ge(a_klo, per_g(3, g) + 3 * (i // UNITS0) + 3)
            pe.wait_ge(a_exp, per_g(4 * UNITS0, g) + 4 * i + j + 1)
            q0 = (b % 2) * SEQ + c * P
            for n, (q, kk) in enumerate(((qT_hi, k_hi), (qT_hi, k_lo), (qT_lo, k_hi))):
                mm = pe.matmul(bank_s[j % 2][:, 0:KVL0], q[:, s, q0:q0 + P], kk[:, b, :], start=n == 0, stop=n == 2)
            mm.then_inc(a_s, 1)

        def pe_pT(pe, g, i, chunks):
            for c in chunks:
                if c == 0:
                    pe.wait_ge(a_norm, per_g(4 * UNITS0, g) + 4 * i + 4)
                if c == 2:
                    pe.wait_ge(a_dup, per_g(UNITS0, g) + i + 1)
                    pe.wait_ge(a_acc, per_g(2 * UNITS0, g) + 2 * i + 2)
                for j in range(4):
                    mm = pe.transpose(bank_t[c][:, j * P:(j + 1) * P], probn[:, j, c * P:(c + 1) * P], ident[:, :])
                mm.then_inc(a_t, 1)

        def pe_pv(pe, g, i):
            b = i % 4
            pe.wait_ge(a_olo, per_g(UNITS0, g) + i + 1)
            if i == 0:
                pe.wait_ge(a_vlo, per_g(3, g) + 3)
            mms = []
            for c in range(2):
                v = TB * b + c
                mms += [(v_hi[:, v], pT_hi[:, c], c), (v_hi[:, v], pT_lo[:, c], c), (v_lo[:, v], pT_hi[:, c], c)]
            mms += [(v_hi[:, NT + b], pT_hi[:, 2], 2), (v_lo[:, NT + b], pT_hi[:, 2], 2)]
            for n, (v, p, c) in enumerate(mms):
                if n == 0 or mms[n - 1][2] != c:
                    pe.wait_ge(a_tlo, per_g(3 * UNITS0, g) + 3 * i + c + 1)
                mm = pe.matmul(bank_o[:, :], v, p, start=n == 0, stop=n == len(mms) - 1)
            mm.then_inc(a_pv, 1)

        def pe_wo(pe, g, i, c, last):
            par = (i // 4) % 2
            if c == 0:
                if i % 4 == 0:
                    pe.wait_ge(a_wo_lo, per_g(PAIRS0, g) + i // 4 + 1)
                pe.wait_ge(a_olo, per_g(UNITS0, g) + i + 2)
                pe.wait_ge(a_acc, per_g(2 * UNITS0, g) + 2 * i + 2)
                if i in (11, 12, 13) and not last:
                    pe.wait_ge(a_vTc, per_g(3, g) + 3 + i - 10)
            dst = bank_b if c == 0 else bank_t[2]
            for hh in range(2):
                q0 = hh * SEQ + c * P
                for n, (o, w) in enumerate(((oT_hi, wo_hi), (oT_hi, wo_lo), (oT_lo, wo_hi))):
                    mm = pe.matmul(dst[:, :], o[:, q0:q0 + P], w[:, par, hh, :], start=hh == 0 and n == 0,
                                   stop=hh == 1 and n == 2)
            mm.then_inc(a_wo, 1)

        def kv_rhs(n):
            if n < 2:
                return (lambda c: xT_hi[:, c, n * 512:(n + 1) * 512], lambda c: xT_lo[:, c, n * 512:(n + 1) * 512])
            return (lambda c: cT_hi[:, c, :], lambda c: cT_lo[:, c, :])

        KV_ORDER = (2, 0, 1)
        k_bank = (bank_b, bank_o, bank_a)
        v_bank = (bank_b, bank_a, bank_o)

        def pe_k(pe, n):
            project(pe, k_bank[n][:, :] if n < 2 else k_bank[n][:, 0:BATCH * CTX],
                    (lambda c: wkv_hi[:, 0, c, :], lambda c: wkv_lo[:, 0, c, :]), kv_rhs(n)).then_inc(a_k, 1)

        def pe_vT(pe, bank, n):
            project(pe, bank[:, :] if n < 2 else bank[:, 0:BATCH * CTX],
                    (lambda c: wkv_hi[:, 1, c, :], lambda c: wkv_lo[:, 1, c, :]), kv_rhs(n)).then_inc(a_vT, 1)

        def pe_v(pe, n):
            for q in range(4):
                mm = pe.transpose(v_bank[n][:, q * P:(q + 1) * P], vT[:, 4 * n + q, :], ident[:, :])
            mm.then_inc(a_v, 1)

        def pe_unit0(pe, g, i, last):
            ahead = not (last and i + 2 >= UNITS0)
            blk = not (last and i + QLEAD >= UNITS0)
            pe_pT(pe, g, i, (0, 1))
            if blk:
                if i == 14 and not last:
                    pe.wait_ge(a_klo, per_g(3, g) + 4)
                if i == 0:
                    pe.wait_ge(a_vlo, per_g(3, g) + 3)
                pe_q(pe, g, i + QLEAD, 0)
            pe_pT(pe, g, i, (2,))
            if blk:
                pe_q(pe, g, i + QLEAD, 1)
            if i == 14 and not last:
                pe.wait_ge(a_klo, per_g(3, g) + 6)
            pe_pv(pe, g, i)
            if last and i >= 14:
                if i == 14:
                    pe.wait_ge(a_exp, 4 * KV0 * UNITS0 + 2)
                else:
                    pe.wait_ge(l_lo, NT + 2)
                pe_ln(pe, 1, i - 14, ln1_banks)
            if blk:
                pe_q(pe, g, i + QLEAD, 2)
            if ahead:
                pe_scores(pe, g, i + 2, 0)
                pe_scores(pe, g, i + 2, 1)
            pe_wo(pe, g, i, 0, last)
            if ahead:
                pe_scores(pe, g, i + 2, 2)
                pe_scores(pe, g, i + 2, 3)
            pe_wo(pe, g, i, 1, last)
            if not last:
                if i in (10, 11, 12):
                    if i == 10:
                        pe.wait_ge(a_wkv_lo, g + 2)
                    pe.wait_ge(a_acc, per_g(2 * UNITS0, g) + 2 * i + 3)
                    pe_vT(pe, bank_b, i - 10)
                if i == 13:
                    pe.wait_ge(a_qlo, per_g(UNITS0, g) + i + QLEAD + 1)
                    pe_k(pe, 2)
                    pe.wait_ge(a_acc, per_g(2 * UNITS0, g) + 2 * i + 3)
                    pe_k(pe, 0)
                    pe_k(pe, 1)
                if i == 15:
                    pe_v(pe, 2)
                    pe.wait_ge(a_acc, per_g(2 * UNITS0, g) + 2 * i + 3)
                    pe_v(pe, 0)
                    pe.wait_ge(a_qlo, per_g(UNITS0, g) + i + QLEAD + 1)
                    pe_v(pe, 1)

        def pe_attn0(pe):
            pe.wait_ge(a_wkv_lo, 1)
            pe.wait_ge(s_clo, 1)
            for n in KV_ORDER:
                if n < 2:
                    pe.wait_ge(l_lo, NT * (n + 1) // 2)
                pe_k(pe, n)
            for step, n in enumerate(KV_ORDER):
                pe.wait_ge(a_klo, step + 1)
                pe_vT(pe, k_bank[n], n)
            pe.wait_ge(a_vTc, 1)
            for part in range(3):
                pe_q(pe, 0, 0, part)
            pe.wait_ge(a_vTc, 3)
            pe_v(pe, 2)
            pe_v(pe, 0)
            for blk in (1, 2):
                for part in range(3):
                    pe_q(pe, 0, blk, part)
                pe_scores(pe, 0, 0, 2 * blk - 2)
                pe_scores(pe, 0, 0, 2 * blk - 1)
            pe_scores(pe, 0, 1, 0)
            pe_scores(pe, 0, 1, 1)
            pe.wait_ge(a_qlo, QLEAD)
            pe_v(pe, 1)
            pe_scores(pe, 0, 1, 2)
            pe_scores(pe, 0, 1, 3)
            with pe.Fori(0, KV0 - 1) as g:
                for i in range(UNITS0):
                    pe_unit0(pe, g, i, False)
            for i in range(UNITS0):
                pe_unit0(pe, KV0 - 1, i, True)

        def split_hi(ac, dst, src, done):
            ac.activation(dst, src, ACT.Copy).then_inc(done, 1)

        def ac_wq(ac, g, pair):
            n = 2 * pair
            chunk_wait(ac, n, 2 * PAIRS0, g)
            if pair >= 2:
                ac.wait_ge(a_q, per_g(UNITS0, g) + 4 * (pair - 1))
            split_hi(ac, wq_hi[:, pair % 2], stage[:, n % RING, :].rearrange("p (c n) -> p c n", c=KC), a_wq_hi)

        def ac_wo(ac, g, pair):
            n = 2 * pair + 1
            chunk_wait(ac, n, 2 * PAIRS0, g)
            if pair >= 1:
                ac.wait_ge(a_wo, per_g(2 * UNITS0, g) + 8 * (pair - 1) + 1)
            split_hi(ac, wo_hi[:, pair % 2], stage[:, n % RING, :].rearrange("p (h n) -> p h n", h=2), a_wo_hi)

        def ac_exp(ac, g, i, j):
            ac.wait_ge(a_max, per_g(4 * UNITS0, g) + 4 * i + j + 1)
            ac.wait_ge(a_norm, per_g(4 * UNITS0, g) + 4 * i)
            ac.wait_ge(a_dup, per_g(UNITS0, g) + i)
            ac.activation(prob[:, j, :], bank_s[j % 2][:, 0:KVL0], ACT.Exp, bias=nmax[:, j:j + 1],
                          accum_out=rsum[:, j:j + 1]).then_inc(a_exp, 1)

        def ac_q(ac, g, blk):
            ac.wait_ge(a_q, per_g(UNITS0, g) + blk + 1)
            ac.activation(qT_hi[:, blk % 4, :], bank_a[:, :], ACT.Copy, scale=SCALE).then_inc(a_qhi, 1)

        def k_dst(t, n):
            if n < 2:
                return t[:, 2 * n:2 * n + 2, 0:SEQ]
            return t[:, :, SEQ:KVL0]

        def k_src(n):
            if n < 2:
                return k_bank[n][:, :].rearrange("p (b n) -> p b n", b=2)
            return k_bank[n][:, 0:BATCH * CTX].rearrange("p (b n) -> p b n", b=BATCH)

        def ac_k(ac, g, step):
            n = KV_ORDER[step]
            ac.wait_ge(a_k, per_g(3, g) + step + 1)
            ac.activation(k_dst(k_hi, n), k_src(n), ACT.Copy).then_inc(a_khi, 1)

        def ac_vT(ac, g, step, bank, n):
            ac.wait_ge(a_vT, per_g(3, g) + step + 1)
            if n < 2:
                ac.activation(vT[:, 4 * n:4 * n + 4, :], bank[:, :].rearrange("p (t n) -> p t n", t=4),
                              ACT.Copy).then_inc(a_vTc, 1)
            else:
                src = bank[:, 0:BATCH * CTX].rearrange("p (b r n) -> p b r n", b=BATCH, r=1)
                ac.activation(vT[:, NT:NT + BATCH, :].rearrange("p b (r n) -> p b r n", r=2),
                              src.broadcast_to([P, BATCH, 2, CTX]), ACT.Copy).then_inc(a_vTc, 1)

        def v_src(n):
            return v_bank[n][:, :].rearrange("p (t n) -> p t n", t=4)

        def ac_v(ac, g, step):
            n = KV_ORDER[step]
            ac.wait_ge(a_v, per_g(3, g) + step + 1)
            ac.activation(v_hi[:, 4 * n:4 * n + 4, :], v_src(n), ACT.Copy).then_inc(a_vhi, 1)

        def ac_wkv(ac, k, dst, done):
            ac.wait_ge(s_kvst, 32 * k + 32)
            split_hi(ac, dst[:, :, :, :], kv_stage[:, :, :, :], done)

        def ac_unit0(ac, g, i, last):
            ahead = not (last and i + 2 >= UNITS0)
            blk = not (last and i + QLEAD >= UNITS0)
            p = i // 4
            for c in range(NCH0):
                ac.wait_ge(a_t, per_g(3 * UNITS0, g) + 3 * i + c + 1)
                ac.activation(pT_hi[:, c, :], bank_t[c][:, :], ACT.Copy).then_inc(a_thi, 1)
                if c == 2 and i % 4 == 1 and not (last and p + 1 >= PAIRS0):
                    ac_wo(ac, g, p + 1)
                if c == 2 and i % 4 == 2 and not (last and p + 2 >= PAIRS0):
                    ac_wq(ac, g, p + 2)
                if c == 2 and i == 4 and not last:
                    ac.wait_ge(a_k, per_g(3, g) + 3)
                    ac.wait_ge(a_vT, per_g(3, g) + 3)
                    ac_wkv(ac, g + 1, wkv_hi, a_wkv_hi)
            ac.wait_ge(a_pv, per_g(UNITS0, g) + i + 1)
            ac.activation(oT_hi[:, :], bank_o[:, :], ACT.Copy).then_inc(a_ohi, 1)
            if last and i == 13:
                ac.wait_ge(a_q, KV0 * UNITS0)
                ac_gu(ac, 0, 0, 0, 0, 0)
            if last and i >= 14:
                ac_ln(ac, 1, i - 14, ln1_banks)
                if i == 14:
                    ac_gu(ac, 0, 1, 1, 0, 0)
            if blk:
                ac_q(ac, g, i + QLEAD)
            if ahead:
                for j in range(4):
                    ac_exp(ac, g, i + 2, j)
            if not last:
                if i in (10, 11, 12):
                    ac_vT(ac, g + 1, i - 10, bank_b, i - 10)
                if i == 13:
                    for step in range(3):
                        ac_k(ac, g + 1, step)
                if i == 15:
                    for step in range(3):
                        ac_v(ac, g + 1, step)

        def ac_attn0(ac):
            for step in range(3):
                ac_k(ac, 0, step)
            for step, n in enumerate(KV_ORDER):
                ac_vT(ac, 0, step, k_bank[n], n)
            ac_q(ac, 0, 0)
            ac_v(ac, 0, 0)
            ac_v(ac, 0, 1)
            for blk in (1, 2):
                ac_q(ac, 0, blk)
                ac_exp(ac, 0, 0, 2 * blk - 2)
                ac_exp(ac, 0, 0, 2 * blk - 1)
            ac_exp(ac, 0, 1, 0)
            ac_exp(ac, 0, 1, 1)
            ac_v(ac, 0, 2)
            ac_exp(ac, 0, 1, 2)
            ac_exp(ac, 0, 1, 3)
            with ac.Fori(0, KV0 - 1) as g:
                for i in range(UNITS0):
                    ac_unit0(ac, g, i, False)
            for i in range(UNITS0):
                ac_unit0(ac, KV0 - 1, i, True)

        def ve_max(ve, g, i, j):
            ve.wait_ge(a_s, per_g(4 * UNITS0, g) + 4 * i + j + 1)
            ve.tensor_reduce(nmax[:, j:j + 1], bank_s[j % 2][:, 0:KVL0], AX_X, ALU.max, negate=True).then_inc(a_max, 1)

        def ve_norm(ve, g, i, first=False):
            ve.wait_ge(a_exp, per_g(4 * UNITS0, g) + 4 * i + 4 + 2)
            ve.wait_ge(a_dup, per_g(UNITS0, g) + i)
            ve.reciprocal(rinv[:, :], rsum[:, :]).then_inc(a_rec, 1)
            ve.wait_ge(a_rec, per_g(UNITS0, g) + i + 1)
            if not first:
                ve.wait_ge(a_t, per_g(3 * UNITS0, g) + 3 * i - 1)
            for j in range(4):
                ve.tensor_scalar(probn[:, j, 0:SEQ], prob[:, j, 0:SEQ], rinv[:, j:j + 1], None,
                                 ALU.mult).then_inc(a_norm, 1)

        def ve_q(ve, g, blk):
            ve.wait_ge(a_qhi, per_g(UNITS0, g) + blk + 1)
            ve.scalar_tensor_tensor(out=qT_lo[:, blk % 4, :], in0=bank_a[:, :], scalar=SCALE,
                                    in1=f32(qT_hi[:, blk % 4, :]), op0=ALU.mult, op1=ALU.subtract).then_inc(a_qlo, 1)

        def ve_k(ve, g, step):
            n = KV_ORDER[step]
            ve.wait_ge(a_khi, per_g(3, g) + step + 1)
            ve.tensor_tensor(k_dst(k_lo, n), k_src(n), f32(k_dst(k_hi, n)), ALU.subtract).then_inc(a_klo, 1)

        def ve_v(ve, g, step):
            n = KV_ORDER[step]
            ve.wait_ge(a_vhi, per_g(3, g) + step + 1)
            ve.tensor_tensor(v_lo[:, 4 * n:4 * n + 4, :], v_src(n), f32(v_hi[:, 4 * n:4 * n + 4, :]),
                             ALU.subtract).then_inc(a_vlo, 1)

        def ve_add0(ve, g, i, c):
            t = TB * (i % 4) + c
            ve.wait_ge(a_wo, per_g(2 * UNITS0, g) + 2 * i + c + 1)
            ve.scalar_tensor_tensor(out=x_sb[:, t, :], in0=(bank_b, bank_t[2])[c][:, :], scalar=tg[:, 0:1],
                                    in1=x_sb[:, t, :], op0=ALU.mult, op1=ALU.add).then_inc(a_acc, 1)

        def ve_pT(ve, g, i, c):
            ve.wait_ge(a_thi, per_g(3 * UNITS0, g) + 3 * i + c + 1)
            if c < 2:
                ve.tensor_tensor(pT_lo[:, c, :], bank_t[c][:, :], f32(pT_hi[:, c, :]), ALU.subtract).then_inc(a_tlo, 1)
            else:
                ve.tensor_tensor(pT_hi[CTX:P, c, :], bank_t[c][CTX:P, :], f32(pT_hi[CTX:P, c, :]),
                                 ALU.subtract).then_inc(a_tlo, 1)

        def ve_unit0(ve, g, i, last):
            ahead = not (last and i + 2 >= UNITS0)
            blk = not (last and i + QLEAD >= UNITS0)
            ve_pT(ve, g, i, 0)
            ve_pT(ve, g, i, 1)
            ve_pT(ve, g, i, 2)
            if not (last and i == UNITS0 - 1):
                ve_norm(ve, g, i + 1)
            if last and i >= 14:
                ve_ln_norm(ve, 1, i - 14)
            ve.wait_ge(a_ohi, per_g(UNITS0, g) + i + 1)
            ve.tensor_tensor(oT_lo[:, :], bank_o[:, :], f32(oT_hi[:, :]), ALU.subtract).then_inc(a_olo, 1)
            if last and i >= 14:
                ve_ln_lo(ve, 1, i - 14, ln1_banks)
            if ahead:
                ve_max(ve, g, i + 2, 0)
                ve_max(ve, g, i + 2, 1)
            if blk:
                ve_q(ve, g, i + QLEAD)
            ve_add0(ve, g, i, 0)
            if ahead:
                ve_max(ve, g, i + 2, 2)
                ve_max(ve, g, i + 2, 3)
            ve_add0(ve, g, i, 1)
            if last and i in (13, 14):
                ve_ln_stats(ve, 1, i - 13, lambda t: x_after[1](ve, t))
            if not last:
                if i == 13:
                    for step in range(3):
                        ve_k(ve, g + 1, step)
                if i == 15:
                    for step in range(3):
                        ve_v(ve, g + 1, step)

        def ve_attn0(ve):
            for step in range(3):
                ve_k(ve, 0, step)
            ve_q(ve, 0, 0)
            ve_v(ve, 0, 0)
            ve_v(ve, 0, 1)
            for blk in (1, 2):
                ve_q(ve, 0, blk)
                ve_max(ve, 0, 0, 2 * blk - 2)
                ve_max(ve, 0, 0, 2 * blk - 1)
            ve_norm(ve, 0, 0, first=True)
            ve_max(ve, 0, 1, 0)
            ve_max(ve, 0, 1, 1)
            ve_v(ve, 0, 2)
            ve_max(ve, 0, 1, 2)
            ve_max(ve, 0, 1, 3)
            with ve.Fori(0, KV0 - 1) as g:
                for i in range(UNITS0):
                    ve_unit0(ve, g, i, False)
            for i in range(UNITS0):
                ve_unit0(ve, KV0 - 1, i, True)

        def split_lo(po, dst, src, hi, done):
            po.tensor_tensor(dst, src, f32(hi), ALU.subtract).then_inc(done, 1)

        def po_wq(po, g, pair):
            po.wait_ge(a_wq_hi, per_g(PAIRS0, g) + pair + 1)
            split_lo(po, wq_lo[:, pair % 2], stage[:, 2 * pair % RING, :].rearrange("p (c n) -> p c n", c=KC),
                     wq_hi[:, pair % 2], a_wq_lo)

        def po_wo(po, g, pair):
            po.wait_ge(a_wo_hi, per_g(PAIRS0, g) + pair + 1)
            split_lo(po, wo_lo[:, pair % 2], stage[:, (2 * pair + 1) % RING, :].rearrange("p (h n) -> p h n", h=2),
                     wo_hi[:, pair % 2], a_wo_lo)

        def po_wkv(po, hi, lo, hi_done, lo_done, n):
            po.wait_ge(hi_done, n)
            split_lo(po, lo[:, :, :, :], kv_stage[:, :, :, :], hi[:, :, :, :], lo_done)

        def po_dup(po, g, i):
            po.wait_ge(a_t, per_g(3 * UNITS0, g) + 3 * i)
            po.wait_ge(a_rec, per_g(UNITS0, g) + i + 1)
            src = prob[:, :, SEQ:KVL0].rearrange("p j (r n) -> p j r n", r=1).broadcast_to([P, 4, 2, CTX])
            r = rinv[:, :].rearrange("p (j r n) -> p j r n", r=1, n=1).broadcast_to([P, 4, 2, CTX])
            po.tensor_tensor(probn[:, :, SEQ:NCH0 * P].rearrange("p j (r n) -> p j r n", r=2), src, r,
                             ALU.mult).then_inc(a_dup, 1)

        def po_unit0(po, g, i, last):
            if not (last and i == UNITS0 - 1):
                po_dup(po, g, i + 1)
            if last and i >= 14:
                po_ln(po, 1, i - 14)
                po_gu(po, i - 14, i - 14)
            p = i // 4
            if i % 4 == 1 and not (last and p + 1 >= PAIRS0):
                po_wo(po, g, p + 1)
            if i % 4 == 2 and not (last and p + 2 >= PAIRS0):
                po_wq(po, g, p + 2)
            if not last and i == 4:
                po_wkv(po, wkv_hi, wkv_lo, a_wkv_hi, a_wkv_lo, g + 2)

        def po_attn0(po):
            po_dup(po, 0, 0)
            with po.Fori(0, KV0 - 1) as g:
                for i in range(UNITS0):
                    po_unit0(po, g, i, False)
            for i in range(UNITS0):
                po_unit0(po, KV0 - 1, i, True)

        def steps(eng, nf, step):
            for half in range(2):
                first, end = half * nf, (half + 1) * nf
                for m in range(first, first + 3):
                    step(m, m, 0, 0)
                rounds = (min(end - 2, 2 * nf - 4) - first - 2) // 2
                with eng.Fori(0, rounds) as it:
                    for s in range(3, 5):
                        step(it * 2 + (first + s), first + s, it, RING)
                for m in range(first + 2 * rounds + 3, end):
                    step(m, m, 0, 0)

        def ffn_ln(n, ms):
            for k, b, at in [(2 * n + 1, 2, 0)] + [(2, 0, NFS[0])] * (n == 0):
                if at <= ms <= at + 2:
                    return ([(k, b), (k, b + 1)] if ms == at else []), ((k, b + ms - at - 1) if ms > at else None)
            return [], None

        def pe_gu(pe, n, m, ms):
            t, s = ffn_t[n], F[n]
            par, half = ms % 2, ms // NFS[n]
            pe.wait_ge(s["gu_lo" if n == 0 else "gu_hi"], m + 1)
            pe.wait_ge(s["h"], m + 1)
            for w, banks, done in ((0, ffn_g, s["gate"]), (1, ffn_u, s["up"])):
                def part(name):
                    return (lambda c: t[name][:, par, w, c, :]) if name in t else None
                project(pe, banks[par][:, :], (part("gu_hi"), part("gu_lo")),
                        (lambda c: xT_hi[:, c, half * 512:(half + 1) * 512],
                         lambda c: xT_lo[:, c, half * 512:(half + 1) * 512])).then_inc(done, 1)

        def pe_down(pe, n, m, ms):
            nf, t, s = NFS[n], ffn_t[n], F[n]
            par, f, half = ms % 2, ms % nf, ms // nf
            pe.wait_ge(s["h_lo"], m + 1)
            pe.wait_ge(s["wd_lo" if n == 0 else "wd_hi"], m + 1)
            passes = [("h_hi", "wd_hi"), ("h_lo", "wd_hi")] + ([("h_hi", "wd_lo")] if n == 0 else [])
            for q in range(4):
                if f == 0 and half == 1:
                    pe.wait_ge(s["x"], q + 1)
                for k, (h, w) in enumerate(passes):
                    mm = pe.matmul(ffn_acc[q][:, :], t[h][:, par, q * P:(q + 1) * P], t[w][:, par, :],
                                   start=f == 0 and k == 0, stop=f == nf - 1 and k == len(passes) - 1)
                if f == nf - 1:
                    mm.then_inc(s["acc"], 1)
            if f != nf - 1:
                mm.then_inc(s["down"], 1)

        def pe_ffn(pe, n, x_done):
            k = 2 * n + 1
            pe.wait_ge(l_lo, NT * k + NT // 2)
            pe_gu(pe, n, 0, 0)

            def step(m, ms, it, per):
                _, finish = ffn_ln(n, ms)
                if ms + 1 < 2 * NFS[n]:
                    pe_gu(pe, n, m + 1, ms + 1)
                if finish:
                    pe.wait_ge(F[n]["h_lo"], m + 1)
                    pe_ln(pe, *finish, (ffn_g[ms % 2], ffn_u[ms % 2]))
                if ms == 0:
                    x_done(pe)
                pe_down(pe, n, m, ms)
                if finish:
                    pe.wait_ge(l_lo, NT * finish[0] + 2 * finish[1] + 2)
            steps(pe, NFS[n], step)

        def ac_gu(ac, n, m, ms, it, per):
            t, s = ffn_t[n], F[n]
            k = ffn_at[n]["gu", ms]
            chunk_wait(ac, k, per, it)
            if ms >= 2:
                ac.wait_ge(s["up"], m - 1)
            ac.activation(t["gu_hi"][:, ms % 2], gu_view(slot(k) if n == 0 else slot16(k)),
                          ACT.Copy).then_inc(s["gu_hi"], 1)

        def ac_wd(ac, n, m, ms, it, per):
            nf, t, s = NFS[n], ffn_t[n], F[n]
            k = ffn_at[n]["wd", ms]
            chunk_wait(ac, k, per, it)
            if ms >= 2:
                half, f = divmod(ms - 2, nf)
                if f == nf - 1:
                    ac.wait_ge(s["acc"], 4 * (half + 1))
                else:
                    ac.wait_ge(s["down"], m - 1 - half)
            ac.activation(t["wd_hi"][:, ms % 2, :], (slot(k) if n == 0 else slot16(k))[:, 0:DM],
                          ACT.Copy).then_inc(s["wd_hi"], 1)

        def ac_silu(ac, n, m, ms):
            t, s = ffn_t[n], F[n]
            half = ms // NFS[n]
            ac.wait_ge(s["gate"], m + 1)
            scale = ag_sb[:, bass.ds(m - half * NFS[n], 1)] if n == 0 else 1.0
            ac.activation(t["s"][:, ms % 2, :], ffn_g[ms % 2][:, :], ACT.Silu, scale=scale).then_inc(s["silu"], 1)
            ac.wait_ge(s["h"], m + 3)
            ac.activation(t["h_hi"][:, ms % 2, :], t["h"][:, ms % 2, :], ACT.Copy).then_inc(s["h_hi"], 1)

        def ac_ffn(ac, n, x_done):
            total = 2 * NFS[n]
            x_done(ac)
            ac_wd(ac, n, 0, 0, 0, 0)
            ac_silu(ac, n, 0, 0)
            ac_gu(ac, n, 2, 2, 0, 0)
            ac_wd(ac, n, 1, 1, 0, 0)

            def step(m, ms, it, per):
                _, finish = ffn_ln(n, ms)
                if finish:
                    ac_ln(ac, *finish, (ffn_g[ms % 2], ffn_u[ms % 2]))
                if ms + 1 < total:
                    ac_silu(ac, n, m + 1, ms + 1)
                if ms + 3 < total:
                    ac_gu(ac, n, m + 3, ms + 3, it, per)
                if ms + 2 < total:
                    ac_wd(ac, n, m + 2, ms + 2, it, per)
            steps(ac, NFS[n], step)

        def ve_h(ve, n, m, ms):
            t, s = ffn_t[n], F[n]
            half, par = ms // NFS[n], ms % 2
            ve.wait_ge(s["up"], m + 1)
            ve.wait_ge(s["silu"], m + 1)
            if n == 0:
                ve.scalar_tensor_tensor(out=t["h"][:, par, :], in0=ffn_u[par][:, :],
                                        scalar=au_sb[:, bass.ds(m - half * NFS[n], 1)], in1=t["s"][:, par, :],
                                        op0=ALU.mult, op1=ALU.mult).then_inc(s["h"], 1)
            else:
                ve.tensor_tensor(t["h"][:, par, :], ffn_u[par][:, :], t["s"][:, par, :], ALU.mult).then_inc(s["h"], 1)
            ve.wait_ge(s["h_hi"], m + 1)
            ve.tensor_tensor(t["h_lo"][:, par, :], t["h"][:, par, :], f32(t["h_hi"][:, par, :]),
                             ALU.subtract).then_inc(s["h_lo"], 1)

        def ve_ffn_x(ve, n, half):
            t, s = ffn_t[n], F[n]
            for q in range(4):
                tile = 4 * half + q
                ve.wait_ge(s["acc"], tile + 1)
                if n == 0:
                    if tile >= 2:
                        ve.wait_ge(s["x"], tile - 1)
                    ve.tensor_tensor(t["scaled"][:, q % 2, :], ffn_acc[q][:, :], tgad[:, :],
                                     ALU.mult).then_inc(s["scaled"], 1)
                    ve.wait_ge(s["scaled"], tile + 1)
                    ve.tensor_tensor(x_sb[:, tile, :], x_sb[:, tile, :], t["scaled"][:, q % 2, :],
                                     ALU.add).then_inc(s["x"], 1)
                else:
                    ve.scalar_tensor_tensor(out=x_sb[:, tile, :], in0=ffn_acc[q][:, :], scalar=tg[:, 3:4],
                                            in1=x_sb[:, tile, :], op0=ALU.mult, op1=ALU.add).then_inc(s["x"], 1)

        def ve_ffn(ve, n):
            nf = NFS[n]
            ve_h(ve, n, 0, 0)

            def step(m, ms, it, per):
                begin, finish = ffn_ln(n, ms)
                if finish:
                    ve_ln_lo(ve, *finish, (ffn_g[ms % 2], ffn_u[ms % 2]))
                if ms + 1 < 2 * nf:
                    ve_h(ve, n, m + 1, ms + 1)
                for k, b in begin:
                    ve_ln_stats(ve, k, b, lambda t: x_after[k](ve, t))
                for k, b in begin:
                    ve_ln_norm(ve, k, b)
                if ms % nf == nf - 1:
                    ve_ffn_x(ve, n, ms // nf)
            steps(ve, nf, step)

        def po_gu(po, m, ms):
            t, s = ffn_t[0], F[0]
            po.wait_ge(s["gu_hi"], m + 1)
            split_lo(po, t["gu_lo"][:, ms % 2], gu_view(slot(ffn_at[0]["gu", ms])), t["gu_hi"][:, ms % 2], s["gu_lo"])

        def po_wd(po, m, ms):
            t, s = ffn_t[0], F[0]
            po.wait_ge(s["wd_hi"], m + 1)
            split_lo(po, t["wd_lo"][:, ms % 2, :], slot(ffn_at[0]["wd", ms])[:, 0:DM], t["wd_hi"][:, ms % 2, :],
                     s["wd_lo"])

        def po_ffn(po, n):
            total = 2 * NFS[n]
            if n == 0:
                po_wd(po, 0, 0)
                po_gu(po, 2, 2)
                po_wd(po, 1, 1)

            def step(m, ms, it, per):
                if n == 0 and ms + 3 < total:
                    po_gu(po, m + 3, ms + 3)
                if n == 0 and ms + 2 < total:
                    po_wd(po, m + 2, ms + 2)
                begin, _ = ffn_ln(n, ms)
                for k, b in begin:
                    po_ln(po, k, b)
            if n == 0:
                steps(po, NFS[n], step)
            else:
                step(0, 0, 0, 0)

        UNITS1 = BATCH

        def place1(h, i):
            return h ^ (i % 2)

        def pe_q1(pe, j, i, part):
            b = i % UNITS1
            if b == 0:
                pe.wait_ge(b_wq_lo, (j + i // UNITS1) * 2 + part + 1)
            for hh in range(2):
                mm = project(pe, (bank_a, bank_b)[part][:, hh * SEQ:(hh + 1) * SEQ],
                             (lambda k: wq1_hi[:, part, k, hh * HD:(hh + 1) * HD],
                              lambda k: wq1_lo[:, part, k, hh * HD:(hh + 1) * HD]),
                             (lambda k: xT_hi[:, k, b * SEQ:(b + 1) * SEQ], lambda k: xT_lo[:, k, b * SEQ:(b + 1) * SEQ]))
            mm.then_inc(b_q, 1)

        def pe_s1(pe, j, i, part, first=False):
            if part == 0:
                if not first:
                    pe.wait_ge(b_add, j * UNITS1 + i)
                if i % UNITS1 == 0:
                    pe.wait_ge(b_klo, j + i // UNITS1 + 1)
            pe.wait_ge(b_qlo, j * (2 * UNITS1) + 2 * i + part + 1)
            for h in (2 * part, 2 * part + 1):
                for c in range(TB):
                    at = place1(h, i) * 2 * CTX
                    for n, q in enumerate((q1T_hi, q1T_lo)):
                        mm = pe.matmul(bank_ss[:, c, at:at + 2 * CTX], q[:, h, c * P:(c + 1) * P],
                                       k1[:, i % UNITS1].rearrange("p r n -> p (r n)"), start=n == 0, stop=n == 1)
            if part == 1:
                mm.then_inc(b_s, 1)

        def pe_sqT(pe, j, i, part):
            pe.wait_ge(b_qsq, j * (2 * UNITS1) + 2 * i + part + 1)
            for c in range(TB):
                for h in (2 * part, 2 * part + 1):
                    at = (2 * c + place1(h, i) % 2) * P
                    mm = pe.transpose(kv1_bank[:, at:at + P], q_sq[:, h, c * P:(c + 1) * P], ident[:, :])
            mm.then_inc(b_sqT, 1)

        def pe_p1T(pe, j, i):
            pe.wait_ge(b_norm, j * UNITS1 + i + 1)
            for hp in range(2):
                for c in range(TB):
                    at = c * GH1 + 2 * hp
                    mm = pe.transpose(t1_bank[:, (hp * TB + c) * P:(hp * TB + c + 1) * P],
                                      prob1n[:, at:at + 2, :].rearrange("p a n -> p (a n)"), ident[:, :])
            mm.then_inc(b_t, 1)

        def pe_vw(pe, j, n, h, first=False):
            if n % 2 == 0 and h % 2 == 0:
                if h == 0:
                    pe.wait_ge(b_vlo, (j + n // 2) * 2 + 2)
                pe.wait_ge(b_wo_lo, (j + n // 2) * 2 + h // 2 + 1)
            if not first:
                pe.wait_ge(b_wlo, (j + 1) * 16 + (n - 2) * 8 + 2 * h)
            at = (h % 2) * CTX
            v = [t[:, n % 2].rearrange("p r n -> p (r n)")[:, at:at + 2 * CTX] for t in (v1_hi, v1_lo)]
            for k, (a, w) in enumerate(((v[0], wo1_hi), (v[0], wo1_lo), (v[1], wo1_hi))):
                mm = pe.matmul(w1_bank[:, :], a, w[:, h, :], start=k == 0, stop=k == 2)
            mm.then_inc(b_w, 1)

        def pe_o1(pe, j, i, c):
            if c == 0:
                pe.wait_ge(b_tlo, j * UNITS1 + i + 1)
                if i % 2 == 0:
                    pe.wait_ge(b_wlo, j * 16 + (i // 2) * 8 + 8)
            pe.wait_ge(b_acc, j * (2 * UNITS1) + 2 * i + c + 1)
            for hp in range(2):
                for k, (p, w) in enumerate(((p1T_hi, vw_hi), (p1T_hi, vw_lo), (p1T_lo, vw_hi))):
                    mm = pe.matmul(o1_bank[:, :], p[:, hp, c * P:(c + 1) * P], w[:, i // 2 % 2, i % 2, hp, :],
                                   start=hp == 0 and k == 0, stop=hp == 1 and k == 2)
            mm.then_inc(b_o, 1)

        def pe_krow(pe, g, first=False):
            pe.wait_ge(b_wkv_lo, g + 1)
            if not first:
                pe.wait_ge(b_klo, g)
            for c in range(2):
                mm = project(pe, kv1_bank[:, c * HD:(c + 1) * HD],
                             (lambda k: cT_hi[:, k, c * P:(c + 1) * P], lambda k: cT_lo[:, k, c * P:(c + 1) * P]),
                             (lambda k: wkv1_hi[:, 0, k, :], lambda k: wkv1_lo[:, 0, k, :]))
            mm.then_inc(b_kr, 1)

        def pe_v1(pe, g):
            pe.wait_ge(b_krs, g + 1)
            project(pe, kv1_bank[:, 0:BATCH * CTX],
                    (lambda k: wkv1_hi[:, 1, k, :], lambda k: wkv1_lo[:, 1, k, :]),
                    (lambda k: cT_hi[:, k, :], lambda k: cT_lo[:, k, :])).then_inc(b_v, 1)

        def pe_kT(pe, g):
            pe.wait_ge(b_kn, g + 1)
            pe.wait_ge(b_vlo, g * 2 + 2)
            for c in range(2):
                mm = pe.transpose(kv1_bank[:, c * P:(c + 1) * P], k_row[:, c, :], ident[:, :])
            mm.then_inc(b_kT, 1)

        def pe_unit1(pe, j, i, last):
            next1, next2 = not (last and i + 1 >= UNITS1), not (last and i + 2 >= UNITS1)
            pe_p1T(pe, j, i)
            if next1:
                pe_s1(pe, j, i + 1, 0)
                if i == 2 and not last:
                    pe.wait_ge(b_vlo, (j + 2) * 2)
                pe.wait_ge(b_ss, j * (2 * UNITS1) + 2 * i + 3)
                pe_sqT(pe, j, i + 1, 1)
                pe_s1(pe, j, i + 1, 1)
            if next2:
                pe_vw(pe, j, i // 2 + 1, i % 2 * 2)
            pe_o1(pe, j, i, 0)
            if last and i >= 2:
                if i == 3:
                    pe.wait_ge(l_lo, 3 * NT + 2)
                pe_ln(pe, 3, i - 2, ln3_banks)
            if i in (1, 2) and not last:
                pe.wait_ge(b_ss, j * (2 * UNITS1) + 2 * i + 4)
                (pe_krow, pe_kT)[i - 1](pe, j + 1)
            if next2:
                pe_q1(pe, j, i + 2, 0)
            pe_o1(pe, j, i, 1)
            if next2:
                pe_vw(pe, j, i // 2 + 1, i % 2 * 2 + 1)
                pe.wait_ge(b_ss, j * (2 * UNITS1) + 2 * i + 4)
                if i == 1 and not last:
                    pe.wait_ge(b_krs, j + 2)
                if i == 2:
                    pe.wait_ge(b_klo, j + 2)
                pe_sqT(pe, j, i + 2, 0)
                pe_q1(pe, j, i + 2, 1)
            if i == 1 and not last:
                pe.wait_ge(b_ss, j * (2 * UNITS1) + 2 * i + 5)
                pe_v1(pe, j + 1)

        def pe_attn1(pe):
            pe.wait_ge(F[0]["h"], 2 * NF0 + 2)
            pe_krow(pe, 0, first=True)
            pe_q1(pe, 0, 0, 0)
            pe.wait_ge(F[0]["x"], NT)
            pe_q1(pe, 0, 0, 1)
            pe_v1(pe, 0)
            pe_ln(pe, 2, 2, ln2_banks)
            pe_kT(pe, 0)
            pe_vw(pe, -1, 2, 0, first=True)
            pe_s1(pe, 0, 0, 0, first=True)
            pe_s1(pe, 0, 0, 1)
            pe_sqT(pe, 0, 0, 0)
            pe_vw(pe, -1, 2, 1)
            pe_q1(pe, 0, 1, 0)
            pe.wait_ge(b_ss, 1)
            pe_sqT(pe, 0, 0, 1)
            pe.wait_ge(l_lo, 2 * NT + 6)
            pe_ln(pe, 2, 3, ln2_banks)
            pe_vw(pe, -1, 2, 2)
            pe_q1(pe, 0, 1, 1)
            pe.wait_ge(b_ss, 2)
            pe_sqT(pe, 0, 1, 0)
            pe_vw(pe, -1, 2, 3)
            pe.wait_ge(l_lo, 3 * NT)
            with pe.Fori(0, KV1 - 1) as j:
                for i in range(UNITS1):
                    pe_unit1(pe, j, i, False)
            for i in range(UNITS1):
                pe_unit1(pe, KV1 - 1, i, True)

        def ac_q1(ac, j, i, part):
            src = (bank_a, bank_b)[part][:, :].rearrange("p (h n) -> p h n", h=2)
            ac.wait_ge(b_q, j * (2 * UNITS1) + 2 * i + part + 1)
            ac.activation(q_sq[:, 2 * part:2 * part + 2, :], src, ACT.Square).then_inc(b_qsq, 1)
            ac.activation(q1T_hi[:, 2 * part:2 * part + 2, :], src, ACT.Copy).then_inc(b_qhi, 1)

        def ac_p1T(ac, j, i):
            ac.wait_ge(b_t, j * UNITS1 + i + 1)
            ac.activation(p1T_hi[:, :, :], t1_bank[:, :].rearrange("p (h n) -> p h n", h=2), ACT.Copy).then_inc(b_thi, 1)

        def vw_halves(n, h):
            for half in range(2):
                rows = slice(half * CTX, (half + 1) * CTX)
                yield rows, (n % 2, half ^ (h % 2), h // 2)

        def ac_vw(ac, j, n, h):
            ac.wait_ge(b_w, (j + 1) * 8 + (n - 2) * 4 + h + 1)
            for rows, (a, b, c) in vw_halves(n, h):
                ac.activation(vw_hi[rows, a, b, c, :], w1_bank[rows, :], ACT.Copy).then_inc(b_whi, 1)

        def score_parts(r):
            return bank_ss[:, :, :].rearrange("p c (h r n) -> p c h r n", h=GH1, r=2)[:, :, :, r, :]

        def ac_cross(ac, j, i):
            ac.wait_ge(b_s, j * UNITS1 + i + 1)
            ac.activation(logit[:, :, :].rearrange("p (c h) n -> p c h n", c=TB), score_parts(1),
                          ACT.Copy).then_inc(b_cross, 1)

        def ac_exp1(ac, j, i):
            ac.wait_ge(b_sub, j * UNITS1 + i + 1)
            ac.activation(prob1[:, :, :], logit[:, :, :], ACT.Exp).then_inc(b_exp, 1)

        def v1_copies(t, src):
            s4 = src.rearrange("p (m b n) -> p m b n", m=2, b=2)
            return (t[:, :, 0:2, :], s4), (t[:, :, 2, :], s4[:, :, 0, :])

        def ac_kv1(ac, job, g):
            rows = kv1_bank[:, 0:2 * HD].rearrange("p (c n) -> p c n", c=2)
            if job == 0:
                ac.wait_ge(b_kr, g + 1)
                ac.activation(k_row[:, :, :], rows, ACT.Copy)
                ac.activation(k_sq[:, :, :], rows, ACT.Square).then_inc(b_krs, 1)
            elif job == 1:
                ac.wait_ge(b_v, g + 1)
                for dst, src in v1_copies(v1_hi, kv1_bank[:, 0:BATCH * CTX]):
                    ac.activation(dst, src, ACT.Copy).then_inc(b_vhi, 1)
            else:
                ac.wait_ge(b_kT, g + 1)
                ac.activation(k1[:, :, 0, :], kv1_bank[:, 0:BATCH * CTX].rearrange("p (b n) -> p b n", b=BATCH),
                              ACT.Identity, scale=kscale[:, 0:1]).then_inc(b_khi, 1)

        def l1_chunk(g, what, part):
            return l1_base + 4 * g + L1_CHUNKS[min(g, 1)].index((what, part))

        def ac_wq1(ac, j, n, part):
            k = l1_chunk(n, "wq", part)
            chunk_wait(ac, k, 4 if n else 0, j)
            if n:
                ac.wait_ge(b_q, j * (2 * UNITS1) + 2 * UNITS1 - 1 + part)
            split_hi(ac, wq1_hi[:, part], slot(k).rearrange("p (c n) -> p c n", c=KC), b_wq_hi)

        def ac_wo1(ac, j, n, part):
            k = l1_chunk(n, "wo", part)
            chunk_wait(ac, k, 4 if n else 0, j)
            if n:
                ac.wait_ge(b_w, j * 8 + 4 + 2 * part + 2)
            split_hi(ac, wo1_hi[:, 2 * part:2 * part + 2, :], slot(k).rearrange("p (h n) -> p h n", h=2), b_wo_hi)

        def ac_unit1(ac, j, i, last):
            next1, next2 = not (last and i + 1 >= UNITS1), not (last and i + 2 >= UNITS1)
            ac_p1T(ac, j, i)
            if next1:
                ac_cross(ac, j, i + 1)
            if last and i >= 2:
                ac_gu(ac, 1, i - 2, i - 2, 0, 0)
                ac_ln(ac, 3, i - 2, ln3_banks)
            if not last:
                if i == 0:
                    ac.wait_ge(b_v, j + 1)
                    ac_wkv(ac, j + (KV0 + 1), wkv1_hi, b_wkv_hi)
                if i == 1:
                    ac_wo1(ac, j, 1, 0)
                if i == 2:
                    ac_wq1(ac, j, 1, 1)
            if next2:
                ac_vw(ac, j, i // 2 + 1, i % 2 * 2)
                if i == 1 and not last:
                    ac_kv1(ac, 0, j + 1)
                if i == 2:
                    ac_kv1(ac, 2, j + 1)
                    ac_wo1(ac, j, 1, 1)
                ac_q1(ac, j, i + 2, 0)
            if next1:
                ac_exp1(ac, j, i + 1)
            if next2:
                ac_vw(ac, j, i // 2 + 1, i % 2 * 2 + 1)
            if i == 1 and not last:
                ac_wq1(ac, j, 1, 0)
            if next2:
                ac_q1(ac, j, i + 2, 1)
            if i == 1 and not last:
                ac_kv1(ac, 1, j + 1)

        def ac_attn1(ac):
            ac_wkv(ac, KV0, wkv1_hi, b_wkv_hi)
            ac_wq1(ac, 0, 0, 0)
            ac_wq1(ac, 0, 0, 1)
            ac_kv1(ac, 0, 0)
            ac_wo1(ac, 0, 0, 0)
            ac_wo1(ac, 0, 0, 1)
            ac.wait_ge(F[0]["x"], NT)
            ac_q1(ac, 0, 0, 0)
            ac_q1(ac, 0, 0, 1)
            ac_kv1(ac, 1, 0)
            ac_ln(ac, 2, 2, ln2_banks)
            ac_kv1(ac, 2, 0)
            ac_vw(ac, -1, 2, 0)
            ac_cross(ac, 0, 0)
            ac_vw(ac, -1, 2, 1)
            ac_q1(ac, 0, 1, 0)
            ac_ln(ac, 2, 3, ln2_banks)
            ac_vw(ac, -1, 2, 2)
            ac_q1(ac, 0, 1, 1)
            ac_exp1(ac, 0, 0)
            ac_vw(ac, -1, 2, 3)
            with ac.Fori(0, KV1 - 1) as j:
                for i in range(UNITS1):
                    ac_unit1(ac, j, i, False)
            for i in range(UNITS1):
                ac_unit1(ac, KV1 - 1, i, True)

        def wide(ap, n):
            a = ap.shape[1]
            return ap.rearrange("p (a n) -> p a n", n=1).broadcast_to([P, a, n])

        def ve_q1(ve, j, i, part):
            ve.wait_ge(b_qhi, j * (2 * UNITS1) + 2 * i + part + 1)
            ve.tensor_tensor(q1T_lo[:, 2 * part:2 * part + 2, :],
                             (bank_a, bank_b)[part][:, :].rearrange("p (h n) -> p h n", h=2),
                             f32(q1T_hi[:, 2 * part:2 * part + 2, :]), ALU.subtract).then_inc(b_qlo, 1)

        def ve_p1T(ve, j, i):
            ve.wait_ge(b_thi, j * UNITS1 + i + 1)
            ve.tensor_tensor(p1T_lo[:, :, :], t1_bank[:, :].rearrange("p (h n) -> p h n", h=2), f32(p1T_hi[:, :, :]),
                             ALU.subtract).then_inc(b_tlo, 1)

        def ve_ss(ve, j, i, part):
            n = j * (2 * UNITS1) + 2 * i + part + 1
            ve.wait_ge(b_sqT, n)
            ve.tensor_reduce(q_ss[:, :, 2 * part:2 * part + 2], kv1_bank[:, :].rearrange("p (c h n) -> p c h n", c=TB, h=2),
                             AX_X, ALU.add).then_inc(b_ss, 1)
            if part == 1:
                ve.wait_ge(b_ss, n)
                ve.tensor_scalar(q_var[:, :], q_ss[:, :, :].rearrange("p c h -> p (c h)"), 1.0 / HD, EPS, ALU.mult,
                                 ALU.add).then_inc(b_var, 1)

        def ve_log_add(ve, j, i):
            ve.wait_ge(b_cross, j * UNITS1 + i + 1)
            l4 = logit[:, :, :].rearrange("p (c h) n -> p c h n", c=TB)
            ve.tensor_tensor(l4, score_parts(0), l4, ALU.add).then_inc(b_add, 1)

        def ve_log_rms(ve, j, i):
            n = j * UNITS1 + i + 1
            ve.wait_ge(b_add, n)
            ve.wait_ge(b_rms, n)
            ve.tensor_tensor(logit[:, :, :], logit[:, :, :], wide(q_rms[:, :], CTX), ALU.mult).then_inc(b_log, 1)

        def ve_log_max(ve, j, i):
            n = j * UNITS1 + i + 1
            ve.wait_ge(b_mask, n)
            ve.tensor_reduce(mx1[:, :], logit[:, :, :], AX_X, ALU.max).then_inc(b_max, 1)

        def ve_log_sub(ve, j, i):
            ve.wait_ge(b_max, j * UNITS1 + i + 1)
            ve.tensor_tensor(logit[:, :, :], logit[:, :, :], wide(mx1[:, :], CTX), ALU.subtract).then_inc(b_sub, 1)

        def ve_rec1(ve, j, i):
            n = j * UNITS1 + i + 1
            ve.wait_ge(b_exp, n)
            ve.tensor_reduce(sum1[:, :], prob1[:, :, :], AX_X, ALU.add).then_inc(b_sum, 1)
            ve.wait_ge(b_sum, n)
            ve.reciprocal(rinv1[:, :], sum1[:, :]).then_inc(b_rec, 1)

        def ve_vw(ve, j, n, h):
            at = (j + 1) * 16 + (n - 2) * 8 + 2 * h
            for half, (rows, (a, b, c)) in enumerate(vw_halves(n, h)):
                ve.wait_ge(b_whi, at + half + 1)
                ve.tensor_tensor(vw_lo[rows, a, b, c, :], w1_bank[rows, :], f32(vw_hi[rows, a, b, c, :]),
                                 ALU.subtract).then_inc(b_wlo, 1)

        def ve_add1(ve, j, i, c):
            t = TB * i + c
            ve.wait_ge(b_o, j * (2 * UNITS1) + 2 * i + c + 1)
            ve.scalar_tensor_tensor(out=x_sb[:, t, :], in0=o1_bank[:, :], scalar=tg[:, 1:2],
                                    in1=x_sb[:, t, :], op0=ALU.mult, op1=ALU.add).then_inc(b_acc, 1)

        def ve_kv1(ve, job, g):
            if job == 0:
                ve.wait_ge(b_krs, g + 1)
                ve.tensor_reduce(k_ss[:, :], k_sq[:, :, :], AX_X, ALU.add).then_inc(b_kss, 1)
                ve.wait_ge(b_kss, g + 1)
                ve.tensor_scalar(k_var[:, :], k_ss[:, :], 1.0 / HD, EPS, ALU.mult, ALU.add).then_inc(b_kvar, 1)
            elif job == 1:
                ve.wait_ge(b_vhi, g * 2 + 2)
                for (dst, src), (hi, _) in zip(v1_copies(v1_lo, kv1_bank[:, 0:BATCH * CTX]),
                                               v1_copies(v1_hi, kv1_bank[:, 0:BATCH * CTX])):
                    ve.tensor_tensor(dst, src, f32(hi), ALU.subtract).then_inc(b_vlo, 1)
            else:
                ve.wait_ge(b_khi, g + 1)
                ve.scalar_tensor_tensor(out=k1[:, :, 1, :], in0=kv1_bank[:, 0:BATCH * CTX].rearrange("p (b n) -> p b n", b=BATCH),
                                        scalar=kscale[:, 0:1], in1=f32(k1[:, :, 0, :]), op0=ALU.mult,
                                        op1=ALU.subtract).then_inc(b_klo, 1)

        def ve_knorm(ve, g):
            ve.wait_ge(b_krms, g + 1)
            ve.tensor_tensor(k_row[:, :, :], k_row[:, :, :], wide(k_rms[:, :], HD), ALU.mult).then_inc(b_kn, 1)

        def ve_unit1(ve, j, i, last):
            next1, next2 = not (last and i + 1 >= UNITS1), not (last and i + 2 >= UNITS1)
            ve_p1T(ve, j, i)
            if last and i >= 2:
                ve_ln_norm(ve, 3, i - 2)
            if next1:
                ve_ss(ve, j, i + 1, 1)
                if i == 2 and not last:
                    ve_knorm(ve, j + 1)
                ve_log_add(ve, j, i + 1)
                ve_log_rms(ve, j, i + 1)
            ve_add1(ve, j, i, 0)
            if next2:
                ve_vw(ve, j, i // 2 + 1, i % 2 * 2)
            if last and i >= 2:
                ve_ln_lo(ve, 3, i - 2, ln3_banks)
            if i in (1, 2) and not last:
                ve_kv1(ve, 2 * i - 2, j + 1)
            if next1:
                ve_log_max(ve, j, i + 1)
                ve_log_sub(ve, j, i + 1)
            if next2:
                ve_q1(ve, j, i + 2, 0)
            if next1:
                ve_rec1(ve, j, i + 1)
            if next2:
                ve_ss(ve, j, i + 2, 0)
            ve_add1(ve, j, i, 1)
            if next2:
                ve_vw(ve, j, i // 2 + 1, i % 2 * 2 + 1)
            if last and i in (1, 2):
                ve_ln_stats(ve, 3, i - 1, lambda t: x_after[3](ve, t))
            if next2:
                ve_q1(ve, j, i + 2, 1)
            if i == 1 and not last:
                ve_kv1(ve, 1, j + 1)

        def ve_attn1(ve):
            ve_kv1(ve, 0, 0)
            ve_ln_stats(ve, 2, 2, lambda t: x_after[2](ve, t))
            ve_q1(ve, 0, 0, 0)
            ve_knorm(ve, 0)
            ve_q1(ve, 0, 0, 1)
            ve_ln_norm(ve, 2, 2)
            ve_kv1(ve, 1, 0)
            ve_ln_lo(ve, 2, 2, ln2_banks)
            ve_kv1(ve, 2, 0)
            ve_vw(ve, -1, 2, 0)
            ve_log_add(ve, 0, 0)
            ve_ss(ve, 0, 0, 0)
            ve_ln_stats(ve, 2, 3, lambda t: x_after[2](ve, t))
            ve_vw(ve, -1, 2, 1)
            ve_ln_norm(ve, 2, 3)
            ve_q1(ve, 0, 1, 0)
            ve_ss(ve, 0, 0, 1)
            ve_ln_lo(ve, 2, 3, ln2_banks)
            ve_log_rms(ve, 0, 0)
            ve_vw(ve, -1, 2, 2)
            ve_log_max(ve, 0, 0)
            ve_log_sub(ve, 0, 0)
            ve_q1(ve, 0, 1, 1)
            ve_rec1(ve, 0, 0)
            ve_ss(ve, 0, 1, 0)
            ve_vw(ve, -1, 2, 3)
            with ve.Fori(0, KV1 - 1) as j:
                for i in range(UNITS1):
                    ve_unit1(ve, j, i, False)
            for i in range(UNITS1):
                ve_unit1(ve, KV1 - 1, i, True)

        def po_pow(po, out_ap, in_ap, done, wait, value):
            po.wait_ge(wait, value)
            po.tensor_tensor(out_ap, in_ap, neg_half[:, 0:in_ap.shape[1]], ALU.pow).then_inc(done, 1)

        def po_log_mask(po, j, i):
            po.wait_ge(b_log, j * UNITS1 + i + 1)
            m = mask_sb[:, :, :].rearrange("p c (h n) -> p c h n", h=1).broadcast_to([P, TB, GH1, CTX])
            l4 = logit[:, :, :].rearrange("p (c h) n -> p c h n", c=TB)
            po.tensor_tensor(l4, l4, m, ALU.add).then_inc(b_mask, 1)

        def po_norm1(po, j, i, first=False):
            po.wait_ge(b_rec, j * UNITS1 + i + 1)
            if not first:
                po.wait_ge(b_t, j * UNITS1 + i)
            po.tensor_tensor(prob1n[:, :, :], prob1[:, :, :], wide(rinv1[:, :], CTX), ALU.mult).then_inc(b_norm, 1)

        def po_wq1(po, j, n, part):
            po.wait_ge(b_wq_hi, (j + n) * 2 + part + 1)
            split_lo(po, wq1_lo[:, part], slot(l1_chunk(n, "wq", part)).rearrange("p (c n) -> p c n", c=KC),
                     wq1_hi[:, part], b_wq_lo)

        def po_wo1(po, j, n, part):
            po.wait_ge(b_wo_hi, (j + n) * 2 + part + 1)
            split_lo(po, wo1_lo[:, 2 * part:2 * part + 2, :],
                     slot(l1_chunk(n, "wo", part)).rearrange("p (h n) -> p h n", h=2),
                     wo1_hi[:, 2 * part:2 * part + 2, :], b_wo_lo)

        def po_unit1(po, j, i, last):
            next1 = not (last and i + 1 >= UNITS1)
            if last and i >= 2:
                po_ln(po, 3, i - 2)
            if next1:
                po_pow(po, q_rms[:, :], q_var[:, :], b_rms, b_var, j * UNITS1 + i + 2)
            if not last:
                if i == 0:
                    po_wkv(po, wkv1_hi, wkv1_lo, b_wkv_hi, b_wkv_lo, j + 2)
                if i == 1:
                    po_wo1(po, j, 1, 0)
                if i == 2:
                    po_wq1(po, j, 1, 1)
            if next1:
                po_log_mask(po, j, i + 1)
            if i == 2 and not last:
                po_wo1(po, j, 1, 1)
            if next1:
                po_norm1(po, j, i + 1)
            if i == 1 and not last:
                po_pow(po, k_rms[:, :], k_var[:, :], b_krms, b_kvar, j + 2)
                po_wq1(po, j, 1, 0)

        def po_attn1(po):
            po_wkv(po, wkv1_hi, wkv1_lo, b_wkv_hi, b_wkv_lo, 1)
            po_wq1(po, 0, 0, 0)
            po_wq1(po, 0, 0, 1)
            po_pow(po, k_rms[:, :], k_var[:, :], b_krms, b_kvar, 1)
            po_ln(po, 2, 2)
            po_wo1(po, 0, 0, 0)
            po_wo1(po, 0, 0, 1)
            po_ln(po, 2, 3)
            po_pow(po, q_rms[:, :], q_var[:, :], b_rms, b_var, 1)
            po_log_mask(po, 0, 0)
            po_norm1(po, 0, 0, first=True)
            with po.Fori(0, KV1 - 1) as j:
                for i in range(UNITS1):
                    po_unit1(po, j, i, False)
            for i in range(UNITS1):
                po_unit1(po, KV1 - 1, i, True)

        @block.gpsimd
        def _(po):
            po.memset(neg_half[:, :], -0.5).then_inc(s_half, 1)
            po.memset(ident[:, :], 0.0).then_inc(s_ident, 1)
            po.wait_ge(s_ident, 1)
            po.affine_select(out=ident[:, :], in_=ident[:, :], compare_op=ALU.not_equal, fill=1.0, base=0,
                             pattern=[[-1, P]], channel_multiplier=1).then_inc(s_ident, 1)
            po.wait_ge(s_half, 1)
            for b in range(BATCH):
                po_ln(po, 0, b)
            po_wkv(po, wkv_hi, wkv_lo, a_wkv_hi, a_wkv_lo, 1)
            po.wait_ge(s_chi, 1)
            split_lo(po, cT_lo[:, :, :], prob[:, :, 0:BATCH * CTX], cT_hi[:, :, :], s_clo)
            po_wq(po, 0, 0)
            po_wo(po, 0, 0)
            po_wq(po, 0, 1)
            po_attn0(po)
            po_ffn(po, 0)
            po_attn1(po)
            po_ffn(po, 1)

        @block.scalar
        def _(ac):
            ac.sem_inc(a_exp, 2)
            for f in F:
                ac.sem_inc(f["h"], 2)
            ac_ln(ac, 0, 0, ln0_banks[0])
            ac_ln(ac, 0, 1, ln0_banks[1])
            ac_wkv(ac, 0, wkv_hi, a_wkv_hi)
            ac.wait_ge(s_ctx, 16)
            split_hi(ac, cT_hi[:, :, :], prob[:, :, 0:BATCH * CTX], s_chi)
            ac_ln(ac, 0, 2, ln0_banks[0])
            ac_ln(ac, 0, 3, ln0_banks[1])
            ac_wq(ac, 0, 0)
            ac_wo(ac, 0, 0)
            ac_wq(ac, 0, 1)
            ac.wait_ge(s_small, 16 * 8)
            ac.activation(tg[:, :], gates[:, :], ACT.Tanh).then_inc(s_tg, 1)
            ac_attn0(ac)
            ac_ffn(ac, 0, lambda eng: eng.wait_ge(a_acc, 2 * KV0 * UNITS0 + 2))
            ac_attn1(ac)
            ac_ffn(ac, 1, lambda eng: eng.wait_ge(b_acc, 1 + 2 * UNITS1 * KV1))

        @block.vector
        def _(ve):
            ve.sem_inc(b_acc, 1)
            ve.sem_inc(a_acc, 2)
            ve.sem_inc(a_olo, 1)
            def stats(b):
                ve_ln_stats(ve, 0, b, lambda t: x_after[0](ve, t))
            stats(0)
            for b in range(BATCH):
                if b + 1 < BATCH:
                    stats(b + 1)
                ve_ln_norm(ve, 0, b)
                if b >= 1:
                    ve_ln_lo(ve, 0, b - 1, ln0_banks[(b - 1) % 2])
            ve_ln_lo(ve, 0, BATCH - 1, ln0_banks[(BATCH - 1) % 2])
            ve.wait_ge(s_small, 16 * 8)
            ve.scalar_tensor_tensor(out=kscale[:, :], in0=qn_w[:, :], scalar=SCALE, in1=kn_w[:, :], op0=ALU.mult,
                                    op1=ALU.mult).then_inc(s_ksc, 1)
            ve.wait_ge(s_tg, 1)
            ve.tensor_scalar(tgad[:, :], ad_row[:, :], tg[:, 2:3], None, ALU.mult).then_inc(F[0]["tgad"], 1)
            ve.wait_ge(s_ksc, 1)
            ve.wait_ge(F[0]["tgad"], 1)
            ve_attn0(ve)
            ve_ffn(ve, 0)
            ve_attn1(ve)
            ve_ffn(ve, 1)

        @block.tensor
        def _(pe):
            pe.wait_ge(s_ident, 2)
            for b in range(BATCH):
                if b >= 2:
                    pe.wait_ge(l_lo, 2 * b - 2)
                pe_ln(pe, 0, b, ln0_banks[b % 2])
            pe_attn0(pe)
            pe_ffn(pe, 0, lambda eng: eng.wait_ge(a_acc, 2 * KV0 * UNITS0 + 2))
            pe_attn1(pe)
            pe_ffn(pe, 1, lambda eng: eng.wait_ge(b_acc, 1 + 2 * UNITS1 * KV1))


def kernel(x, ctx_4096, mask_1x1xSxS2_ff0, g_xattn, g_ffn, L0_xattn_Wq, L0_xattn_Wk, L0_xattn_Wv, L0_xattn_Wo,
           L0_ffn_Wg, L0_ffn_Wu, L0_ffn_Wd, L0_ffn_ag, L0_ffn_au, L0_ffn_ad, L1_xattn_q_proj_w, L1_xattn_k_proj_w,
           L1_xattn_v_proj_w, L1_xattn_o_proj_w, L1_xattn_q_norm_w, L1_xattn_k_norm_w, L1_ffn_W_gate, L1_ffn_W_up,
           L1_ffn_W_down):
    import numpy as np
    import concourse.bacc as bacc
    from concourse.bass_utils import run_bass_kernel_spmd

    def t(a):
        return np.ascontiguousarray(np.asarray(a).T)

    def padded(a, axis):
        a = np.asarray(a)
        width = [(0, 0)] * a.ndim
        width[axis] = (0, F0_PAD - F0)
        return np.pad(a, width)

    arrays = {
        "x": np.asarray(x).reshape(BATCH * SEQ, DM),
        "ctxT": t(np.asarray(ctx_4096).reshape(BATCH * CTX, DM)),
        "mask": np.asarray(mask_1x1xSxS2_ff0).reshape(SEQ, CTX),
        "g_xattn": np.asarray(g_xattn), "g_ffn": np.asarray(g_ffn),
        "wq0": np.asarray(L0_xattn_Wq), "wk0": np.asarray(L0_xattn_Wk),
        "wv0": np.asarray(L0_xattn_Wv), "wo0": np.asarray(L0_xattn_Wo),
        "wg0T": t(padded(L0_ffn_Wg, 0)), "wu0T": t(padded(L0_ffn_Wu, 0)), "wd0T": t(padded(L0_ffn_Wd, 1)),
        "ag": t(padded(L0_ffn_ag, 0).reshape(NF0, P)), "au": t(padded(L0_ffn_au, 0).reshape(NF0, P)),
        "ad": np.asarray(L0_ffn_ad),
        "wq1T": t(L1_xattn_q_proj_w), "wk1T": t(L1_xattn_k_proj_w), "wv1T": t(L1_xattn_v_proj_w),
        "wo1T": t(L1_xattn_o_proj_w),
        "qnorm": np.asarray(L1_xattn_q_norm_w).reshape(HD, 1), "knorm": np.asarray(L1_xattn_k_norm_w).reshape(HD, 1),
        "wg1T": t(L1_ffn_W_gate), "wu1T": t(L1_ffn_W_up), "wd1T": t(L1_ffn_W_down),
    }
    arrays = {f"in_{k}": np.ascontiguousarray(v) for k, v in arrays.items()}
    nc = bacc.Bacc("TRN2", target_bir_lowering=False, num_devices=1)
    aps = [nc.dram_tensor(k, v.shape, mybir.dt.from_np(v.dtype), kind="ExternalInput").ap() for k, v in arrays.items()]
    out = nc.dram_tensor("out_x", (BATCH * SEQ, DM), F32, kind="ExternalOutput").ap()
    flamingo_two_layers(nc, *aps, out)
    r = run_bass_kernel_spmd(nc, [arrays], core_ids=[0])
    return r.results[0]["out_x"].reshape(BATCH, SEQ, DM)
```
